# Optimizing a Trainium2 kernel written in Bass

```python
import numpy as np
import jax
import jax.numpy as jnp

def _softmax(x, axis=-1):
    return jax.nn.softmax(x, axis=axis)

def _gelu(x):
    return jax.nn.gelu(x, approximate=True)

def _silu(x):
    return jax.nn.silu(x)

def _sigmoid(x):
    return jax.nn.sigmoid(x)

def _layernorm(x, axis=-1, eps=1e-05):
    m = jnp.mean(x, axis=axis, keepdims=True)
    v = jnp.var(x, axis=axis, keepdims=True)
    return (x - m) / jnp.sqrt(v + eps)

def _scatter_add(tgt, idx, src, axis=0):
    return tgt.at[idx].add(src)

def _segment_sum(src, seg, n):
    return jax.ops.segment_sum(src, seg, n)
kernel_name = 'mk_gnn_preln_d4_gnn_r64_3e697e'

def setup_inputs(seed: int=0):
    np.random.seed(seed)
    _w = jnp.asarray

    def _rec_inputs():
        import jax
        import jax.numpy as jnp
        _gk = jax.random.key(seed)
        x = -0.0001006 + 1 * jax.random.normal(jax.random.fold_in(_gk, 1), (50000, 96), jnp.float32)
        src = jax.random.randint(jax.random.fold_in(_gk, 2), (25000,), 0, 50000, jnp.int32)
        dst = jax.random.randint(jax.random.fold_in(_gk, 3), (25000,), 0, 50000, jnp.int32)
        _o = jnp.argsort(dst, stable=True)
        src = src[_o]
        dst = dst[_o]
        edge_attr_64 = 0.000189758 + 1.00013 * jax.random.normal(jax.random.fold_in(_gk, 12), (25000, 64), jnp.float32)
        edge_weight = jax.random.uniform(jax.random.fold_in(_gk, 14), (25000,), jnp.float32, 0.0, 0.999998)
        return (x, src, dst, edge_attr_64, edge_weight)
    x, src, dst, edge_attr_64, edge_weight = _rec_inputs()

    def _L0_gnn_setup():
        import jax, jax.numpy as jnp
        import numpy as np
        N_NODES = 50000
        N_EDGES = 12500
        D = 96

        def _gcn_conv(x, src, dst, ew, W, b):
            n = x.shape[0]
            loop = jnp.arange(n)
            src_a = jnp.concatenate([src, loop])
            dst_a = jnp.concatenate([dst, loop])
            w_a = jnp.concatenate([ew, jnp.ones((n,), ew.dtype)])
            deg = jax.ops.segment_sum(w_a, dst_a, num_segments=n)
            dis = jnp.where(deg > 0, jax.lax.rsqrt(deg), jnp.zeros_like(deg))
            norm = dis[src_a] * w_a * dis[dst_a]
            h = x @ W
            msg = h[src_a] * norm[:, None]
            out = jax.ops.segment_sum(msg, dst_a, num_segments=n)
            return out + b
        key = jax.random.key(seed)
        ks = jax.random.split(key, 10)
        x = jax.random.normal(ks[0], (N_NODES, D), dtype=jnp.float32)
        edge_index = jax.random.randint(ks[1], (2, N_EDGES), 0, N_NODES, dtype=jnp.int64)
        edge_weight = jax.random.uniform(ks[2], (N_EDGES,), dtype=jnp.float32)
        s = 1.0 / np.sqrt(D)
        W1 = jax.random.uniform(ks[3], (D, D), jnp.float32, -s, s)
        b1 = jnp.zeros((D,), jnp.float32)
        W2 = jax.random.uniform(ks[4], (D, D), jnp.float32, -s, s)
        b2 = jnp.zeros((D,), jnp.float32)
        W3 = jax.random.uniform(ks[5], (D, D), jnp.float32, -s, s)
        b3 = jnp.zeros((D,), jnp.float32)
        return {'x': x, 'edge_index': edge_index, 'edge_weight': edge_weight, 'W1': W1, 'b1': b1, 'W2': W2, 'b2': b2, 'W3': W3, 'b3': b3}
    _L0_gnn_all = _L0_gnn_setup()
    _L0_gnn_in = {k: v for k, v in _L0_gnn_all.items() if k in ('W1', 'b1', 'W2', 'b2', 'W3', 'b3')}
    del _L0_gnn_all

    def _L1_gnn_setup():
        import jax, jax.numpy as jnp
        import numpy as np
        N_NODES = 50000
        N_EDGES = 12500
        DIM = 96
        HEADS = 4
        LAYERS = 3
        NEG_SLOPE = 0.2

        def _gat_layer(x, src, dst, W, a_src, a_dst, b):
            N = x.shape[0]
            H, C = a_src.shape
            h = (x @ W).reshape(N, H, C)
            alpha_s = jnp.einsum('nhc,hc->nh', h, a_src)
            alpha_d = jnp.einsum('nhc,hc->nh', h, a_dst)
            e = jax.nn.leaky_relu(alpha_s[src] + alpha_d[dst], NEG_SLOPE)
            m = jax.ops.segment_max(e, dst, num_segments=N)
            m = jnp.where(jnp.isfinite(m), m, 0.0)
            ex = jnp.exp(e - m[dst])
            den = jax.ops.segment_sum(ex, dst, num_segments=N)
            alpha = ex / (den[dst] + 1e-16)
            msg = h[src] * alpha[:, :, None]
            out = jax.ops.segment_sum(msg, dst, num_segments=N)
            return out.reshape(N, H * C) + b
        key = jax.random.key(seed)
        ks = jax.random.split(key, 6)
        C = DIM // HEADS
        x = jax.random.normal(ks[0], (N_NODES, DIM), dtype=jnp.float32)
        edge_index = jax.random.randint(ks[1], (2, N_EDGES), 0, N_NODES, dtype=jnp.int32)
        W = jax.random.normal(ks[2], (LAYERS, DIM, DIM), dtype=jnp.float32) * (1.0 / np.sqrt(DIM))
        att_src = jax.random.normal(ks[3], (LAYERS, HEADS, C), dtype=jnp.float32) * (1.0 / np.sqrt(C))
        att_dst = jax.random.normal(ks[4], (LAYERS, HEADS, C), dtype=jnp.float32) * (1.0 / np.sqrt(C))
        bias = jnp.zeros((LAYERS, DIM), dtype=jnp.float32)
        return {'x': x, 'edge_index': edge_index, 'W': W, 'att_src': att_src, 'att_dst': att_dst, 'bias': bias}
    _L1_gnn_all = _L1_gnn_setup()
    _L1_gnn_in = {k: v for k, v in _L1_gnn_all.items() if k in ('W', 'att_src', 'att_dst', 'bias')}
    del _L1_gnn_all

    def _L2_gnn_setup():
        import jax, jax.numpy as jnp
        import numpy as np
        N_NODES = 50000
        N_EDGES = 12500
        D_MODEL = 96
        HEADS = 4
        key = jax.random.key(seed)
        ks = jax.random.split(key, 6)
        scale = 1.0 / np.sqrt(D_MODEL)
        return {'embeds': jax.random.normal(ks[0], (N_NODES, D_MODEL), dtype=jnp.float32), 'qW': jax.random.normal(ks[1], (D_MODEL, D_MODEL), dtype=jnp.float32) * scale, 'kW': jax.random.normal(ks[2], (D_MODEL, D_MODEL), dtype=jnp.float32) * scale, 'vW': jax.random.normal(ks[3], (D_MODEL, D_MODEL), dtype=jnp.float32) * scale, 'rows': jax.random.randint(ks[4], (N_EDGES,), 0, N_NODES, dtype=jnp.int32), 'cols': jax.random.randint(ks[5], (N_EDGES,), 0, N_NODES, dtype=jnp.int32)}
    _L2_gnn_all = _L2_gnn_setup()
    _L2_gnn_in = {k: v for k, v in _L2_gnn_all.items() if k in ('qW', 'kW', 'vW')}
    del _L2_gnn_all

    def _L3_gnn_setup():
        import jax, jax.numpy as jnp
        import numpy as np
        N, E = (50000, 12500)
        NODE_DIM, EDGE_DIM = (96, 64)
        IN_DIM = 2 * NODE_DIM + EDGE_DIM
        key = jax.random.key(seed)
        k = jax.random.split(key, 7)
        h = jax.random.normal(k[0], (N, NODE_DIM), dtype=jnp.float32)
        edge_index = jax.random.randint(k[1], (2, E), 0, N, dtype=jnp.int64)
        edge_attr = jax.random.normal(k[2], (E, EDGE_DIM), dtype=jnp.float32)
        s = 1.0 / np.sqrt(IN_DIM)
        W_e = jax.random.uniform(k[3], (IN_DIM, NODE_DIM), jnp.float32, -s, s)
        b_e = jax.random.uniform(k[4], (NODE_DIM,), jnp.float32, -s, s)
        W_n = jax.random.uniform(k[5], (IN_DIM, NODE_DIM), jnp.float32, -s, s)
        b_n = jax.random.uniform(k[6], (NODE_DIM,), jnp.float32, -s, s)
        return {'h': h, 'edge_index': edge_index, 'edge_attr': edge_attr, 'W_e': W_e, 'b_e': b_e, 'W_n': W_n, 'b_n': b_n}
    _L3_gnn_all = _L3_gnn_setup()
    _L3_gnn_in = {k: v for k, v in _L3_gnn_all.items() if k in ('W_e', 'b_e', 'W_n', 'b_n')}
    del _L3_gnn_all
    return {'x': x, 'src': src, 'dst': dst, 'edge_attr_64': edge_attr_64, 'edge_weight': edge_weight, 'L0_gnn_W1': _L0_gnn_in['W1'], 'L0_gnn_b1': _L0_gnn_in['b1'], 'L0_gnn_W2': _L0_gnn_in['W2'], 'L0_gnn_b2': _L0_gnn_in['b2'], 'L0_gnn_W3': _L0_gnn_in['W3'], 'L0_gnn_b3': _L0_gnn_in['b3'], 'L1_gnn_W': _L1_gnn_in['W'], 'L1_gnn_att_src': _L1_gnn_in['att_src'], 'L1_gnn_att_dst': _L1_gnn_in['att_dst'], 'L1_gnn_bias': _L1_gnn_in['bias'], 'L2_gnn_qW': _L2_gnn_in['qW'], 'L2_gnn_kW': _L2_gnn_in['kW'], 'L2_gnn_vW': _L2_gnn_in['vW'], 'L3_gnn_W_e': _L3_gnn_in['W_e'], 'L3_gnn_b_e': _L3_gnn_in['b_e'], 'L3_gnn_W_n': _L3_gnn_in['W_n'], 'L3_gnn_b_n': _L3_gnn_in['b_n']}

def reference(x, src, dst, edge_attr_64, edge_weight, L0_gnn_W1, L0_gnn_b1, L0_gnn_W2, L0_gnn_b2, L0_gnn_W3, L0_gnn_b3, L1_gnn_W, L1_gnn_att_src, L1_gnn_att_dst, L1_gnn_bias, L2_gnn_qW, L2_gnn_kW, L2_gnn_vW, L3_gnn_W_e, L3_gnn_b_e, L3_gnn_W_n, L3_gnn_b_n):
    import jax
    import jax.numpy as jnp

    def _L0_gnn_ref(x, edge_index, edge_weight, W1, b1, W2, b2, W3, b3):
        import jax, jax.numpy as jnp
        import numpy as np
        N_NODES = 50000
        N_EDGES = 12500
        D = 96

        def _gcn_conv(x, src, dst, ew, W, b):
            n = x.shape[0]
            loop = jnp.arange(n)
            src_a = jnp.concatenate([src, loop])
            dst_a = jnp.concatenate([dst, loop])
            w_a = jnp.concatenate([ew, jnp.ones((n,), ew.dtype)])
            deg = jax.ops.segment_sum(w_a, dst_a, num_segments=n)
            dis = jnp.where(deg > 0, jax.lax.rsqrt(deg), jnp.zeros_like(deg))
            norm = dis[src_a] * w_a * dis[dst_a]
            h = x @ W
            msg = h[src_a] * norm[:, None]
            out = jax.ops.segment_sum(msg, dst_a, num_segments=n)
            return out + b
        src, dst = (edge_index[0], edge_index[1])
        h = _gcn_conv(x, src, dst, edge_weight, W1, b1)
        h = jax.nn.relu(h)
        h = _gcn_conv(h, src, dst, edge_weight, W2, b2)
        h = jax.nn.relu(h)
        h = _gcn_conv(h, src, dst, edge_weight, W3, b3)
        return h

    def _L1_gnn_ref(x, edge_index, W, att_src, att_dst, bias):
        import jax, jax.numpy as jnp
        import numpy as np
        N_NODES = 50000
        N_EDGES = 12500
        DIM = 96
        HEADS = 4
        LAYERS = 3
        NEG_SLOPE = 0.2

        def _gat_layer(x, src, dst, W, a_src, a_dst, b):
            N = x.shape[0]
            H, C = a_src.shape
            h = (x @ W).reshape(N, H, C)
            alpha_s = jnp.einsum('nhc,hc->nh', h, a_src)
            alpha_d = jnp.einsum('nhc,hc->nh', h, a_dst)
            e = jax.nn.leaky_relu(alpha_s[src] + alpha_d[dst], NEG_SLOPE)
            m = jax.ops.segment_max(e, dst, num_segments=N)
            m = jnp.where(jnp.isfinite(m), m, 0.0)
            ex = jnp.exp(e - m[dst])
            den = jax.ops.segment_sum(ex, dst, num_segments=N)
            alpha = ex / (den[dst] + 1e-16)
            msg = h[src] * alpha[:, :, None]
            out = jax.ops.segment_sum(msg, dst, num_segments=N)
            return out.reshape(N, H * C) + b
        src = edge_index[0]
        dst = edge_index[1]
        for l in range(W.shape[0]):
            x = jax.nn.relu(_gat_layer(x, src, dst, W[l], att_src[l], att_dst[l], bias[l]))
        return x

    def _L2_gnn_ref(embeds, qW, kW, vW, rows, cols):
        import jax, jax.numpy as jnp
        import numpy as np
        N_NODES = 50000
        N_EDGES = 12500
        D_MODEL = 96
        HEADS = 4
        nvar, d = embeds.shape
        dh = d // HEADS
        e = rows.shape[0]
        q = (embeds[rows] @ qW).reshape(e, HEADS, dh)
        k = (embeds[cols] @ kW).reshape(e, HEADS, dh)
        v = (embeds[cols] @ vW).reshape(e, HEADS, dh)
        scores = jnp.clip(jnp.einsum('ehd,ehd->eh', q, k), -10.0, 10.0)
        exp_s = jnp.exp(scores)
        norms = jax.ops.segment_sum(exp_s, rows, num_segments=nvar)[rows]
        w = exp_s / (norms + 1e-08)
        res = jax.ops.segment_sum(w[:, :, None] * v, rows, num_segments=nvar).reshape(nvar, d)
        return embeds + res

    def _L3_gnn_ref(h, edge_index, edge_attr, W_e, b_e, W_n, b_n):
        import jax, jax.numpy as jnp
        import numpy as np
        N, E = (50000, 12500)
        NODE_DIM, EDGE_DIM = (96, 64)
        IN_DIM = 2 * NODE_DIM + EDGE_DIM
        src, dst = (edge_index[0], edge_index[1])
        concat = jnp.concatenate([h[src], h[dst], edge_attr], axis=-1)
        gates = jax.nn.sigmoid(concat @ W_e + b_e)
        messages = jax.nn.softplus(concat @ W_n + b_n)
        gated = gates * messages
        n = h.shape[0]
        h_new = jax.ops.segment_sum(gated, dst, num_segments=n)
        edge_count = jax.ops.segment_sum(jnp.ones((dst.shape[0],), h.dtype), dst, num_segments=n)
        edge_count = jnp.clip(edge_count, 1.0, None)[:, None]
        return h + h_new / edge_count
    edge_index = jnp.stack([src, dst])
    h = jnp.maximum(_layernorm(x, axis=-1), 0.0)
    x = x + _L0_gnn_ref(h, edge_index, edge_weight, L0_gnn_W1, L0_gnn_b1, L0_gnn_W2, L0_gnn_b2, L0_gnn_W3, L0_gnn_b3)
    h = jnp.maximum(_layernorm(x, axis=-1), 0.0)
    x = x + _L1_gnn_ref(h, edge_index, L1_gnn_W, L1_gnn_att_src, L1_gnn_att_dst, L1_gnn_bias)
    h = jnp.maximum(_layernorm(x, axis=-1), 0.0)
    x = x + _L2_gnn_ref(h, L2_gnn_qW, L2_gnn_kW, L2_gnn_vW, src, dst)
    h = jnp.maximum(_layernorm(x, axis=-1), 0.0)
    x = x + _L3_gnn_ref(h, edge_index, edge_attr_64, L3_gnn_W_e, L3_gnn_b_e, L3_gnn_W_n, L3_gnn_b_n)
    return x

_drawn_inputs = setup_inputs


def setup_inputs(seed=0):
    import zlib

    import numpy as np

    out = dict(_drawn_inputs(seed))
    spreads = {'L0_gnn_b1': (0.0, 0.498),
     'L0_gnn_b2': (0.0, 0.1),
     'L0_gnn_b3': (0.0, 0.1),
     'L1_gnn_bias': (0.0, 0.1)}
    factors = {'edge_weight': 4.466,
     'L1_gnn_att_src': 24.042,
     'L1_gnn_att_dst': 64.0,
     'L3_gnn_W_e': 2.684,
     'L3_gnn_b_e': 39.457,
     'L3_gnn_b_n': 23.18}
    for name, (base, spread) in spreads.items():
        noise = np.random.default_rng([zlib.crc32(name.encode()), seed]).standard_normal(out[name].shape)
        drawn = base * np.exp(spread * noise) if base else spread * noise
        out[name] = jnp.asarray(drawn.astype(out[name].dtype))
    for name, factor in factors.items():
        out[name] = (out[name] * factor).astype(out[name].dtype)
    return out
```

```python
import concourse.bass as bass
from concourse import mybir
from contextlib import ExitStack

ALU = mybir.AluOpType
ACT = mybir.ActivationFunctionType
AX = mybir.AxisListType
F32 = mybir.dt.float32
I32 = mybir.dt.int32

P = 128
N, D, E, DE = 50000, 96, 25000, 64
HEADS = 4
HC = D // HEADS
C = 7
CR = C * P
ET = 28 * C
EP = ET * P
ECH = ET // C
NCH = 56
NP = NCH * CR
ROWS = EP + NP
J = EP // P
ZROWS = EP + 2 * CR
GW = D + 2 * HEADS
BIG = 1.0e30
SKIP = 65536.0
EPS = 1.0e-5
M_DST, M_PREV, M_NORM, M_SELF, M_REP, M_N = 0, 1, 2, 3, 4, 5
I_SRCROW, I_SRCROW2, I_SRC, I_DST, I_OUT, I_N = 0, 1, 2, 3, 4, 5


POOL_DMA = {}
COUNTED = {}


class Stage:

    def __init__(self, nc, name, plain, credited, credit_of=None):
        self.nc, self.stack = nc, ExitStack()
        self.name = name
        self.s = {n: POOL_DMA[n] if n in POOL_DMA else self.stack.enter_context(nc.semaphore(f"{name}_{n}"))
                  for n in [*plain, *credited]}
        with nc.Block() as block:
            @block.sync
            def _(sp):
                for n in self.s:
                    if n not in POOL_DMA:
                        sp.sem_clear(self.s[n])
        with nc.Block() as block:
            @block.sync
            def _(sp):
                for n in credited:
                    sp.sem_inc(self.s[n], (credit_of or {}).get(n, 2))
                sp.drain()

    def __getitem__(self, n):
        return self.s[n]

    def sb(self, name, shape, dt=F32):
        return self.stack.enter_context(self.nc.sbuf_tensor(f"{self.name}_{name}", shape, dt))

    def close(self, **pool):
        for n, added in pool.items():
            COUNTED[n] += added
        self.stack.close()


def chunk_rows(table, n, base=0):
    return table[bass.ds(n * CR + base, CR), :].rearrange("(p c) d -> p c d", c=C)


def chunk_tiles(table, n):
    return table[bass.ds(n * CR, CR), :].rearrange("(c p) d -> p c d", p=P)


def over(ap, shape):
    return ap.to_broadcast(shape)


def build(nc, t, out):
    top = ExitStack()
    with top:
        def dram(name, shape, dt=F32):
            return nc.dram_tensor(name, shape, dt).ap()

        def sb(name, shape, dt=F32):
            return top.enter_context(nc.sbuf_tensor(name, shape, dt))

        for n in ("g0", "g1", "sc0", "sc1", "add0", "add1"):
            POOL_DMA[n] = top.enter_context(nc.semaphore(n))
            COUNTED[n] = 0
        ident = sb("ident", [P, P])
        last_row = sb("last_row", [P, 1])
        eps_col = sb("eps_col", [P, 1])
        META = sb("META", [P, M_N, ET])
        IDX = sb("IDX", [P, I_N, ET], I32)
        FL = {n: sb(f"fl_{n}", [P, J]) for n in ("same_prev", "same_next", "tail", "first", "last",
                                                "pen_prev", "pen_first")}
        RT = {n: sb(f"rt_{n}", [HEADS, P]) for n in ("whole_prev", "whole_next", "pen_whole")}
        ps = top.enter_context(nc.psum_tensor("ps", [P, 4096], F32))

        d = dict(
            lin=dram("lin", (6, EP)), search=dram("search", (ET, 3 * P)),
            hx=dram("hx", (NP, 2 * D)), x0d=dram("x0d", (EP, D)),
            z=dram("z", (EP, D)), h1=dram("h1", (ROWS, D)), h2=dram("h2", (ROWS, D)),
            x1=dram("x1", (ROWS, D)), a0=dram("a0", (ROWS, D)), gt=dram("gt", (ROWS, GW)),
            gr=dram("gr", (EP, GW)), asrc=dram("asrc", (EP, HEADS)), alpha=dram("alpha", (EP, HEADS)),
            zg=dram("zg", (ZROWS, D)), h2n=dram("h2n", (ROWS, D)), qy=dram("qy", (ROWS, 2 * D)),
            kvy=dram("kvy", (EP, 3 * D)), ys=dram("ys", (EP, D)), yd=dram("yd", (EP, D)),
            msg=dram("msg", (EP, D + HEADS)), res=dram("res", (NP + CR, D + HEADS)),
            msg3=dram("msg3", (EP, D + 1)), base=dram("base", (EP, D)), z3=dram("z3", (EP, D + 1)),
        )
        g = dict(ident=ident, last_row=last_row, eps_col=eps_col, META=META, IDX=IDX, FL=FL, RT=RT, ps=ps)
        prepare(nc, t, d, g)
        search(nc, t, d, g)
        norm_stage(nc, "h0", t, d, g, out)
        aggregate(nc, "gcn1", t, d, g)
        product_stage(nc, "gcn1", t, d, g)
        aggregate(nc, "gcn2", t, d, g)
        product_stage(nc, "gcn2", t, d, g)
        aggregate(nc, "gcn3", t, d, g)
        product_stage(nc, "gcn3", t, d, g)
        norm_stage(nc, "a0", t, d, g, out)
        for layer in range(3):
            product_stage(nc, f"gat{layer}", t, d, g)
            gat_gather(nc, layer, t, d, g)
            gat_softmax(nc, layer, t, d, g)
            aggregate(nc, f"gat{layer}", t, d, g)
        norm_stage(nc, "x2", t, d, g, out)
        product_stage(nc, "q", t, d, g)
        product_stage(nc, "kv", t, d, g)
        patch_last_rows(nc, t, d, g)
        attention(nc, t, d, g)
        accumulate(nc, t, d, g)
        norm_stage(nc, "fin", t, d, g, out)
        gates(nc, t, d, g)
        aggregate(nc, "edge", t, d, g)
        finish(nc, t, d, g, out)


class Scans:

    def __init__(self, nc, st, g, heads):
        self.nc, self.st, self.g, self.heads, self.n = nc, st, g, heads, 0
        self.edge = st.sb("edge", [P, HEADS])
        self.edge_t = st.sb("edge_t", [HEADS, P])
        self.carry_t = st.sb("carry_t", [HEADS, P + 1])
        self.carry = st.sb("carry", [P, HEADS])

    def begin(self, v):
        v.memset(self.edge[:], 0.0)
        v.drain()

    def cross(self, v, y, col, flags, op0, op1, first, back):
        nc, g, st, H = self.nc, self.g, self.st, self.heads
        v.drain()
        v.tensor_copy(self.edge[:, 0:H], y[:, col, :]).then_inc(st["to_pe"], 1)
        v.wait_ge(st["from_pe"], 2 * self.n + 1)
        v.tensor_copy(self.edge_t[:], g["ps"][0:HEADS, 0:P])
        v.memset(self.carry_t[:], first)
        v.drain()
        if back:
            v.tensor_tensor_scan(self.carry_t[:, 0:P][:, ::-1], g["RT"][flags][:, ::-1],
                                 self.edge_t[:, ::-1], first, op0, op1).then_inc(st["to_pe"], 1)
        else:
            v.tensor_tensor_scan(self.carry_t[:, 1:P + 1], g["RT"][flags][:],
                                 self.edge_t[:], first, op0, op1).then_inc(st["to_pe"], 1)
        v.wait_ge(st["from_pe"], 2 * self.n + 2)
        v.tensor_copy(self.carry[:], g["ps"][:, 512:512 + HEADS])
        v.drain()
        self.n += 1

    def total(self, v, y, x):
        F = self.g["FL"]
        for h in range(self.heads):
            v.tensor_tensor_scan(y[:, :, h], F["same_prev"][:], x[:, :, h], 0.0, ALU.mult, ALU.add)
        self.cross(v, y, J - 1, "whole_prev", ALU.mult, ALU.add, 0.0, False)
        for h in range(self.heads):
            v.scalar_tensor_tensor(out=y[:, :, h], in0=F["first"][:], scalar=self.carry[:, h:h + 1],
                                   in1=y[:, :, h], op0=ALU.mult, op1=ALU.add)
        v.drain()

    def maximum(self, v, y, x):
        F = self.g["FL"]
        for h in range(self.heads):
            v.tensor_tensor_scan(y[:, :, h], F["pen_prev"][:], x[:, :, h], -BIG, ALU.add, ALU.max)
        self.cross(v, y, J - 1, "pen_whole", ALU.add, ALU.max, -BIG, False)
        for h in range(self.heads):
            v.scalar_tensor_tensor(out=y[:, :, h], in0=F["pen_first"][:], scalar=self.carry[:, h:h + 1],
                                   in1=y[:, :, h], op0=ALU.add, op1=ALU.max)
        v.drain()

    def spread(self, v, y, x, tmp):
        F = self.g["FL"]
        for h in range(self.heads):
            v.tensor_tensor(tmp[:, :, h], x[:, :, h], F["tail"][:], ALU.mult)
        v.drain()
        for h in range(self.heads):
            v.tensor_tensor_scan(y[:, ::-1, h], F["same_next"][:, ::-1], tmp[:, ::-1, h], 0.0, ALU.mult, ALU.add)
        self.cross(v, y, 0, "whole_next", ALU.mult, ALU.add, 0.0, True)
        for h in range(self.heads):
            v.scalar_tensor_tensor(out=y[:, :, h], in0=F["last"][:], scalar=self.carry[:, h:h + 1],
                                   in1=y[:, :, h], op0=ALU.mult, op1=ALU.add)
        v.drain()


def pe_part(nc, st, g, sc, backs, pe):
    for n, back in enumerate(backs):
        pe.wait_ge(st["to_pe"], 2 * n + 1)
        nc.tensor.transpose(g["ps"][0:HEADS, 0:P], sc.edge[:], g["ident"][:]).then_inc(st["from_pe"], 1)
        pe.wait_ge(st["to_pe"], 2 * n + 2)
        c = sc.carry_t[:, 1:P + 1] if back else sc.carry_t[:, 0:P]
        nc.tensor.transpose(g["ps"][:, 512:512 + HEADS], c, g["ident"][0:HEADS, 0:HEADS]).then_inc(st["from_pe"], 1)


def prepare(nc, t, d, g):
    st = Stage(nc, "prep", ["tick", "ld", "k", "to_pe", "from_pe", "rt", "sq", "out"], [])
    raw = st.sb("raw", [P, 3, J], I32)
    ew = st.sb("ew", [P, J])
    eno = st.sb("eno", [P, J])
    dp, dc, dn = (st.sb(x, [P, J]) for x in ("dp", "dc", "dn"))
    X, Y, Z, T = (st.sb(x, [P, J, 1]) for x in ("X", "Y", "Z", "T"))
    whole = st.sb("whole", [P, 3, HEADS])
    L = st.sb("L", [P, 6, J])
    ti = st.sb("ti", [P, 2, ET], I32)
    zero = st.sb("zero", [P, C * (D + HEADS)])
    sc = Scans(nc, st, g, 1)
    F, RT, ps, ident = g["FL"], g["RT"], g["ps"], g["ident"]

    with nc.Block() as block:
        @block.sync
        def _(sp):
            sp.dma_start(raw[:], t["dst_runs"]).then_inc(st["ld"], 16)
            sp.dma_start(ew[:], t["ew_runs"]).then_inc(st["ld"], 16)
            sp.dma_start(eno[:], t["edge_no"]).then_inc(st["ld"], 16)
            sp.dma_start(ti[:, 0, :], t["dst_tiles"]).then_inc(st["ld"], 16)
            sp.dma_start(ti[:, 1, :], t["prev_tiles"]).then_inc(st["ld"], 16)
            sp.wait_ge(st["k"], 3)
            with sp.Fori(0, NCH + 1) as i:
                sp.dma_start(d["res"][bass.ds(i * CR, CR), :].rearrange("(p c) d -> p (c d)", c=C),
                             zero[:]).then_inc(st["out"], 16)
            for i in range(2):
                sp.dma_start(d["zg"][EP + i * CR:EP + (i + 1) * CR, :].rearrange("(p c) d -> p (c d)", c=C),
                             zero[:, 0:C * D]).then_inc(st["out"], 16)
            sp.wait_ge(st["out"], 16 * (NCH + 3))
            sp.wait_ge(st["sq"], 3)
            sp.dma_start(d["lin"].rearrange("s (q j) -> q s j", j=J), L[:]).then_inc(st["ld"], 16)
            sp.wait_ge(st["ld"], 96)
            for s in range(3):
                sp.dma_start(d["search"][:, s * P:(s + 1) * P],
                             d["lin"][s, :].rearrange("(k f) -> k f", f=P)).then_inc(st["ld"], 16)
            sp.wait_ge(st["ld"], 144)

        @block.gpsimd
        def _(po):
            po.memset(ident[:], 0.0)
            po.memset(g["last_row"][:], 0.0)
            po.drain()
            po.affine_select(out=ident[:], in_=ident[:], compare_op=ALU.not_equal, fill=1.0,
                             base=0, pattern=[[-1, P]], channel_multiplier=1).then_inc(st["k"], 1)
            po.affine_select(out=g["last_row"][:], in_=g["last_row"][:], compare_op=ALU.not_equal, fill=1.0,
                             base=1 - P, pattern=[[1, 1]], channel_multiplier=1).then_inc(st["k"], 1)
            po.memset(zero[:], 0.0).then_inc(st["k"], 1)

        @block.tensor
        def _(pe):
            pe.wait_ge(st["k"], 2)
            pe.wait_ge(st["rt"], 1)
            for n in range(3):
                last = nc.tensor.transpose(ps[0:HEADS, 1024 + n * P:1024 + (n + 1) * P], whole[:, n, :], ident[:])
            last.then_inc(st["rt"], 1)
            pe_part(nc, st, g, sc, [False, True, True], pe)

        @block.scalar
        def _(act):
            act.wait_ge(st["sq"], 1)
            act.activation(Z[:], Z[:], ACT.Sqrt).then_inc(st["sq"], 1)

        @block.vector
        def _(v):
            v.memset(g["eps_col"][:], EPS)
            sc.begin(v)
            v.wait_ge(st["ld"], 80)
            v.wait_ge(st["k"], 3)
            for n, a in enumerate((dp, dc, dn)):
                v.tensor_copy(a[:], raw[:, n, :])
            v.drain()
            v.tensor_tensor(F["same_prev"][:], dc[:], dp[:], ALU.is_equal)
            v.tensor_tensor(F["same_next"][:], dc[:], dn[:], ALU.is_equal)
            v.tensor_scalar(F["first"][:], dc[:], dp[:, 0:1], None, ALU.is_equal)
            v.tensor_scalar(F["last"][:], dc[:], dn[:, J - 1:J], None, ALU.is_equal)
            v.tensor_tensor(whole[:, 0, :], over(dc[:, J - 1:J], [P, HEADS]), over(dp[:, 0:1], [P, HEADS]), ALU.is_equal)
            v.tensor_tensor(whole[:, 1, :], over(dc[:, 0:1], [P, HEADS]), over(dn[:, J - 1:J], [P, HEADS]), ALU.is_equal)
            v.drain()
            v.tensor_scalar(F["tail"][:], F["same_next"][:], -1.0, 1.0, ALU.mult, ALU.add)
            v.tensor_scalar(F["pen_prev"][:], F["same_prev"][:], -1.0, BIG, ALU.add, ALU.mult)
            v.tensor_scalar(F["pen_first"][:], F["first"][:], -1.0, BIG, ALU.add, ALU.mult)
            v.tensor_scalar(whole[:, 2, :], whole[:, 0, :], -1.0, BIG, ALU.add, ALU.mult).then_inc(st["rt"], 1)
            v.wait_ge(st["rt"], 2)
            for n, name in enumerate(("whole_prev", "whole_next", "pen_whole")):
                v.tensor_copy(RT[name][:], ps[0:HEADS, 1024 + n * P:1024 + (n + 1) * P])
            v.drain()
            v.tensor_copy(X[:, :, 0], ew[:])
            v.drain()
            sc.total(v, Y, X)
            sc.spread(v, X, Y, T)
            v.tensor_scalar(Y[:], X[:], 1.0, None, ALU.add)
            v.drain()
            v.tensor_scalar(X[:], Y[:], 0.0, None, ALU.is_gt)
            v.tensor_scalar(Z[:], Y[:], 1.0e-30, None, ALU.max).then_inc(st["sq"], 1)
            v.wait_ge(st["sq"], 2)
            v.reciprocal(Y[:], Z[:])
            v.drain()
            v.tensor_tensor(L[:, 3, :], Y[:, :, 0], X[:, :, 0], ALU.mult)
            v.drain()
            v.tensor_scalar(Y[:, :, 0], eno[:], 1.0, None, ALU.mult)
            v.drain()
            sc.spread(v, X, Y, T)
            v.tensor_copy(L[:, 5, :], X[:, :, 0])
            v.tensor_copy(L[:, 4, :], F["tail"][:])
            v.tensor_copy(L[:, 0, :], dc[:])
            v.tensor_tensor(L[:, 2, :], L[:, 3, :], F["tail"][:], ALU.mult)
            v.scalar_tensor_tensor(out=L[:, 1, :], in0=eno[:], scalar=1.0, in1=F["tail"][:], op0=ALU.add, op1=ALU.mult)
            v.tensor_copy(g["META"][:, M_DST, :], ti[:, 0, :])
            v.tensor_copy(g["META"][:, M_PREV, :], ti[:, 1, :]).then_inc(st["sq"], 1)
    st.close()


def search(nc, t, d, g):
    st = Stage(nc, "find", ["tick", "ix", "ld", "tl", "kf", "g0", "g1"], ["fine"])
    src = st.sb("src", [P, ET], I32)
    srcf = st.sb("srcf", [P, ET])
    firsti = st.sb("firsti", [P, ET], I32)
    first = st.sb("first", [P, ET])
    junk = st.sb("junk", [P, ET])
    K = st.sb("K", [P, ET])
    KI = st.sb("KI", [P, ET], I32)
    kc = st.sb("kc", [P, 2, C], I32)
    S = st.sb("S", [P, 2, C, 3 * P])
    acc = st.sb("acc", [P, 2, 2, C])
    POS = st.sb("POS", [P, 2, ET])
    HALF = ET // 2
    TR = st.sb("TR", [HALF, 3, 2, P])
    TL = st.sb("TL", [P, 3, ET])
    ew = st.sb("ew", [P, ET])
    a, b, c = (st.sb(x, [P, ET]) for x in ("a", "b", "c"))
    dsti = st.sb("dsti", [P, ET], I32)
    got = [st["g0"], st["g1"]]
    META, IDX = g["META"], g["IDX"]

    with nc.Block() as block:
        @block.sync
        def _(sp):
            sp.dma_start(src[:], t["src_tiles"]).then_inc(st["ld"], 16)
            sp.dma_start(firsti[:], over(t["first"].unsqueeze(0), [P, ET])).then_inc(st["ld"], 16)
            sp.dma_start(ew[:], t["ew_tiles"]).then_inc(st["ld"], 16)
            sp.dma_start(dsti[:], t["dst_tiles"]).then_inc(st["ld"], 16)
            for s in range(3):
                sp.dma_start(TR[:, s], d["lin"][3 + s, :].rearrange("(a k p) -> k a p", a=2, p=P)).then_inc(st["ld"], 16)

        @block.tensor
        def _(pe):
            pe.wait_ge(st["ld"], 112)
            for s in range(3):
                for a_ in (0, 1):
                    last = nc.tensor.transpose(g["ps"][:, (2 * s + a_) * P:(2 * s + a_) * P + HALF], TR[:, s, a_, :],
                                               g["ident"][0:HALF, 0:HALF])
            last.then_inc(st["tl"], 1)

        @block.gpsimd
        def _(po):
            po.wait_ge(st["kf"], 1)
            with po.Fori(0, ECH // 2) as i:
                for k in (0, 1):
                    n = 2 * i + k
                    po.wait_ge(st["fine"], n + 1)
                    po.tensor_copy(kc[:, k, :], KI[:, bass.ds(n * C, C)]).then_inc(st["ix"], 1)
                    po.wait_ge(st["ix"], n + 1)
                    po.sem_inc(st["tick"], 1)
                    for c_ in range(C):
                        po.indirect_dma_start(out=S[:, k, c_, :], out_offset=None, in_=d["search"],
                                              in_offset=bass.IndirectOffsetOnAxis(ap=kc[:, k, c_:c_ + 1], axis=0),
                                              bounds_check=ET - 1, oob_is_err=False).then_inc(got[k], 16)

        @block.vector
        def _(v):
            v.wait_ge(st["ld"], 112)
            v.wait_ge(st["tl"], 1)
            for s in range(3):
                for a_ in (0, 1):
                    v.tensor_copy(TL[:, s, a_ * HALF:(a_ + 1) * HALF],
                                  g["ps"][:, (2 * s + a_) * P:(2 * s + a_) * P + HALF])
            v.tensor_copy(srcf[:], src[:])
            v.tensor_copy(first[:], firsti[:])
            v.drain()
            with v.Fori(0, ET // C) as i:
                for c_ in range(C):
                    v.tensor_scalar(junk[:], first[:], srcf[:, bass.ds(i * C + c_, 1)], -1.0, ALU.is_le, ALU.add,
                                    accum_out=acc[:, 0, 0, c_:c_ + 1])
                    v.drain()
                v.tensor_copy(K[:, bass.ds(i * C, C)], acc[:, 0, 0, :])
                v.drain()
            v.tensor_scalar(KI[:], K[:], 0.0, None, ALU.max).then_inc(st["kf"], 1)
            with v.Fori(0, ECH // 2) as i:
                for k in (0, 1):
                    n = 2 * i + k
                    v.wait_ge(got[k], COUNTED[f"g{k}"] + 16 * C * (i + 1))
                    for c_ in range(C):
                        for s in (0, 1):
                            v.scalar_tensor_tensor(out=junk[:, 0:P], in0=S[:, k, c_, 0:P],
                                                   scalar=srcf[:, bass.ds(n * C + c_, 1)],
                                                   in1=S[:, k, c_, (s + 1) * P:(s + 2) * P],
                                                   op0=ALU.is_equal, op1=ALU.mult,
                                                   accum_out=acc[:, k, s, c_:c_ + 1])
                            v.drain()
                    v.tensor_copy(POS[:, :, bass.ds(n * C, C)], acc[:, k, :, :]).then_inc(st["fine"], 1)
            v.drain()
            v.tensor_scalar(a[:], POS[:, 0, :], 0.5, None, ALU.is_gt)
            v.tensor_scalar(b[:], srcf[:], float(EP), None, ALU.add)
            v.drain()
            v.scalar_tensor_tensor(out=c[:], in0=POS[:, 0, :], scalar=-1.0, in1=b[:], op0=ALU.add, op1=ALU.subtract)
            v.drain()
            v.tensor_tensor(c[:], c[:], a[:], ALU.mult)
            v.drain()
            v.tensor_tensor(IDX[:, I_SRCROW, :], c[:], b[:], ALU.add)
            v.drain()
            v.scalar_tensor_tensor(out=c[:], in0=POS[:, 0, :], scalar=-1.0 - EP, in1=a[:], op0=ALU.add, op1=ALU.mult)
            v.drain()
            v.tensor_scalar(IDX[:, I_SRCROW2, :], c[:], float(EP), None, ALU.add)
            v.tensor_copy(IDX[:, I_SRC, :], src[:])
            v.tensor_copy(IDX[:, I_DST, :], dsti[:])
            v.tensor_scalar(b[:], TL[:, 1, :], -SKIP, SKIP, ALU.mult, ALU.add)
            v.drain()
            v.tensor_tensor(IDX[:, I_OUT, :], b[:], META[:, M_DST, :], ALU.add)
            v.scalar_tensor_tensor(out=c[:], in0=a[:], scalar=-1.0, in1=POS[:, 1, :], op0=ALU.mult, op1=ALU.add)
            v.drain()
            v.tensor_scalar(c[:], c[:], 1.0, None, ALU.add)
            v.drain()
            v.tensor_tensor(c[:], c[:], ew[:], ALU.mult)
            v.drain()
            v.tensor_tensor(META[:, M_NORM, :], c[:], TL[:, 0, :], ALU.mult)
            v.tensor_tensor(a[:], TL[:, 0, :], TL[:, 0, :], ALU.mult)
            v.drain()
            v.tensor_tensor(META[:, M_SELF, :], a[:], TL[:, 1, :], ALU.mult)
            v.tensor_scalar(META[:, M_REP, :], TL[:, 1, :], g["last_row"][:], None, ALU.max)
    st.close(g0=8 * C * ECH, g1=8 * C * ECH)


def layer_norm(nc, v, st, X, H, SQ, small, n, av):
    tiles = X.shape[1]
    v.reduce_sum(small[:, 0, :], X, AX.X)
    v.drain()
    v.tensor_scalar(small[:, 0, :], small[:, 0, :], 1.0 / D, None, ALU.mult)
    v.drain()
    v.tensor_tensor(H, X, over(small[:, 0, :].unsqueeze(2), [P, tiles, D]), ALU.subtract)
    v.drain()
    v.tensor_tensor(SQ, H, H, ALU.mult)
    v.drain()
    v.reduce_sum(small[:, 1, :], SQ, AX.X).then_inc(st["var"], 1)
    v.wait_ge(av, n + 3)
    v.tensor_tensor(H, H, over(small[:, 2, :].unsqueeze(2), [P, tiles, D]), ALU.mult)
    v.drain()


def norm_scalar(act, st, g, small, n):
    act.wait_ge(st["var"], n + 3)
    act.activation(small[:, 1, :], small[:, 1, :], ACT.Ln, bias=g["eps_col"][:], scale=1.0 / D)
    act.drain()
    act.activation(small[:, 2, :], small[:, 1, :], ACT.Exp, scale=-0.5).then_inc(st["root"], 1)


def norm_stage(nc, kind, t, d, g, out):
    st = Stage(nc, f"n_{kind}", ["tick", "ld0", "ld1", "st0", "st1", "b", "bc"], ["x", "var", "root", "h"])
    A = st.sb("A", [P, 2, C, D])
    B = st.sb("B", [P, 2, C, D + HEADS])
    X = st.sb("X", [P, 2, C, D])
    H = st.sb("H", [P, 2, C, D])
    Y = st.sb("Y", [P, 2, C, D])
    SQ = st.sb("SQ", [P, C, D])
    small = st.sb("small", [P, 2, 3, C])
    bias = st.sb("bias", [P, D])
    rb = st.sb("rb", [P, C, HEADS])
    ld, sto = [st["ld0"], st["ld1"]], [st["st0"], st["st1"]]
    edges = kind in ("a0", "x2")
    main = {"h0": t["x"], "a0": d["x1"], "x2": d["x1"], "fin": None}[kind]
    parts = [(ECH, 0, kind == "x2")] if edges else []
    parts.append((NCH, EP if edges else 0, kind == "fin"))
    nld = [1 + p[2] for p in parts]
    total = sum(p[0] for p in parts)

    def stores(k, n, row, edge_part):
        if kind == "h0":
            return [(chunk_rows(d["hx"][:, 0:D], n), H[:, k]), (chunk_rows(d["hx"][:, D:2 * D], n), A[:, k])]
        if kind == "a0":
            return [(chunk_rows(d["a0"], n, row), H[:, k])]
        if kind == "x2":
            s = [(chunk_rows(d["h2n"], n, row), H[:, k]), (chunk_rows(d["qy"][:, D:2 * D], n, row), Y[:, k])]
            if edge_part:
                s.append((chunk_rows(d["kvy"][:, 2 * D:3 * D], n), Y[:, k]))
            return s
        return [(chunk_rows(out, n), Y[:, k])]

    nst = [len(stores(0, 0, 0, edges and i == 0)) for i in range(len(parts))]

    with nc.Block() as block:
        @block.sync
        def _(sp):
            if kind == "x2":
                sp.dma_start(bias[:], over(t["gat_b"][2:3, :], [P, D])).then_inc(st["b"], 16)
            seen = 0
            for part, (chunks, row, second) in enumerate(parts):
                with sp.Fori(0, chunks // 2) as i:
                    for k in (0, 1):
                        n = 2 * i + k
                        if kind == "h0":
                            sp.wait_ge(sto[k], 32 * i)
                            sp.sem_inc(st["tick"], 1)
                        sp.wait_ge(st["h"], n + seen + 1)
                        if kind == "fin":
                            sp.dma_start(A[:, k], chunk_rows(d["qy"][:, D:2 * D], n, EP)).then_inc(ld[k], 16)
                            sp.dma_start(B[:, k], chunk_rows(d["res"], n)).then_inc(ld[k], 16)
                        else:
                            sp.dma_start(A[:, k], chunk_rows(main, n, row)).then_inc(ld[k], 16)
                            if second:
                                sp.dma_start(B[:, k, :, 0:D], chunk_rows(d["zg"], n)).then_inc(ld[k], 16)
                seen += chunks

        @block.vector
        def _(v):
            if kind == "x2":
                v.wait_ge(st["b"], 16)
            seen, loads, stored = 0, 0, 0
            for part, (chunks, row, second) in enumerate(parts):
                with v.Fori(0, chunks // 2) as i:
                    for k in (0, 1):
                        n = 2 * i + k + seen
                        v.wait_ge(ld[k], 16 * nld[part] * (i + 1) + loads)
                        if part == 0:
                            v.wait_ge(sto[k], 16 * nst[0] * i)
                        else:
                            v.wait_ge(sto[k], 16 * nst[part] * i + stored)
                        x = A[:, k]
                        if kind == "x2":
                            x = X[:, k]
                            bb = over(bias[:].unsqueeze(1), [P, C, D])
                            if second:
                                v.tensor_tensor(x, B[:, k, :, 0:D], bb, ALU.add)
                                v.drain()
                                v.tensor_scalar(x, x, 0.0, None, ALU.max)
                            else:
                                v.tensor_scalar(x, bb, 0.0, None, ALU.max)
                            v.drain()
                            v.tensor_tensor(x, x, A[:, k], ALU.add)
                            v.drain()
                        if kind == "fin":
                            x = X[:, k]
                            v.tensor_scalar(rb[:], B[:, k, :, D:D + HEADS], 1.0e-8, None, ALU.add)
                            v.drain()
                            v.reciprocal(rb[:], rb[:])
                            v.drain()
                            v.tensor_tensor(x.rearrange("p c (h e) -> p c h e", h=HEADS),
                                            B[:, k, :, 0:D].rearrange("p c (h e) -> p c h e", h=HEADS),
                                            over(rb[:].unsqueeze(3), [P, C, HEADS, HC]), ALU.mult)
                            v.drain()
                            v.tensor_tensor(x, x, A[:, k], ALU.add)
                            v.drain()
                        layer_norm(nc, v, st, x, H[:, k], SQ[:], small[:, k], n, st["root"])
                        if kind in ("h0", "a0"):
                            v.tensor_scalar(H[:, k], H[:, k], 0.0, None, ALU.max).then_inc(st["h"], 1)
                        else:
                            v.tensor_scalar(H[:, k], H[:, k], 0.0, None, ALU.max)
                            v.drain()
                            v.tensor_tensor(Y[:, k], H[:, k], x, ALU.add).then_inc(st["h"], 1)
                seen += chunks
                loads += 16 * nld[part] * (chunks // 2)
                stored += 16 * nst[part] * (chunks // 2)

        @block.scalar
        def _(act):
            seen = 0
            for part, (chunks, row, second) in enumerate(parts):
                with act.Fori(0, chunks // 2) as i:
                    for k in (0, 1):
                        n = 2 * i + k
                        norm_scalar(act, st, g, small[:, k], n + seen)
                        act.wait_ge(st["h"], n + seen + 3)
                        for to, of in stores(k, n, row, edges and part == 0):
                            act.dma_start(to, of).then_inc(sto[k], 16)
                seen += chunks
            last = sum(16 * nst[p] * (parts[p][0] // 2) for p in range(len(parts)))
            for k in (0, 1):
                act.wait_ge(sto[k], last)
    st.close()


def product_stage(nc, kind, t, d, g):
    layer = int(kind[-1]) if kind[-1].isdigit() else 0
    width = {"gcn": D, "gat": GW, "q": D, "kv": 2 * D}[kind.rstrip("0123456789")]
    st = Stage(nc, f"p_{kind}", ["tick", "w", "wx", "ld0", "ld1", "st0", "st1", "fin"], ["tr", "ht", "mm", "ev"])
    A = st.sb("A", [P, 2, C, D])
    X0 = st.sb("X0", [P, 2, C, D])
    HT = st.sb("HT", [D + 1, 2, CR])
    O = st.sb("O", [P, 2, C, width])
    W = st.sb("W", [D + 1, width])
    bcol = st.sb("bcol", [D, 1])
    att = st.sb("att", [D, 2, D])
    tmp = st.sb("tmp", [D, 2, D])
    ld, sto = [st["ld0"], st["ld1"]], [st["st0"], st["st1"]]
    ps, ident = g["ps"], g["ident"]
    R = lambda table, base=0: lambda n: chunk_rows(table, n, base)
    if kind in ("gcn1", "gcn2"):
        before, after = {"gcn1": (d["hx"][:, 0:D], d["h1"]), "gcn2": (d["h1"], d["h2"])}[kind]
        parts = [(ECH, R(d["z"]), None, R(after)),
                 (NCH, R(before, 0 if kind == "gcn1" else EP), None, R(after, EP))]
    elif kind == "gcn3":
        parts = [(ECH, R(d["z"]), R(d["x0d"]), R(d["x1"])), (NCH, R(d["h2"], EP), R(t["x"]), R(d["x1"], EP))]
    elif kind == "gat0":
        parts = [(ECH + NCH, R(d["a0"]), None, R(d["gt"]))]
    elif kind in ("gat1", "gat2"):
        parts = [(ECH + 2, R(d["zg"]), None, R(d["gt"]))]
    elif kind == "q":
        parts = [(ECH + NCH, R(d["h2n"]), None, R(d["qy"][:, 0:D]))]
    else:
        parts = [(ECH, R(d["h2n"]), None, R(d["kvy"][:, 0:2 * D]))]
    adds = kind == "gcn3"
    gcn = kind.startswith("gcn")
    gat = kind.startswith("gat")
    per_bank = 512 // width
    K = D + 1 if gcn else D
    chunks_in = sum(p[0] for p in parts)

    def o_at(c):
        return 2048 + (c // per_bank) * 512 + (c % per_bank) * width

    with nc.Block() as block:
        @block.sync
        def _(sp):
            if gcn:
                sp.dma_start(W[0:D, :], t[f"gcn_w{layer}"]).then_inc(st["w"], 16)
                sp.dma_start(W[D:D + 1, :], t[f"gcn_b{layer}"].unsqueeze(0)).then_inc(st["w"], 16)
            elif gat:
                sp.dma_start(W[0:D, 0:D], t["gat_w"][layer, :, :]).then_inc(st["w"], 16)
                for s, name in enumerate(("gat_src", "gat_dst")):
                    sp.dma_start(att[:, s, :], over(t[name][layer].rearrange("h c -> (h c)").unsqueeze(0), [D, D]))\
                        .then_inc(st["w"], 16)
                if layer:
                    sp.dma_start(bcol[:], t["gat_b"][layer - 1, :].unsqueeze(1)).then_inc(st["w"], 16)
            elif kind == "q":
                sp.dma_start(W[0:D, :], t["q_w"]).then_inc(st["w"], 16)
            else:
                sp.dma_start(W[0:D, 0:D], t["k_w"]).then_inc(st["w"], 16)
                sp.dma_start(W[0:D, D:2 * D], t["v_w"]).then_inc(st["w"], 16)
            seen = 0
            for chunks, read, add, write in parts:
                with sp.Fori(0, chunks // 2) as i:
                    for k in (0, 1):
                        n = 2 * i + k
                        sp.wait_ge(st["ev"], n + seen + 1)
                        sp.dma_start(A[:, k], read(n)).then_inc(ld[k], 16)
                        if adds:
                            sp.dma_start(X0[:, k], add(n)).then_inc(ld[k], 16)
                seen += chunks

        nw = 32 if gcn else (48 + 16 * (layer > 0)) if gat else 16 if kind == "q" else 32

        @block.vector
        def _(v):
            v.wait_ge(st["w"], nw)
            v.memset(HT[:, :, :], 1.0)
            v.drain()
            if gat:
                for s in (0, 1):
                    v.tensor_tensor(tmp[:, s, :], W[0:D, 0:D], att[:, s, :], ALU.mult)
                v.drain()
                for s in (0, 1):
                    v.reduce_sum(W[0:D, D + s * HEADS:D + (s + 1) * HEADS],
                                 tmp[:, s, :].rearrange("p (h e) -> p h e", h=HEADS), AX.X)
                v.drain()
            v.memset(tmp[:, 0, :], 0.0).then_inc(st["wx"], 1)
            with v.Fori(0, chunks_in // 2) as i:
                for k in (0, 1):
                    n = 2 * i + k
                    v.wait_ge(st["tr"], n + 3)
                    v.wait_ge(st["mm"], n + 1)
                    if gat and layer:
                        v.tensor_scalar(HT[0:D, k, :], ps[0:D, (k * 1024):(k * 1024) + CR], bcol[:], 0.0,
                                        ALU.add, ALU.max).then_inc(st["ht"], 1)
                    else:
                        v.tensor_copy(HT[0:D, k, :], ps[0:D, (k * 1024):(k * 1024) + CR]).then_inc(st["ht"], 1)

        @block.tensor
        def _(pe):
            pe.wait_ge(st["wx"], 1)

            def to_columns(n, k, i):
                pe.wait_ge(ld[k], 16 * (1 + adds) * (i + 1))
                pe.wait_ge(st["ht"], n + 1)
                for c in range(C):
                    last = nc.tensor.transpose(ps[0:D, (k * 1024) + c * P:(k * 1024) + (c + 1) * P], A[:, k, c, :], ident[:])
                last.then_inc(st["tr"], 1)

            def multiply(n, k):
                pe.wait_ge(st["ht"], n + 3)
                pe.wait_ge(st["ev"], n + 2)
                for c in range(C):
                    last = nc.tensor.matmul(ps[:, o_at(c):o_at(c) + width], HT[0:K, k, c * P:(c + 1) * P],
                                            W[0:K, :], start=True, stop=True)
                last.then_inc(st["mm"], 1)

            to_columns(0, 0, 0)
            with pe.Fori(0, chunks_in // 2 - 1) as i:
                to_columns(2 * i + 1, 1, i)
                multiply(2 * i, 0)
                to_columns(2 * i + 2, 0, i + 1)
                multiply(2 * i + 1, 1)
            m = chunks_in - 2
            to_columns(m + 1, 1, m // 2)
            multiply(m, 0)
            multiply(m + 1, 1)

        @block.scalar
        def _(act):
            seen = 0
            done = 0
            for chunks, read, add, write in parts:
                with act.Fori(0, chunks // 2) as i:
                    for k in (0, 1):
                        n = 2 * i + k
                        act.wait_ge(st["mm"], n + seen + 3)
                        act.wait_ge(sto[k], 16 * i + done)
                        c = 0
                        while c < C:
                            m = min(per_bank, C - c)
                            s = ps[:, o_at(c):o_at(c) + m * width].rearrange("p (c w) -> p c w", w=width)
                            f = ACT.Relu if kind in ("gcn1", "gcn2") else ACT.Copy
                            last = act.activation(O[:, k, c:c + m, :], s, f)
                            c += m
                        if adds:
                            last.then_inc(st["fin"], 1)
                            act.wait_ge(st["fin"], 2 * (n + seen) + 2)
                            act.sem_inc(st["ev"], 1)
                        else:
                            last.then_inc(st["ev"], 1)
                            act.wait_ge(st["ev"], n + seen + 3)
                        act.dma_start(write(n), O[:, k]).then_inc(sto[k], 16)
                seen += chunks
                done += 16 * (chunks // 2)
            for k in (0, 1):
                act.wait_ge(sto[k], done)

        if adds:
            @block.gpsimd
            def _(po):
                with po.Fori(0, chunks_in // 2) as i:
                    for k in (0, 1):
                        n = 2 * i + k
                        po.wait_ge(ld[k], 32 * (i + 1))
                        po.wait_ge(st["fin"], 2 * n + 1)
                        po.tensor_tensor(O[:, k], O[:, k], X0[:, k], ALU.add).then_inc(st["fin"], 1)
    st.close()


def aggregate(nc, kind, t, d, g):
    gcn, gat, edge = kind.startswith("gcn"), kind.startswith("gat"), kind == "edge"
    first = kind == "gcn1"
    w = D + 1 if edge else D
    gw = {True: 2 * D}.get(first, GW if gat else w)
    st = Stage(nc, f"a_{kind}", ["tick", "ix", "ld0", "ld1", "g0", "g1", "st0", "st1", "zero"], ["s", "pz", "ev"],
               {"pz": 2 * C, "ev": 2 * C})
    G = st.sb("G", [P, 2, C, gw])
    OWN = st.sb("OWN", [P, 2, C, gw]) if gcn else None
    MSG = st.sb("MSG", [P, 2, C, D]) if gat else None
    al = st.sb("al", [P, 2, C, HEADS])
    DR = st.sb("DR", [P, 2, CR], I32)
    S = st.sb("S", [P, 2, C, P])
    XC = st.sb("XC", [P, 2, C, P])
    DG = st.sb("DG", [P, 2, C, P]) if gcn else None
    Z = st.sb("Z", [P, 2, C, w])
    mc = st.sb("mc", [P, 2, M_N, C])
    ic = st.sb("ic", [P, 2, 2, C], I32)
    ld, got, sto = [st["ld0"], st["ld1"]], [st["g0"], st["g1"]], [st["st0"], st["st1"]]
    ps = g["ps"]
    table = {"gcn1": d["hx"], "gcn2": d["h1"], "gcn3": d["h2"]}.get(kind)
    nld = 1 + (2 if gat else 1 if edge else 0 if first else 1)
    ngot = 2 * C if first else C
    to = d["z3"] if edge else d["zg"] if gat else d["z"]
    nst = 2 if first else 1

    with nc.Block() as block:
        @block.sync
        def _(sp):
            with sp.Fori(0, ECH // 2) as i:
                for k in (0, 1):
                    n = 2 * i + k
                    sp.wait_ge(st["s"], n + 1)
                    sp.dma_start(DR[:, k], over(t["dst_lin"][bass.ds(n * CR, CR)].unsqueeze(0), [P, CR])).then_inc(ld[k], 16)
                    if gat:
                        sp.dma_start(G[:, k], chunk_tiles(d["gr"], n)).then_inc(ld[k], 16)
                        sp.dma_start(al[:, k], chunk_tiles(d["alpha"], n)).then_inc(ld[k], 16)
                    elif not first:
                        sp.wait_ge(st["pz"], C * n + C)
                        if edge:
                            sp.dma_start(G[:, k], chunk_tiles(d["msg3"], n)).then_inc(ld[k], 16)
                        else:
                            sp.dma_start(OWN[:, k], chunk_tiles(table[0:EP, :], n)).then_inc(ld[k], 16)

        if gcn:
            @block.gpsimd
            def _(po):
                with po.Fori(0, ECH // 2) as i:
                    for k in (0, 1):
                        n = 2 * i + k
                        po.wait_ge(st["pz"], C * n + C)
                        if first:
                            po.wait_ge(sto[k], 16 * nst * i)
                        po.tensor_copy(ic[:, k, 0, :], g["IDX"][:, I_SRC if first else I_SRCROW, bass.ds(n * C, C)])
                        po.tensor_copy(ic[:, k, 1, :], g["IDX"][:, I_DST, bass.ds(n * C, C)]).then_inc(st["ix"], 1)
                        po.wait_ge(st["ix"], n + 1)
                        po.sem_inc(st["tick"], 1)
                        for c in range(C):
                            po.indirect_dma_start(out=G[:, k, c, :], out_offset=None, in_=table,
                                                  in_offset=bass.IndirectOffsetOnAxis(ap=ic[:, k, 0, c:c + 1], axis=0),
                                                  bounds_check=table.shape[0] - 1, oob_is_err=False).then_inc(got[k], 16)
                            if first:
                                po.indirect_dma_start(out=OWN[:, k, c, :], out_offset=None, in_=table,
                                                      in_offset=bass.IndirectOffsetOnAxis(ap=ic[:, k, 1, c:c + 1], axis=0),
                                                      bounds_check=NP - 1, oob_is_err=False).then_inc(got[k], 16)

        @block.vector
        def _(v):
            v.memset(Z[:, 1, C - 1, :], 0.0).then_inc(st["zero"], 1)
            with v.Fori(0, ECH // 2) as i:
                for k in (0, 1):
                    n = 2 * i + k
                    v.wait_ge(ld[k], 16 * nld * (i + 1))
                    v.wait_ge(st["pz"], C * n + C)
                    v.tensor_copy(mc[:, k], g["META"][:, :, bass.ds(n * C, C)])
                    v.drain()
                    if gat:
                        v.tensor_tensor(MSG[:, k].rearrange("p c (h e) -> p c h e", h=HEADS),
                                        G[:, k, :, 0:D].rearrange("p c (h e) -> p c h e", h=HEADS),
                                        over(al[:, k].unsqueeze(3), [P, C, HEADS, HC]), ALU.mult)
                    for c in range(C):
                        row = DR[:, k, c * P:(c + 1) * P]
                        if gcn:
                            v.tensor_scalar(S[:, k, c, :], row, mc[:, k, M_DST, c:c + 1], mc[:, k, M_NORM, c:c + 1],
                                            ALU.is_equal, ALU.mult)
                            v.tensor_scalar(DG[:, k, c, :], g["ident"][:], mc[:, k, M_SELF, c:c + 1], None, ALU.mult)
                        else:
                            v.tensor_scalar(S[:, k, c, :], row, mc[:, k, M_DST, c:c + 1], None, ALU.is_equal)
                        last = v.tensor_scalar(XC[:, k, c, :], row, mc[:, k, M_PREV, c:c + 1], g["last_row"][:],
                                               ALU.is_equal, ALU.mult)
                    last.then_inc(st["s"], 1)

        @block.tensor
        def _(pe):
            pe.wait_ge(st["zero"], 1)
            with pe.Fori(0, ECH // 2) as i:
                for k in (0, 1):
                    n = 2 * i + k
                    pe.wait_ge(st["s"], n + 3)
                    if gcn:
                        pe.wait_ge(got[k], COUNTED[f"g{k}"] + 16 * ngot * (i + 1))
                    pe.wait_ge(ld[k], 16 * nld * (i + 1))
                    for c in range(C):
                        z = ps[:, ((k * C + c) % 2) * 512:((k * C + c) % 2) * 512 + w]
                        rows = MSG[:, k, c, :] if gat else G[:, k, c, 0:w]
                        nc.tensor.matmul(z, S[:, k, c, :], rows, start=True, stop=False)
                        if gcn:
                            nc.tensor.matmul(z, DG[:, k, c, :], OWN[:, k, c, 0:D], start=False, stop=False)
                        before = Z[:, k, c - 1, :] if c else Z[:, 1 - k, C - 1, :]
                        pe.wait_ge(st["ev"], C * n + c + 2 * C)
                        nc.tensor.matmul(z, XC[:, k, c, :], before, start=False, stop=True).then_inc(st["pz"], 1)

        @block.scalar
        def _(act):
            with act.Fori(0, ECH // 2) as i:
                for k in (0, 1):
                    n = 2 * i + k
                    act.wait_ge(sto[k], 16 * nst * i)
                    for c in range(C):
                        act.wait_ge(st["pz"], C * n + c + 2 * C + 1)
                        z = ps[:, ((k * C + c) % 2) * 512:((k * C + c) % 2) * 512 + w]
                        act.activation(Z[:, k, c, :], z, ACT.Copy).then_inc(st["ev"], 1)
                    act.wait_ge(st["ev"], C * n + 3 * C)
                    act.dma_start(chunk_tiles(to[0:EP, :], n), Z[:, k]).then_inc(sto[k], 16)
                    if first:
                        act.dma_start(chunk_tiles(d["x0d"], n), OWN[:, k, :, D:2 * D]).then_inc(sto[k], 16)
            for k in (0, 1):
                act.wait_ge(sto[k], 16 * nst * (ECH // 2))
    if gcn:
        st.close(g0=8 * ngot * ECH, g1=8 * ngot * ECH)
    else:
        st.close()


def gat_gather(nc, layer, t, d, g):
    st = Stage(nc, f"gg{layer}", ["tick", "ix", "g0", "g1", "st0", "st1"], [])
    G = st.sb("G", [P, 2, C, GW])
    ic = st.sb("ic", [P, 2, C], I32)
    got, sto = [st["g0"], st["g1"]], [st["st0"], st["st1"]]
    rows = ROWS if layer == 0 else ZROWS
    with nc.Block() as block:
        @block.gpsimd
        def _(po):
            with po.Fori(0, ECH // 2) as i:
                for k in (0, 1):
                    n = 2 * i + k
                    po.wait_ge(sto[k], 32 * i)
                    po.tensor_copy(ic[:, k, :], g["IDX"][:, I_SRCROW2 if layer else I_SRCROW, bass.ds(n * C, C)]).then_inc(st["ix"], 1)
                    po.wait_ge(st["ix"], n + 1)
                    po.sem_inc(st["tick"], 1)
                    for c in range(C):
                        po.indirect_dma_start(out=G[:, k, c, :], out_offset=None, in_=d["gt"],
                                              in_offset=bass.IndirectOffsetOnAxis(ap=ic[:, k, c:c + 1], axis=0),
                                              bounds_check=rows - 1, oob_is_err=False).then_inc(got[k], 16)

        @block.sync
        def _(sp):
            with sp.Fori(0, ECH // 2) as i:
                for k in (0, 1):
                    n = 2 * i + k
                    sp.wait_ge(got[k], COUNTED[f"g{k}"] + 16 * C * (i + 1))
                    sp.dma_start(chunk_tiles(d["gr"], n), G[:, k]).then_inc(sto[k], 16)
                    sp.dma_start(chunk_tiles(d["asrc"], n), G[:, k, :, D:D + HEADS]).then_inc(sto[k], 16)
            for k in (0, 1):
                sp.wait_ge(sto[k], 32 * (ECH // 2))
    st.close(g0=8 * C * ECH, g1=8 * C * ECH)


def gat_softmax(nc, layer, t, d, g):
    st = Stage(nc, f"gs{layer}", ["tick", "ld", "to_pe", "from_pe", "e", "st"], [])
    AS, AD, B, T, M = (st.sb(x, [P, J, HEADS]) for x in ("AS", "AD", "B", "T", "M"))
    sc = Scans(nc, st, g, HEADS)
    with nc.Block() as block:
        @block.sync
        def _(sp):
            sp.dma_start(AS[:], d["asrc"].rearrange("(q j) h -> q j h", j=J)).then_inc(st["ld"], 16)
            sp.dma_start(AD[:], d["gt"][0:EP, D + HEADS:GW].rearrange("(q j) h -> q j h", j=J)).then_inc(st["ld"], 16)
            sp.wait_ge(st["e"], 3)
            sp.dma_start(d["alpha"].rearrange("(q j) h -> q j h", j=J), AS[:]).then_inc(st["st"], 16)
            sp.wait_ge(st["st"], 16)

        @block.tensor
        def _(pe):
            pe_part(nc, st, g, sc, [True, False, True, False, True], pe)

        @block.scalar
        def _(act):
            act.wait_ge(st["e"], 1)
            act.activation(AS[:], AS[:], ACT.Exp).then_inc(st["e"], 1)

        @block.vector
        def _(v):
            sc.begin(v)
            v.wait_ge(st["ld"], 32)
            sc.spread(v, B, AD, T)
            v.tensor_tensor(AS[:], AS[:], B[:], ALU.add)
            v.drain()
            v.scalar_tensor_tensor(out=AS[:], in0=AS[:], scalar=0.2, in1=AS[:], op0=ALU.mult, op1=ALU.max)
            v.drain()
            sc.maximum(v, M, AS)
            sc.spread(v, B, M, T)
            v.tensor_tensor(AS[:], AS[:], B[:], ALU.subtract).then_inc(st["e"], 1)
            v.wait_ge(st["e"], 2)
            sc.total(v, M, AS)
            sc.spread(v, B, M, T)
            v.tensor_scalar(B[:], B[:], 1.0e-16, None, ALU.add)
            v.drain()
            v.reciprocal(M[:], B[:])
            v.drain()
            v.tensor_tensor(AS[:], AS[:], M[:], ALU.mult).then_inc(st["e"], 1)
    st.close()


def patch_last_rows(nc, t, d, g):
    st = Stage(nc, "patch", ["tick", "ld", "c", "g0", "st"], [])
    half = ET // 2
    tf = st.sb("tf", [half, 2, P])
    tii = st.sb("tii", [half, 2], I32)
    R = st.sb("R", [half, 2, 3 * D])
    kvy_tiles = d["kvy"].rearrange("(k p) w -> k p w", p=P)
    with nc.Block() as block:
        @block.sync
        def _(sp):
            sp.dma_start(tf[:], d["lin"][5, :].rearrange("(a k p) -> k a p", a=2, p=P)).then_inc(st["ld"], 16)
            sp.wait_ge(st["g0"], COUNTED["g0"] + 32)
            for a in (0, 1):
                sp.dma_start(kvy_tiles[a * half:(a + 1) * half, P - 1, :], R[:, a, :]).then_inc(st["st"], 16)
            sp.wait_ge(st["st"], 32)

        @block.vector
        def _(v):
            v.wait_ge(st["ld"], 16)
            v.tensor_copy(tii[:], tf[:, :, P - 1]).then_inc(st["c"], 1)

        @block.gpsimd
        def _(po):
            po.wait_ge(st["c"], 1)
            for a in (0, 1):
                po.indirect_dma_start(out=R[:, a, :], out_offset=None, in_=d["kvy"],
                                      in_offset=bass.IndirectOffsetOnAxis(ap=tii[:, a:a + 1], axis=0),
                                      bounds_check=EP - 1, oob_is_err=False).then_inc(st["g0"], 16)
    st.close(g0=32)


def attention(nc, t, d, g):
    st = Stage(nc, "att", ["tick", "ix", "ld0", "ld1", "g0", "g1", "st0", "st1"], ["s", "kv", "ev", "sc", "ex", "ms"])
    G = st.sb("G", [P, 2, C, 2 * D])
    K = st.sb("K", [P, 2, C, 3 * D])
    KD = st.sb("KD", [P, 2, C, 3 * D])
    DR = st.sb("DR", [P, 2, CR], I32)
    S = st.sb("S", [P, 2, C, P])
    PR = st.sb("PR", [P, C, D])
    ss = st.sb("ss", [P, 2, C, HEADS])
    MS = st.sb("MS", [P, 2, C, D + HEADS])
    mc = st.sb("mc", [P, 2, M_N, C])
    ic = st.sb("ic", [P, 2, C], I32)
    ld, got, sto = [st["ld0"], st["ld1"]], [st["g0"], st["g1"]], [st["st0"], st["st1"]]
    ps = g["ps"]
    with nc.Block() as block:
        @block.sync
        def _(sp):
            with sp.Fori(0, ECH // 2) as i:
                for k in (0, 1):
                    n = 2 * i + k
                    sp.wait_ge(st["kv"], n + 1)
                    sp.dma_start(DR[:, k], over(t["dst_lin"][bass.ds(n * CR, CR)].unsqueeze(0), [P, CR])).then_inc(ld[k], 16)
                    sp.dma_start(K[:, k], chunk_tiles(d["kvy"], n)).then_inc(ld[k], 16)

        @block.gpsimd
        def _(po):
            with po.Fori(0, ECH // 2) as i:
                for k in (0, 1):
                    n = 2 * i + k
                    po.wait_ge(sto[k], 48 * i)
                    po.tensor_copy(ic[:, k, :], g["IDX"][:, I_SRCROW, bass.ds(n * C, C)]).then_inc(st["ix"], 1)
                    po.wait_ge(st["ix"], n + 1)
                    po.sem_inc(st["tick"], 1)
                    for c in range(C):
                        po.indirect_dma_start(out=G[:, k, c, :], out_offset=None, in_=d["qy"],
                                              in_offset=bass.IndirectOffsetOnAxis(ap=ic[:, k, c:c + 1], axis=0),
                                              bounds_check=ROWS - 1, oob_is_err=False).then_inc(got[k], 16)

        @block.tensor
        def _(pe):
            with pe.Fori(0, ECH // 2) as i:
                for k in (0, 1):
                    n = 2 * i + k
                    pe.wait_ge(st["s"], n + 3)
                    pe.wait_ge(ld[k], 32 * (i + 1))
                    pe.wait_ge(st["ev"], n + 2)
                    for c in range(C):
                        last = nc.tensor.matmul(ps[:, c * 512:c * 512 + 3 * D], S[:, k, c, :], K[:, k, c, :],
                                                start=True, stop=True)
                    last.then_inc(st["kv"], 1)

        @block.scalar
        def _(act):
            with act.Fori(0, ECH // 2) as i:
                for k in (0, 1):
                    n = 2 * i + k
                    act.wait_ge(st["kv"], n + 3)
                    act.wait_ge(sto[k], 48 * i)
                    for c in range(C):
                        last = act.activation(KD[:, k, c, :], ps[:, c * 512:c * 512 + 3 * D], ACT.Copy)
                    last.then_inc(st["ev"], 1)
                    act.wait_ge(st["sc"], n + 3)
                    act.activation(MS[:, k, :, D:D + HEADS], ss[:, k], ACT.Exp).then_inc(st["ex"], 1)
                    act.wait_ge(st["ms"], n + 3)
                    act.dma_start(chunk_tiles(d["msg"], n), MS[:, k]).then_inc(sto[k], 16)
                    act.dma_start(chunk_tiles(d["ys"], n), G[:, k, :, D:2 * D]).then_inc(sto[k], 16)
                    act.dma_start(chunk_tiles(d["yd"], n), KD[:, k, :, 2 * D:3 * D]).then_inc(sto[k], 16)
            for k in (0, 1):
                act.wait_ge(sto[k], 48 * (ECH // 2))

        @block.vector
        def _(v):
            with v.Fori(0, ECH // 2) as i:
                for k in (0, 1):
                    n = 2 * i + k
                    v.wait_ge(ld[k], 32 * (i + 1))
                    v.wait_ge(st["kv"], n + 1)
                    v.tensor_copy(mc[:, k], g["META"][:, :, bass.ds(n * C, C)])
                    v.drain()
                    for c in range(C):
                        last = v.tensor_scalar(S[:, k, c, :], DR[:, k, c * P:(c + 1) * P], mc[:, k, M_DST, c:c + 1],
                                               mc[:, k, M_REP, c:c + 1], ALU.is_equal, ALU.mult)
                    last.then_inc(st["s"], 1)
                    v.wait_ge(st["ev"], n + 3)
                    v.wait_ge(got[k], COUNTED[f"g{k}"] + 16 * C * (i + 1))
                    v.tensor_tensor(PR[:], G[:, k, :, 0:D], KD[:, k, :, 0:D], ALU.mult)
                    v.drain()
                    v.reduce_sum(ss[:, k], PR[:].rearrange("p c (h e) -> p c h e", h=HEADS), AX.X)
                    v.drain()
                    v.tensor_scalar(ss[:, k], ss[:, k], -10.0, 10.0, ALU.max, ALU.min).then_inc(st["sc"], 1)
                    v.wait_ge(st["ex"], n + 3)
                    v.tensor_tensor(MS[:, k, :, 0:D].rearrange("p c (h e) -> p c h e", h=HEADS),
                                    KD[:, k, :, D:2 * D].rearrange("p c (h e) -> p c h e", h=HEADS),
                                    over(MS[:, k, :, D:D + HEADS].unsqueeze(3), [P, C, HEADS, HC]),
                                    ALU.mult).then_inc(st["ms"], 1)
    st.close(g0=8 * C * ECH, g1=8 * C * ECH)


def accumulate(nc, t, d, g):
    st = Stage(nc, "acc", ["tick", "ld0", "ld1", "k", "dump", "add0", "add1"], ["s", "mm", "ev"])
    MS = st.sb("MS", [P, 2, C, D + HEADS])
    SR = st.sb("SR", [P, 2, CR], I32)
    S = st.sb("S", [P, 2, C, CR])
    LOW = st.sb("LOW", [P, C, CR])
    junk = st.sb("junk", [P, CR])
    cnt = st.sb("cnt", [P, C])
    dump = st.sb("dump", [P, C])
    sc = st.sb("sc", [P, 2, C])
    SF = st.sb("SF", [P, ET])
    ic = st.sb("ic", [P, 2, C], I32)
    O = st.sb("O", [P, 2, C, D + HEADS])
    ld, add = [st["ld0"], st["ld1"]], [st["add0"], st["add1"]]
    ps = g["ps"]
    WM = D + HEADS

    def at(b):
        return (b // 4) * 512 + (b % 4) * P

    with nc.Block() as block:
        @block.sync
        def _(sp):
            sp.dma_start(dump[:], t["dump_row"]).then_inc(st["dump"], 16)
            with sp.Fori(0, ECH // 2) as i:
                for k in (0, 1):
                    n = 2 * i + k
                    sp.wait_ge(st["mm"], n + 1)
                    sp.dma_start(SR[:, k], over(t["src_lin"][bass.ds(n * CR, CR)].unsqueeze(0), [P, CR])).then_inc(ld[k], 16)
                    sp.dma_start(MS[:, k], chunk_tiles(d["msg"], n)).then_inc(ld[k], 16)

        @block.gpsimd
        def _(po):
            po.memset(LOW[:], 1.0)
            po.drain()
            po.affine_select(out=LOW[:], in_=LOW[:], compare_op=ALU.is_gt, fill=0.0, base=0,
                             pattern=[[P, C], [-1, CR]], channel_multiplier=1).then_inc(st["k"], 1)
            with po.Fori(0, ECH // 2) as i:
                for k in (0, 1):
                    n = 2 * i + k
                    po.wait_ge(st["ev"], n + 3)
                    po.sem_inc(st["tick"], 1)
                    for c in range(C):
                        po.indirect_dma_start(out=d["res"], in_=O[:, k, c, :], in_offset=None,
                                              out_offset=bass.IndirectOffsetOnAxis(ap=ic[:, k, c:c + 1], axis=0),
                                              bounds_check=NP + CR - 1, oob_is_err=True,
                                              compute_op=ALU.add).then_inc(add[k], 16)
                    po.wait_ge(add[k], COUNTED[f"add{k}"] + 16 * C * (i + 1))
            for k in (0, 1):
                po.wait_ge(add[k], COUNTED[f"add{k}"] + 16 * C * (ECH // 2))

        @block.tensor
        def _(pe):
            with pe.Fori(0, ECH // 2) as i:
                for k in (0, 1):
                    n = 2 * i + k
                    pe.wait_ge(st["s"], n + 3)
                    pe.wait_ge(ld[k], 32 * (i + 1))
                    pe.wait_ge(st["ev"], n + 2)
                    for b in range(C):
                        for a in range(C):
                            last = nc.tensor.matmul(ps[:, at(b):at(b) + WM], S[:, k, a, b * P:(b + 1) * P],
                                                    MS[:, k, a, :], start=(a == 0), stop=(a == C - 1))
                    last.then_inc(st["mm"], 1)

        @block.vector
        def _(v):
            v.wait_ge(st["k"], 1)
            v.wait_ge(st["dump"], 16)
            v.tensor_copy(SF[:], g["IDX"][:, I_SRC, :])
            v.drain()
            with v.Fori(0, ECH // 2) as i:
                for k in (0, 1):
                    n = 2 * i + k
                    v.wait_ge(ld[k], 32 * (i + 1))
                    v.wait_ge(st["mm"], n + 1)
                    v.tensor_copy(sc[:, k], SF[:, bass.ds(n * C, C)])
                    v.drain()
                    for c in range(C):
                        v.tensor_scalar(S[:, k, c, :], SR[:, k, :], sc[:, k, c:c + 1], None, ALU.is_equal)
                    v.drain()
                    for c in range(C):
                        v.scalar_tensor_tensor(out=junk[:], in0=S[:, k, c, :], scalar=1.0, in1=LOW[:, c, :],
                                               op0=ALU.mult, op1=ALU.mult, accum_out=cnt[:, c:c + 1])
                        v.drain()
                    v.tensor_scalar(cnt[:], cnt[:], 0.5, None, ALU.is_gt).then_inc(st["s"], 1)
                    v.drain()
                    v.tensor_tensor(junk[:, 0:C], dump[:], sc[:, k], ALU.subtract)
                    v.drain()
                    v.tensor_tensor(junk[:, 0:C], junk[:, 0:C], cnt[:], ALU.mult)
                    v.drain()
                    v.wait_ge(add[k], COUNTED[f"add{k}"] + 16 * C * i)
                    v.tensor_tensor(ic[:, k], junk[:, 0:C], sc[:, k], ALU.add)
                    v.wait_ge(st["mm"], n + 3)
                    v.tensor_copy(O[:, k, 0:4, :], ps[:, 0:512].rearrange("p (c w) -> p c w", w=P)[:, :, 0:WM])
                    v.drain()
                    v.tensor_copy(O[:, k, 4:C, :],
                                  ps[:, 512:512 + 3 * P].rearrange("p (c w) -> p c w", w=P)[:, :, 0:WM]).then_inc(st["ev"], 1)
    st.close(add0=8 * C * ECH, add1=8 * C * ECH)


def gates(nc, t, d, g):
    st = Stage(nc, "gate", ["tick", "ix", "w", "ld0", "ld1", "g0", "g1", "st0", "st1"],
               ["x", "var", "root", "h", "tr", "ht", "mm", "ab", "ms"])
    Y = st.sb("Y", [P, 2, 2 * C, D])
    RG = st.sb("RG", [P, 2, 2 * C, D + HEADS])
    EA = st.sb("EA", [DE, 2, CR])
    H = st.sb("H", [P, 2 * C, D])
    SQ = st.sb("SQ", [P, 2 * C, D])
    small = st.sb("small", [P, 3, 2 * C])
    rb = st.sb("rb", [P, 2 * C, HEADS])
    B = st.sb("B", [P, 2, C, D])
    HT = st.sb("HT", [D + 1, C, 2 * P])
    W = st.sb("W", [D + 1, 3, 2 * D])
    AB, TT, LG = (st.sb(x, [P, C, 2 * D]) for x in ("AB", "TT", "LG"))
    MS = st.sb("MS", [P, 2, C, D + 1])
    GE = st.sb("GE", [P, C, D])
    ic = st.sb("ic", [P, 2, 2, C], I32)
    ld, got, sto = [st["ld0"], st["ld1"]], [st["g0"], st["g1"]], [st["st0"], st["st1"]]
    ps, ident = g["ps"], g["ident"]
    z = ps[:, 2048:2048 + C * 256].rearrange("p (c w) -> p c w", w=256)[:, :, 0:2 * D]

    with nc.Block() as block:
        @block.sync
        def _(sp):
            for s, (w, b) in enumerate((("we", "be"), ("wn", "bn"))):
                cols = slice(s * D, (s + 1) * D)
                for part in range(2):
                    sp.dma_start(W[0:D, part, cols], t[w][part * D:(part + 1) * D, :]).then_inc(st["w"], 16)
                sp.dma_start(W[0:DE, 2, cols], t[w][2 * D:2 * D + DE, :]).then_inc(st["w"], 16)
                sp.dma_start(W[D:D + 1, 0, cols], t[b].unsqueeze(0)).then_inc(st["w"], 16)
            with sp.Fori(0, ECH // 2) as i:
                for k in (0, 1):
                    n = 2 * i + k
                    sp.wait_ge(st["mm"], n + 1)
                    sp.dma_start(Y[:, k, 0:C, :], chunk_tiles(d["ys"], n)).then_inc(ld[k], 16)
                    sp.dma_start(Y[:, k, C:2 * C, :], chunk_tiles(d["yd"], n)).then_inc(ld[k], 16)
                    sp.dma_start(EA[:, k, :], t["ea_t"][:, bass.ds(n * CR, CR)]).then_inc(ld[k], 16)

        @block.gpsimd
        def _(po):
            with po.Fori(0, ECH // 2) as i:
                for k in (0, 1):
                    n = 2 * i + k
                    po.wait_ge(st["h"], n + 1)
                    po.tensor_copy(ic[:, k, 0, :], g["IDX"][:, I_SRC, bass.ds(n * C, C)])
                    po.tensor_copy(ic[:, k, 1, :], g["IDX"][:, I_DST, bass.ds(n * C, C)]).then_inc(st["ix"], 1)
                    po.wait_ge(st["ix"], n + 1)
                    po.sem_inc(st["tick"], 1)
                    for s in (0, 1):
                        for c in range(C):
                            po.indirect_dma_start(out=RG[:, k, s * C + c, :], out_offset=None, in_=d["res"],
                                                  in_offset=bass.IndirectOffsetOnAxis(ap=ic[:, k, s, c:c + 1], axis=0),
                                                  bounds_check=NP - 1, oob_is_err=False).then_inc(got[k], 16)

        @block.vector
        def _(v):
            v.wait_ge(st["w"], 128)
            v.memset(HT[:], 1.0)
            v.memset(MS[:], 1.0)
            v.drain()
            with v.Fori(0, ECH // 2) as i:
                for k in (0, 1):
                    n = 2 * i + k
                    v.wait_ge(ld[k], 48 * (i + 1))
                    v.wait_ge(got[k], COUNTED[f"g{k}"] + 16 * 2 * C * (i + 1))
                    v.wait_ge(st["tr"], n + 2)
                    v.tensor_scalar(rb[:], RG[:, k, :, D:D + HEADS], 1.0e-8, None, ALU.add)
                    v.drain()
                    v.reciprocal(rb[:], rb[:])
                    v.drain()
                    v.tensor_tensor(H[:].rearrange("p c (h e) -> p c h e", h=HEADS),
                                    RG[:, k, :, 0:D].rearrange("p c (h e) -> p c h e", h=HEADS),
                                    over(rb[:].unsqueeze(3), [P, 2 * C, HEADS, HC]), ALU.mult)
                    v.drain()
                    v.tensor_tensor(Y[:, k], Y[:, k], H[:], ALU.add)
                    v.drain()
                    layer_norm(nc, v, st, Y[:, k], H[:], SQ[:], small[:], n, st["root"])
                    v.wait_ge(sto[k], 32 * i)
                    v.tensor_scalar(H[:], H[:], 0.0, None, ALU.max)
                    v.drain()
                    v.tensor_tensor(B[:, k], Y[:, k, C:2 * C, :], H[:, C:2 * C, :], ALU.add).then_inc(st["h"], 1)
                    v.wait_ge(st["tr"], n + 3)
                    v.wait_ge(st["mm"], n + 2)
                    v.tensor_copy(HT[0:D], ps[0:D, 0:C * 256].rearrange("p (c w) -> p c w", w=256)).then_inc(st["ht"], 1)
                    v.wait_ge(st["mm"], n + 3)
                    v.wait_ge(st["ab"], n + 3)
                    v.tensor_scalar(GE[:], z[:, :, 0:D], 0.0, None, ALU.is_ge)
                    v.drain()
                    v.tensor_tensor(GE[:], GE[:], TT[:, :, 0:D], ALU.max)
                    v.tensor_scalar(TT[:, :, D:2 * D], TT[:, :, 0:D], 1.0, None, ALU.add)
                    v.drain()
                    v.reciprocal(TT[:, :, 0:D], TT[:, :, D:2 * D])
                    v.scalar_tensor_tensor(out=LG[:, :, D:2 * D], in0=z[:, :, D:2 * D], scalar=0.0,
                                           in1=LG[:, :, D:2 * D], op0=ALU.max, op1=ALU.add)
                    v.drain()
                    v.tensor_tensor(GE[:], GE[:], TT[:, :, 0:D], ALU.mult)
                    v.drain()
                    v.tensor_tensor(MS[:, k, :, 0:D], GE[:], LG[:, :, D:2 * D], ALU.mult).then_inc(st["ms"], 1)

        @block.tensor
        def _(pe):
            pe.wait_ge(st["w"], 128)
            with pe.Fori(0, ECH // 2) as i:
                for k in (0, 1):
                    n = 2 * i + k
                    pe.wait_ge(st["h"], n + 3)
                    pe.wait_ge(st["ht"], n + 2)
                    for c in range(C):
                        for s in (0, 1):
                            last = nc.tensor.transpose(ps[0:D, c * 256 + s * P:c * 256 + (s + 1) * P],
                                                       H[:, s * C + c, :], ident[:])
                    last.then_inc(st["tr"], 1)
                    pe.wait_ge(st["ht"], n + 3)
                    pe.wait_ge(st["ms"], n + 2)
                    for c in range(C):
                        o = ps[:, 2048 + c * 256:2048 + c * 256 + 2 * D]
                        nc.tensor.matmul(o, HT[0:D + 1, c, 0:P], W[0:D + 1, 0, :], start=True, stop=False)
                        nc.tensor.matmul(o, HT[0:D, c, P:2 * P], W[0:D, 1, :], start=False, stop=False)
                        last = nc.tensor.matmul(o, EA[:, k, c * P:(c + 1) * P], W[0:DE, 2, :], start=False, stop=True)
                    last.then_inc(st["mm"], 1)

        @block.scalar
        def _(act):
            with act.Fori(0, ECH // 2) as i:
                for k in (0, 1):
                    n = 2 * i + k
                    norm_scalar(act, st, g, small[:], n)
                    act.wait_ge(st["mm"], n + 3)
                    act.wait_ge(st["ms"], n + 2)
                    act.activation(AB[:], z, ACT.Abs)
                    act.drain()
                    act.activation(TT[:], AB[:], ACT.Exp, scale=-1.0)
                    act.drain()
                    act.activation(LG[:], TT[:], ACT.Ln, bias=1.0).then_inc(st["ab"], 1)
                    act.wait_ge(st["ms"], n + 3)
                    act.dma_start(chunk_tiles(d["msg3"], n), MS[:, k]).then_inc(sto[k], 16)
                    act.dma_start(chunk_tiles(d["base"], n), B[:, k]).then_inc(sto[k], 16)
            for k in (0, 1):
                act.wait_ge(sto[k], 32 * (ECH // 2))
    st.close(g0=2 * 8 * C * ECH, g1=2 * 8 * C * ECH)


def finish(nc, t, d, g, out):
    st = Stage(nc, "end", ["tick", "ix", "ld0", "ld1", "sc0", "sc1"], ["o"])
    Z = st.sb("Z", [P, 2, C, D + 1])
    B = st.sb("B", [P, 2, C, D])
    r = st.sb("r", [P, C])
    O = st.sb("O", [P, 2, C, D])
    ic = st.sb("ic", [P, 2, C], I32)
    ld, sca = [st["ld0"], st["ld1"]], [st["sc0"], st["sc1"]]
    with nc.Block() as block:
        @block.sync
        def _(sp):
            with sp.Fori(0, ECH // 2) as i:
                for k in (0, 1):
                    n = 2 * i + k
                    sp.wait_ge(st["o"], n + 1)
                    sp.dma_start(Z[:, k], chunk_tiles(d["z3"], n)).then_inc(ld[k], 16)
                    sp.dma_start(B[:, k], chunk_tiles(d["base"], n)).then_inc(ld[k], 16)

        @block.vector
        def _(v):
            with v.Fori(0, ECH // 2) as i:
                for k in (0, 1):
                    n = 2 * i + k
                    v.wait_ge(ld[k], 32 * (i + 1))
                    v.tensor_scalar(r[:], Z[:, k, :, D], 1.0, None, ALU.max)
                    v.drain()
                    v.reciprocal(r[:], r[:])
                    v.drain()
                    v.wait_ge(sca[k], COUNTED[f"sc{k}"] + 16 * C * i)
                    v.tensor_tensor(O[:, k], Z[:, k, :, 0:D], over(r[:].unsqueeze(2), [P, C, D]), ALU.mult)
                    v.drain()
                    v.tensor_tensor(O[:, k], O[:, k], B[:, k], ALU.add).then_inc(st["o"], 1)

        @block.gpsimd
        def _(po):
            with po.Fori(0, ECH // 2) as i:
                for k in (0, 1):
                    n = 2 * i + k
                    po.wait_ge(sca[k], COUNTED[f"sc{k}"] + 16 * C * i)
                    po.tensor_copy(ic[:, k, :], g["IDX"][:, I_OUT, bass.ds(n * C, C)]).then_inc(st["ix"], 1)
                    po.wait_ge(st["ix"], n + 1)
                    po.sem_inc(st["tick"], 1)
                    po.wait_ge(st["o"], n + 3)
                    po.sem_inc(st["tick"], 1)
                    for c in range(C):
                        po.indirect_dma_start(out=out, in_=O[:, k, c, :], in_offset=None,
                                              out_offset=bass.IndirectOffsetOnAxis(ap=ic[:, k, c:c + 1], axis=0),
                                              bounds_check=NP - 1, oob_is_err=False).then_inc(sca[k], 16)
            for k in (0, 1):
                po.wait_ge(sca[k], COUNTED[f"sc{k}"] + 16 * C * (ECH // 2))
    st.close(sc0=8 * C * ECH, sc1=8 * C * ECH)


def kernel(**inputs):
    import numpy as np
    import concourse.bacc as bacc
    from concourse.bass_utils import run_bass_kernel_spmd

    a = {k: np.asarray(v) for k, v in inputs.items()}

    def padded(x, rows, value):
        x = np.ascontiguousarray(x)
        return np.concatenate([x, np.full((rows - x.shape[0], *x.shape[1:]), value, x.dtype)])

    src, dst = padded(a["src"], EP, N), padded(a["dst"], EP, N)
    ew = padded(a["edge_weight"], EP, 0)
    around = np.concatenate([np.full(1, -1, dst.dtype), dst, np.full(1, N + 1, dst.dtype)])
    arrays = {
        "x": padded(a["x"], NP, 0),
        "src_lin": src, "dst_lin": dst, "src_tiles": src.reshape(ET, P).T, "dst_tiles": dst.reshape(ET, P).T,
        "dst_runs": np.stack([around[i:i + EP].reshape(P, J) for i in range(3)], axis=1),
        "first": dst[::P], "prev_tiles": np.broadcast_to(around[0:EP:P], (P, ET)),
        "ew_runs": ew.reshape(P, J), "ew_tiles": ew.reshape(ET, P).T,
        "edge_no": np.arange(EP, dtype=np.float32).reshape(P, J),
        "dump_row": (NP + np.arange(CR, dtype=np.float32)).reshape(C, P).T,
        "ea_t": padded(a["edge_attr_64"], EP, 0).T,
        "gat_w": a["L1_gnn_W"], "gat_src": a["L1_gnn_att_src"], "gat_dst": a["L1_gnn_att_dst"],
        "gat_b": a["L1_gnn_bias"], "q_w": a["L2_gnn_qW"], "k_w": a["L2_gnn_kW"], "v_w": a["L2_gnn_vW"],
        "we": a["L3_gnn_W_e"], "be": a["L3_gnn_b_e"], "wn": a["L3_gnn_W_n"], "bn": a["L3_gnn_b_n"],
    }
    for i in (1, 2, 3):
        arrays[f"gcn_w{i}"], arrays[f"gcn_b{i}"] = a[f"L0_gnn_W{i}"], a[f"L0_gnn_b{i}"]
    arrays = {k: np.ascontiguousarray(v) for k, v in arrays.items()}

    nc = bacc.Bacc("TRN2", target_bir_lowering=False, num_devices=1)
    t = {k: nc.dram_tensor(f"in_{k}", v.shape, mybir.dt.from_np(v.dtype), kind="ExternalInput").ap()
         for k, v in arrays.items()}
    out = nc.dram_tensor("out_0", (NP, D), F32, kind="ExternalOutput").ap()
    build(nc, t, out)
    r = run_bass_kernel_spmd(nc, [{f"in_{k}": v for k, v in arrays.items()}], core_ids=[0])
    return r.results[0]["out_0"][0:N]
```

```python
import concourse.bass as bass
from concourse import mybir
from contextlib import ExitStack

ALU = mybir.AluOpType
ACT = mybir.ActivationFunctionType
AX = mybir.AxisListType
F32 = mybir.dt.float32
I32 = mybir.dt.int32

P = 128
N, D, E, DE = 50000, 96, 25000, 64
HEADS = 4
HC = D // HEADS
C = 7
CR = C * P
ET = 28 * C
EP = ET * P
ECH = ET // C
NCH = 56
NP = NCH * CR
ROWS = EP + NP
J = EP // P
ZROWS = EP + 2 * CR
GW = D + 2 * HEADS
BIG = 1.0e30
SKIP = 65536.0
EPS = 1.0e-5
M_DST, M_PREV, M_NORM, M_SELF, M_REP, M_N = 0, 1, 2, 3, 4, 5
I_SRCROW, I_SRCROW2, I_SRC, I_DST, I_OUT, I_N = 0, 1, 2, 3, 4, 5


POOL_DMA = {}
COUNTED = {}


class Stage:

    def __init__(self, nc, name, plain, credited, credit_of=None):
        self.nc, self.stack = nc, ExitStack()
        self.name = name
        self.s = {n: POOL_DMA[n] if n in POOL_DMA else self.stack.enter_context(nc.semaphore(f"{name}_{n}"))
                  for n in [*plain, *credited]}
        with nc.Block() as block:
            @block.sync
            def _(sp):
                for n in self.s:
                    if n not in POOL_DMA:
                        sp.sem_clear(self.s[n])
        with nc.Block() as block:
            @block.sync
            def _(sp):
                for n in credited:
                    sp.sem_inc(self.s[n], (credit_of or {}).get(n, 2))
                sp.drain()

    def __getitem__(self, n):
        return self.s[n]

    def sb(self, name, shape, dt=F32):
        return self.stack.enter_context(self.nc.sbuf_tensor(f"{self.name}_{name}", shape, dt))

    def close(self, **pool):
        for n, added in pool.items():
            COUNTED[n] += added
        self.stack.close()


def chunk_rows(table, n, base=0):
    return table[bass.ds(n * CR + base, CR), :].rearrange("(p c) d -> p c d", c=C)


def chunk_tiles(table, n):
    return table[bass.ds(n * CR, CR), :].rearrange("(c p) d -> p c d", p=P)


def over(ap, shape):
    return ap.to_broadcast(shape)


def build(nc, t, out):
    top = ExitStack()
    with top:
        def dram(name, shape, dt=F32):
            return nc.dram_tensor(name, shape, dt).ap()

        def sb(name, shape, dt=F32):
            return top.enter_context(nc.sbuf_tensor(name, shape, dt))

        for n in ("g0", "g1", "sc0", "sc1", "add0", "add1"):
            POOL_DMA[n] = top.enter_context(nc.semaphore(n))
            COUNTED[n] = 0
        ident = sb("ident", [P, P])
        eps_col = sb("eps_col", [P, 1])
        last_row = sb("last_row", [P, 1])
        META = sb("META", [P, M_N, ET])
        IDX = sb("IDX", [P, I_N, ET], I32)
        FL = {n: sb(f"fl_{n}", [P, J]) for n in ("same_prev", "same_next", "tail", "first", "last",
                                                "pen_prev", "pen_first")}
        RT = {n: sb(f"rt_{n}", [HEADS, P]) for n in ("whole_prev", "whole_next", "pen_whole")}
        ps = top.enter_context(nc.psum_tensor("ps", [P, 4096], F32))

        d = dict(
            lin=dram("lin", (6, EP)), search=dram("search", (ET, 3 * P)),
            hx=dram("hx", (NP, 2 * D)), x0d=dram("x0d", (EP, D)),
            h1=dram("h1", (ROWS, D)), h2=dram("h2", (ROWS, D)),
            x1=dram("x1", (ROWS, D)), gt=dram("gt", (ROWS, GW)), gt2=dram("gt2", (EP + P, GW)),
            gr=dram("gr", (EP, GW)), asrc=dram("asrc", (EP, HEADS)), alpha=dram("alpha", (EP, HEADS)),
            zr=dram("zr", (EP, D)), qy=dram("qy", (ROWS, 2 * D)),
            ykv=dram("ykv", (EP, 3 * D)), ys=dram("ys", (EP, D)), yd=dram("yd", (EP, D)),
            msg=dram("msg", (EP, D + HEADS)), res=dram("res", (NP + CR, D + HEADS)),
            msg3=dram("msg3", (EP, D + 1)), base=dram("base", (EP, D)),
        )
        g = dict(nc=nc, t=t, d=d, out=out, ident=ident, last_row=last_row, eps_col=eps_col,
                 META=META, IDX=IDX, FL=FL, RT=RT, ps=ps)
        prepare(nc, t, d, g)
        run(g, find_sources(g), rows(g, "h1"))
        run(g, aggregate(g, "gcn1"), rows(g, "h2"))
        run(g, aggregate(g, "gcn2"), rows(g, "x1"))
        run(g, aggregate(g, "gcn3"), rows(g, "gt"))
        run(g, rows(g, "gt_edges"))
        for layer in range(3):
            if layer == 0:
                run(g, gat_gather(g, layer), rows(g, "qy"))
            else:
                run(g, gat_gather(g, layer))
            gat_softmax(nc, layer, t, d, g)
            run(g, aggregate(g, f"gat{layer}"))
        run(g, rows(g, "qkv_edges"))
        patch_last_rows(nc, t, d, g)
        run(g, attention(g))
        accumulate(nc, t, d, g)
        run(g, rows(g, "out"))
        gates(nc, t, d, g)
        run(g, aggregate(g, "edge"))


class Work:

    def __init__(self, st, per=1, pool=None, deep=False):
        self.st, self.per, self.pool, self.deep = st, per, pool or {}, deep
        self.before, self.steps, self.after = {}, {}, {}

    def on(self, engine, *steps, before=None, after=None):
        self.steps[engine] = steps
        self.before[engine], self.after[engine] = before, after


def run(g, *works):
    nc = g["nc"]
    pairs = ECH // 2

    def program(engine, eng):
        mine = [w for w in works if engine in w.steps]
        if not mine:
            return
        lags = max([lag for w in mine for _, lag in w.steps[engine]], default=0)

        def turns(i, edge=True):
            for k in (0, 1):
                for w in mine:
                    for j in range(w.per):
                        slot = w.per * k + j
                        for step, lag in w.steps[engine]:
                            back = slot - lag
                            n = 2 * w.per * i + back
                            if edge and not 0 <= n < ECH * w.per:
                                continue
                            if w.deep:
                                step(eng, n, back % 2, w.per * i + back // 2, back % (2 * w.per), i + back // (2 * w.per))
                            else:
                                step(eng, n, back % 2, w.per * i + back // 2)

        for w in mine:
            if w.before[engine]:
                w.before[engine](eng)
        if lags:
            turns(0)
        if any(w.steps[engine] for w in mine):
            with eng.Fori(1 if lags else 0, pairs) as i:
                turns(i, False)
        if lags:
            turns(pairs)
        for w in mine:
            if w.after[engine]:
                w.after[engine](eng)

    with nc.Block() as block:
        @block.sync
        def _(sp):
            program("sync", sp)

        @block.gpsimd
        def _(po):
            program("gpsimd", po)

        @block.vector
        def _(v):
            program("vector", v)

        @block.tensor
        def _(pe):
            program("tensor", pe)

        @block.scalar
        def _(act):
            program("scalar", act)
    for w in reversed(works):
        w.st.close(**w.pool)


class Scans:

    def __init__(self, nc, st, g, heads):
        self.nc, self.st, self.g, self.heads, self.n = nc, st, g, heads, 0
        self.edge = st.sb("edge", [P, HEADS])
        self.edge_t = st.sb("edge_t", [HEADS, P])
        self.carry_t = st.sb("carry_t", [HEADS, P + 1])
        self.carry = st.sb("carry", [P, HEADS])

    def begin(self, v):
        v.memset(self.edge[:], 0.0)
        v.drain()

    def cross(self, v, y, col, flags, op0, op1, first, back):
        nc, g, st, H = self.nc, self.g, self.st, self.heads
        v.drain()
        v.tensor_copy(self.edge[:, 0:H], y[:, col, :]).then_inc(st["to_pe"], 1)
        v.wait_ge(st["from_pe"], 2 * self.n + 1)
        v.tensor_copy(self.edge_t[:], g["ps"][0:HEADS, 0:P])
        v.memset(self.carry_t[:], first)
        v.drain()
        if back:
            v.tensor_tensor_scan(self.carry_t[:, 0:P][:, ::-1], g["RT"][flags][:, ::-1],
                                 self.edge_t[:, ::-1], first, op0, op1).then_inc(st["to_pe"], 1)
        else:
            v.tensor_tensor_scan(self.carry_t[:, 1:P + 1], g["RT"][flags][:],
                                 self.edge_t[:], first, op0, op1).then_inc(st["to_pe"], 1)
        v.wait_ge(st["from_pe"], 2 * self.n + 2)
        v.tensor_copy(self.carry[:], g["ps"][:, 512:512 + HEADS])
        v.drain()
        self.n += 1

    def total(self, v, y, x):
        F = self.g["FL"]
        for h in range(self.heads):
            v.tensor_tensor_scan(y[:, :, h], F["same_prev"][:], x[:, :, h], 0.0, ALU.mult, ALU.add)
        self.cross(v, y, J - 1, "whole_prev", ALU.mult, ALU.add, 0.0, False)
        for h in range(self.heads):
            v.scalar_tensor_tensor(out=y[:, :, h], in0=F["first"][:], scalar=self.carry[:, h:h + 1],
                                   in1=y[:, :, h], op0=ALU.mult, op1=ALU.add)
        v.drain()

    def maximum(self, v, y, x):
        F = self.g["FL"]
        for h in range(self.heads):
            v.tensor_tensor_scan(y[:, :, h], F["pen_prev"][:], x[:, :, h], -BIG, ALU.add, ALU.max)
        self.cross(v, y, J - 1, "pen_whole", ALU.add, ALU.max, -BIG, False)
        for h in range(self.heads):
            v.scalar_tensor_tensor(out=y[:, :, h], in0=F["pen_first"][:], scalar=self.carry[:, h:h + 1],
                                   in1=y[:, :, h], op0=ALU.add, op1=ALU.max)
        v.drain()

    def spread(self, v, y, x, tmp):
        F = self.g["FL"]
        for h in range(self.heads):
            v.tensor_tensor(tmp[:, :, h], x[:, :, h], F["tail"][:], ALU.mult)
        v.drain()
        for h in range(self.heads):
            v.tensor_tensor_scan(y[:, ::-1, h], F["same_next"][:, ::-1], tmp[:, ::-1, h], 0.0, ALU.mult, ALU.add)
        self.cross(v, y, 0, "whole_next", ALU.mult, ALU.add, 0.0, True)
        for h in range(self.heads):
            v.scalar_tensor_tensor(out=y[:, :, h], in0=F["last"][:], scalar=self.carry[:, h:h + 1],
                                   in1=y[:, :, h], op0=ALU.mult, op1=ALU.add)
        v.drain()


def pe_part(nc, st, g, sc, backs, pe):
    for n, back in enumerate(backs):
        pe.wait_ge(st["to_pe"], 2 * n + 1)
        nc.tensor.transpose(g["ps"][0:HEADS, 0:P], sc.edge[:], g["ident"][:]).then_inc(st["from_pe"], 1)
        pe.wait_ge(st["to_pe"], 2 * n + 2)
        c = sc.carry_t[:, 1:P + 1] if back else sc.carry_t[:, 0:P]
        nc.tensor.transpose(g["ps"][:, 512:512 + HEADS], c, g["ident"][0:HEADS, 0:HEADS]).then_inc(st["from_pe"], 1)


def prepare(nc, t, d, g):
    st = Stage(nc, "prep", ["tick", "ld", "k", "to_pe", "from_pe", "rt", "sq", "out"], [])
    raw = st.sb("raw", [P, 3, J], I32)
    ew = st.sb("ew", [P, J])
    eno = st.sb("eno", [P, J])
    dp, dc, dn = (st.sb(x, [P, J]) for x in ("dp", "dc", "dn"))
    X, Y, Z, T = (st.sb(x, [P, J, 1]) for x in ("X", "Y", "Z", "T"))
    whole = st.sb("whole", [P, 3, HEADS])
    L = st.sb("L", [P, 6, J])
    ti = st.sb("ti", [P, 2, ET], I32)
    zero = st.sb("zero", [P, C * (D + HEADS)])
    sc = Scans(nc, st, g, 1)
    F, RT, ps, ident = g["FL"], g["RT"], g["ps"], g["ident"]

    with nc.Block() as block:
        @block.sync
        def _(sp):
            sp.dma_start(raw[:], t["dst_runs"]).then_inc(st["ld"], 16)
            sp.dma_start(ew[:], t["ew_runs"]).then_inc(st["ld"], 16)
            sp.dma_start(eno[:], t["edge_no"]).then_inc(st["ld"], 16)
            sp.dma_start(ti[:, 0, :], t["dst_tiles"]).then_inc(st["ld"], 16)
            sp.dma_start(ti[:, 1, :], t["prev_tiles"]).then_inc(st["ld"], 16)
            sp.wait_ge(st["k"], 3)
            with sp.Fori(0, NCH + 1) as i:
                sp.dma_start(d["res"][bass.ds(i * CR, CR), :].rearrange("(p c) d -> p (c d)", c=C),
                             zero[:]).then_inc(st["out"], 16)
            sp.wait_ge(st["out"], 16 * (NCH + 1))
            sp.wait_ge(st["sq"], 3)
            sp.dma_start(d["lin"].rearrange("s (q j) -> q s j", j=J), L[:]).then_inc(st["ld"], 16)
            sp.wait_ge(st["ld"], 96)
            for s in range(3):
                sp.dma_start(d["search"][:, s * P:(s + 1) * P],
                             d["lin"][s, :].rearrange("(k f) -> k f", f=P)).then_inc(st["ld"], 16)
            sp.wait_ge(st["ld"], 144)

        @block.gpsimd
        def _(po):
            po.memset(ident[:], 0.0)
            po.memset(g["last_row"][:], 0.0)
            po.drain()
            po.affine_select(out=ident[:], in_=ident[:], compare_op=ALU.not_equal, fill=1.0,
                             base=0, pattern=[[-1, P]], channel_multiplier=1).then_inc(st["k"], 1)
            po.affine_select(out=g["last_row"][:], in_=g["last_row"][:], compare_op=ALU.not_equal, fill=1.0,
                             base=1 - P, pattern=[[1, 1]], channel_multiplier=1).then_inc(st["k"], 1)
            po.memset(zero[:], 0.0).then_inc(st["k"], 1)

        @block.tensor
        def _(pe):
            pe.wait_ge(st["k"], 2)
            pe.wait_ge(st["rt"], 1)
            for n in range(3):
                last = nc.tensor.transpose(ps[0:HEADS, 1024 + n * P:1024 + (n + 1) * P], whole[:, n, :], ident[:])
            last.then_inc(st["rt"], 1)
            pe_part(nc, st, g, sc, [False, True, True], pe)

        @block.scalar
        def _(act):
            act.wait_ge(st["sq"], 1)
            act.activation(Z[:], Z[:], ACT.Sqrt).then_inc(st["sq"], 1)

        @block.vector
        def _(v):
            v.memset(g["eps_col"][:], EPS)
            sc.begin(v)
            v.wait_ge(st["ld"], 80)
            v.wait_ge(st["k"], 3)
            for n, a in enumerate((dp, dc, dn)):
                v.tensor_copy(a[:], raw[:, n, :])
            v.drain()
            v.tensor_tensor(F["same_prev"][:], dc[:], dp[:], ALU.is_equal)
            v.tensor_tensor(F["same_next"][:], dc[:], dn[:], ALU.is_equal)
            v.tensor_scalar(F["first"][:], dc[:], dp[:, 0:1], None, ALU.is_equal)
            v.tensor_scalar(F["last"][:], dc[:], dn[:, J - 1:J], None, ALU.is_equal)
            v.tensor_tensor(whole[:, 0, :], over(dc[:, J - 1:J], [P, HEADS]), over(dp[:, 0:1], [P, HEADS]), ALU.is_equal)
            v.tensor_tensor(whole[:, 1, :], over(dc[:, 0:1], [P, HEADS]), over(dn[:, J - 1:J], [P, HEADS]), ALU.is_equal)
            v.drain()
            v.tensor_scalar(F["tail"][:], F["same_next"][:], -1.0, 1.0, ALU.mult, ALU.add)
            v.tensor_scalar(F["pen_prev"][:], F["same_prev"][:], -1.0, BIG, ALU.add, ALU.mult)
            v.tensor_scalar(F["pen_first"][:], F["first"][:], -1.0, BIG, ALU.add, ALU.mult)
            v.tensor_scalar(whole[:, 2, :], whole[:, 0, :], -1.0, BIG, ALU.add, ALU.mult).then_inc(st["rt"], 1)
            v.wait_ge(st["rt"], 2)
            for n, name in enumerate(("whole_prev", "whole_next", "pen_whole")):
                v.tensor_copy(RT[name][:], ps[0:HEADS, 1024 + n * P:1024 + (n + 1) * P])
            v.drain()
            v.tensor_copy(X[:, :, 0], ew[:])
            v.drain()
            sc.total(v, Y, X)
            sc.spread(v, X, Y, T)
            v.tensor_scalar(Y[:], X[:], 1.0, None, ALU.add)
            v.drain()
            v.tensor_scalar(X[:], Y[:], 0.0, None, ALU.is_gt)
            v.tensor_scalar(Z[:], Y[:], 1.0e-30, None, ALU.max).then_inc(st["sq"], 1)
            v.wait_ge(st["sq"], 2)
            v.reciprocal(Y[:], Z[:])
            v.drain()
            v.tensor_tensor(L[:, 3, :], Y[:, :, 0], X[:, :, 0], ALU.mult)
            v.drain()
            v.tensor_scalar(Y[:, :, 0], eno[:], 1.0, None, ALU.mult)
            v.drain()
            sc.spread(v, X, Y, T)
            v.tensor_copy(L[:, 5, :], X[:, :, 0])
            v.tensor_copy(L[:, 4, :], F["tail"][:])
            v.tensor_copy(L[:, 0, :], dc[:])
            v.tensor_tensor(L[:, 2, :], L[:, 3, :], F["tail"][:], ALU.mult)
            v.scalar_tensor_tensor(out=L[:, 1, :], in0=eno[:], scalar=1.0, in1=F["tail"][:], op0=ALU.add, op1=ALU.mult)
            v.tensor_copy(g["META"][:, M_DST, :], ti[:, 0, :])
            v.tensor_copy(g["META"][:, M_PREV, :], ti[:, 1, :]).then_inc(st["sq"], 1)
    st.close()


def find_sources(g):
    nc, t, d = g["nc"], g["t"], g["d"]
    st = Stage(nc, "find", ["tick", "ld", "tl", "g0", "g1"], ["kf", "fine"])
    w = Work(st, pool=dict(g0=8 * C * ECH, g1=8 * C * ECH))
    half = ET // 2
    src = st.sb("src", [P, ET], I32)
    srcf = st.sb("srcf", [P, ET])
    firsti = st.sb("firsti", [P, ET], I32)
    first = st.sb("first", [P, ET])
    junk = st.sb("junk", [P, C, ET])
    kf = st.sb("kf", [P, 2, C])
    kc = st.sb("kc", [P, 2, C], I32)
    S = st.sb("S", [P, 2, C, 3 * P])
    acc = st.sb("acc", [P, 2, 2, C])
    POS = st.sb("POS", [P, 2, ET])
    TR = st.sb("TR", [half, 3, 2, P])
    TL = st.sb("TL", [P, 3, ET])
    ew = st.sb("ew", [P, ET])
    a, b, c = (st.sb(x, [P, ET]) for x in ("a", "b", "c"))
    dsti = st.sb("dsti", [P, ET], I32)
    got = [st["g0"], st["g1"]]
    META, IDX, ps = g["META"], g["IDX"], g["ps"]

    def load(sp):
        sp.dma_start(src[:], t["src_tiles"]).then_inc(st["ld"], 16)
        sp.dma_start(firsti[:], over(t["first"].unsqueeze(0), [P, ET])).then_inc(st["ld"], 16)
        sp.dma_start(ew[:], t["ew_tiles"]).then_inc(st["ld"], 16)
        sp.dma_start(dsti[:], t["dst_tiles"]).then_inc(st["ld"], 16)
        for s in range(3):
            sp.dma_start(TR[:, s], d["lin"][3 + s, :].rearrange("(a k p) -> k a p", a=2, p=P)).then_inc(st["ld"], 16)

    def turn_runs(pe):
        pe.wait_ge(st["ld"], 112)
        for s in range(3):
            for h in (0, 1):
                last = nc.tensor.transpose(ps[:, (2 * s + h) * P:(2 * s + h) * P + half], TR[:, s, h, :],
                                           g["ident"][0:half, 0:half])
        last.then_inc(st["tl"], 1)

    def begin(v):
        v.wait_ge(st["ld"], 112)
        v.tensor_copy(srcf[:], src[:])
        v.tensor_copy(first[:], firsti[:])
        v.wait_ge(st["tl"], 1)
        for s in range(3):
            for h in (0, 1):
                v.tensor_copy(TL[:, s, h * half:(h + 1) * half], ps[:, (2 * s + h) * P:(2 * s + h) * P + half])
        v.drain()

    def coarse(v, n, k, i):
        v.drain()
        v.wait_ge(st["fine"], n + 1)
        for c_ in range(C):
            v.tensor_scalar(junk[:, c_, :], first[:], srcf[:, bass.ds(n * C + c_, 1)], -1.0, ALU.is_le, ALU.add,
                            accum_out=kf[:, k, c_:c_ + 1])
        v.drain()
        v.tensor_scalar(kc[:, k, :], kf[:, k, :], 0.0, None, ALU.max).then_inc(st["kf"], 1)

    def fetch(po, n, k, i):
        po.wait_ge(st["kf"], n + 3)
        po.sem_inc(st["tick"], 1)
        for c_ in range(C):
            po.indirect_dma_start(out=S[:, k, c_, :], out_offset=None, in_=d["search"],
                                  in_offset=bass.IndirectOffsetOnAxis(ap=kc[:, k, c_:c_ + 1], axis=0),
                                  bounds_check=ET - 1, oob_is_err=False).then_inc(got[k], 16)

    base = dict(COUNTED)

    def fine(v, n, k, i):
        v.drain()
        v.wait_ge(got[k], base[f"g{k}"] + 16 * C * (i + 1))
        for s in (0, 1):
            for c_ in range(C):
                v.scalar_tensor_tensor(out=junk[:, c_, 0:P], in0=S[:, k, c_, 0:P],
                                       scalar=srcf[:, bass.ds(n * C + c_, 1)],
                                       in1=S[:, k, c_, (s + 1) * P:(s + 2) * P],
                                       op0=ALU.is_equal, op1=ALU.mult, accum_out=acc[:, k, s, c_:c_ + 1])
            v.drain()
        v.tensor_copy(POS[:, :, bass.ds(n * C, C)], acc[:, k, :, :]).then_inc(st["fine"], 1)

    def end(v):
        v.drain()
        v.tensor_scalar(a[:], POS[:, 0, :], 0.5, None, ALU.is_gt)
        v.tensor_scalar(b[:], srcf[:], float(EP), None, ALU.add)
        v.drain()
        v.scalar_tensor_tensor(out=c[:], in0=POS[:, 0, :], scalar=-1.0, in1=b[:], op0=ALU.add, op1=ALU.subtract)
        v.drain()
        v.tensor_tensor(c[:], c[:], a[:], ALU.mult)
        v.drain()
        v.tensor_tensor(IDX[:, I_SRCROW, :], c[:], b[:], ALU.add)
        v.drain()
        v.scalar_tensor_tensor(out=c[:], in0=POS[:, 0, :], scalar=-1.0 - EP, in1=a[:], op0=ALU.add, op1=ALU.mult)
        v.drain()
        v.tensor_scalar(IDX[:, I_SRCROW2, :], c[:], float(EP), None, ALU.add)
        v.tensor_copy(IDX[:, I_SRC, :], src[:])
        v.tensor_copy(IDX[:, I_DST, :], dsti[:])
        v.tensor_scalar(b[:], TL[:, 1, :], -SKIP, SKIP, ALU.mult, ALU.add)
        v.drain()
        v.tensor_tensor(IDX[:, I_OUT, :], b[:], META[:, M_DST, :], ALU.add)
        v.scalar_tensor_tensor(out=c[:], in0=a[:], scalar=-1.0, in1=POS[:, 1, :], op0=ALU.mult, op1=ALU.add)
        v.drain()
        v.tensor_scalar(c[:], c[:], 1.0, None, ALU.add)
        v.drain()
        v.tensor_tensor(c[:], c[:], ew[:], ALU.mult)
        v.drain()
        v.tensor_tensor(META[:, M_NORM, :], c[:], TL[:, 0, :], ALU.mult)
        v.tensor_tensor(a[:], TL[:, 0, :], TL[:, 0, :], ALU.mult)
        v.drain()
        v.tensor_tensor(META[:, M_SELF, :], a[:], TL[:, 1, :], ALU.mult)
        v.tensor_scalar(META[:, M_REP, :], TL[:, 1, :], g["last_row"][:], None, ALU.max)

    w.on("sync", before=load)
    w.on("tensor", before=turn_runs)
    w.on("vector", (coarse, 0), (fine, 1), before=begin, after=end)
    w.on("gpsimd", (fetch, 0))
    return w


def norm_stats(v, st, X, small, S6):
    tiles = X.shape[1]
    for c in range(tiles):
        v.bn_stats(S6[:, c, :], X[:, c, :])
    v.drain()
    v.tensor_tensor(small[:, 0, :], S6[:, :, 1], S6[:, :, 4], ALU.add)
    v.tensor_tensor(small[:, 2, :], S6[:, :, 1], S6[:, :, 4], ALU.subtract)
    v.tensor_tensor(small[:, 1, :], S6[:, :, 2], S6[:, :, 5], ALU.add)
    v.drain()
    v.tensor_scalar(small[:, 0, :], small[:, 0, :], -0.5, None, ALU.mult)
    v.tensor_tensor(small[:, 2, :], small[:, 2, :], small[:, 2, :], ALU.mult)
    v.drain()
    v.scalar_tensor_tensor(out=small[:, 1, :], in0=small[:, 2, :], scalar=D / 4.0, in1=small[:, 1, :],
                           op0=ALU.mult, op1=ALU.add).then_inc(st["var"], 1)


def norm_shift(v, st, small):
    v.reciprocal(small[:, 2, :], small[:, 3, :])
    v.drain()
    v.tensor_tensor(small[:, 4, :], small[:, 0, :], small[:, 2, :], ALU.mult).then_inc(st["nb"], 1)


def groups_of(width):
    m = min(4, 512 // width)
    return [list(range(c, min(c + m, C))) for c in range(0, C, m)]


def rows(g, kind):
    nc, t, d, out = g["nc"], g["t"], g["d"], g["out"]
    edges = kind.endswith("edges")
    norm = kind not in ("h2", "x1")
    product = kind != "out"
    width = {"gt": GW, "gt_edges": GW, "qkv_edges": 3 * D}.get(kind, D)
    bias = kind in ("h1", "h2", "x1")
    G = len(groups_of(width))
    has_y = kind in ("qy", "qkv_edges", "out")
    NB = 2 if edges else 4
    per = dict(tr=2, ht=2, mm=G, ev=G)
    per.update({n: 1 for n in ("var", "root", "nb", "h", "y")})
    st = Stage(nc, f"r_{kind}", ["tick", "w", "wx", "st0", "st1"] + [f"{x}{b}" for x in ("ld", "sh") for b in range(NB)],
               list(per), {n: NB * p for n, p in per.items()})

    def at(name, n, back=0, part=None):
        return per[name] * (n - back + NB) + (per[name] if part is None else part + 1)

    w = Work(st, 1 if edges else 2, deep=True)
    ld, sh, sto = [st[f"ld{b}"] for b in range(NB)], [st[f"sh{b}"] for b in range(NB)], [st["st0"], st["st1"]]
    ps, ident = g["ps"], g["ident"]
    ow = {"qy": 2 * D, "qkv_edges": 4 * D, "out": D}.get(kind, width)
    if kind == "h1":
        XH = st.sb("XH", [P, NB, C, 2 * D])
        H, A = XH[:, :, :, 0:D], XH[:, :, :, D:2 * D]
    else:
        H, A = (st.sb("H", [P, 2, C, D]) if norm else None), st.sb("A", [P, NB, C, D])
    X2 = st.sb("X2", [P, 2, C, D]) if has_y else None
    R2 = st.sb("R2", [P, NB, C, D + HEADS])
    S6 = st.sb("S6", [P, C, 6])
    small = st.sb("small", [P, 2, 5, C])
    rb = st.sb("rb", [P, C, HEADS])
    HT = st.sb("HT", [D + 1, 2, CR])
    O = st.sb("O", [P, 2, C, ow])
    W = st.sb("W", [D + 1, width])
    extra = weights(g, st, W, kind)
    K = D + 1 if bias else D
    brow = st.sb("brow", [P, D])
    row = 0 if edges else EP

    first = {"h1": t["x"], "h2": d["h1"], "x1": d["h2"], "out": d["qy"][:, D:2 * D]}.get(kind, d["x1"])
    second = {"x1": t["x"], "qkv_edges": d["zr"], "out": d["res"]}.get(kind)
    second_row = 0

    def xs(k, b):
        return X2[:, k] if has_y else A[:, b], H[:, b if kind == "h1" else k]

    to = {"h1": d["h1"], "h2": d["h2"], "x1": d["x1"], "gt": d["gt"], "gt_edges": d["gt"], "qy": d["qy"],
          "out": out}.get(kind)
    nld = 2 if second is not None else 1
    nst = 2 if kind == "qkv_edges" else 1

    def load(sp, n, k, i, b, j):
        if kind == "h1":
            sp.wait_ge(sh[b], 16 * j)
            sp.sem_inc(st["tick"], 1)
        sp.wait_ge(st[used], at(used, n, NB))
        sp.dma_start(A[:, b], chunk_rows(first, n, 0 if kind == "h1" else row)).then_inc(ld[b], 16)
        if second is not None:
            to2 = R2[:, b] if kind == "out" else R2[:, b, :, 0:D]
            sp.dma_start(to2, chunk_rows(second, n)).then_inc(ld[b], 16)

    def begin_v(v):
        if product:
            v.memset(HT[:, :, :], 1.0)
            v.drain()
            extra["vector"](v)
        if kind == "qy":
            v.wait_ge(st["w"], extra["loads"])
            v.tensor_scalar(brow[:], brow[:], 0.0, None, ALU.max)
            v.drain()

    def stats(v, n, k, i, b, j):
        X, _ = xs(k, b)
        v.drain()
        v.wait_ge(ld[b], 16 * nld * (j + 1))
        v.wait_ge(st["h"], at("h", n, 2))
        if kind == "qy":
            v.tensor_tensor(X, A[:, b], over(brow[:].unsqueeze(1), [P, C, D]), ALU.add)
            v.drain()
        if kind == "qkv_edges":
            v.tensor_tensor(X, A[:, b], R2[:, b, :, 0:D], ALU.add)
            v.drain()
        if kind == "out":
            v.tensor_scalar(rb[:], R2[:, b, :, D:D + HEADS], 1.0e-8, None, ALU.add)
            v.drain()
            v.reciprocal(rb[:], rb[:])
            v.drain()
            v.tensor_tensor(X.rearrange("p c (h e) -> p c h e", h=HEADS),
                            R2[:, b, :, 0:D].rearrange("p c (h e) -> p c h e", h=HEADS),
                            over(rb[:].unsqueeze(3), [P, C, HEADS, HC]), ALU.mult)
            v.drain()
            v.tensor_tensor(X, X, A[:, b], ALU.add)
            v.drain()
        norm_stats(v, st, X, small[:, k], S6)

    def shift(v, n, k, i, b, j):
        v.wait_ge(st["root"], at("root", n))
        norm_shift(v, st, small[:, k])

    def sum_y(v, n, k, i, b, j):
        X, Hn = xs(k, b)
        v.wait_ge(st["h"], at("h", n))
        v.wait_ge(sto[k], 16 * nst * i)
        to_y = O[:, k] if kind == "out" else O[:, k, :, D:2 * D]
        v.tensor_tensor(to_y, X, Hn, ALU.add).then_inc(st["y"], 1)

    def to_sbuf(v, n, k, i, b, j):
        for h, cols in enumerate((slice(0, 4 * P), slice(4 * P, CR))):
            v.wait_ge(st["tr"], at("tr", n, part=h))
            if h == 0:
                v.wait_ge(st["mm"], at("mm", n, 2))
            v.tensor_copy(HT[0:D, k, cols], ps[0:D, 2048 + cols.start:2048 + cols.stop]).then_inc(st["ht"], 1)

    def root(act, n, k, i, b, j):
        act.wait_ge(st["var"], at("var", n))
        act.activation(small[:, k, 3, :], small[:, k, 1, :], ACT.Sqrt, bias=g["eps_col"][:], scale=1.0 / D)           .then_inc(st["root"], 1)

    def apply(act, n, k, i, b, j):
        X, Hn = xs(k, b)
        if product:
            act.wait_ge(st["tr"], at("tr", n, 2))
        if has_y:
            act.wait_ge(st["y"], at("y", n, 2))
        act.wait_ge(st["nb"], at("nb", n))
        for c in range(C):
            last = act.activation(Hn[:, c, :], X[:, c, :], ACT.Relu, bias=small[:, k, 4, c:c + 1],
                                  scale=small[:, k, 2, c:c + 1])
        last.then_inc(st["h"], 1)

    def store_h(act, n, k, i, b, j):
        act.wait_ge(st["h"], at("h", n))
        act.dma_start(chunk_rows(d["hx"], n), XH[:, b]).then_inc(sh[b], 16)

    def turn(pe, n, k, i, b, j):
        if norm:
            pe.wait_ge(st["h"], at("h", n))
            rows_ = xs(k, b)[1]
        else:
            pe.wait_ge(ld[b], 16 * nld * (j + 1))
            rows_ = A[:, b]
        for h, tiles in enumerate(((0, 1, 2, 3), (4, 5, 6))):
            pe.wait_ge(st["ht"], at("ht", n, 1, h))
            for c in tiles:
                last = nc.tensor.transpose(ps[0:D, 2048 + c * P:2048 + (c + 1) * P], rows_[:, c, :], ident[:])
            last.then_inc(st["tr"], 1)

    def multiply(pe, n, k, i, b, j):
        for q, tiles in enumerate(groups_of(width)):
            pe.wait_ge(st["ht"], at("ht", n, part=int(tiles[-1] >= 4)))
            pe.wait_ge(st["ev"], at("ev", n, part=q - 2))
            bank = 3072 + 512 * ((G * k + q) % 2)
            for m, c in enumerate(tiles):
                last = nc.tensor.matmul(ps[:, bank + m * width:bank + (m + 1) * width],
                                        HT[0:K, k, c * P:(c + 1) * P], W[0:K, :], start=True, stop=True)
            last.then_inc(st["mm"], 1)

    def from_psum(eng, n, k, i, b, j):
        eng.wait_ge(sto[k], 16 * nst * i)
        for q, tiles in enumerate(groups_of(width)):
            eng.wait_ge(st["mm"], at("mm", n, part=q))
            bank = 3072 + 512 * ((G * k + q) % 2)
            z = ps[:, bank:bank + len(tiles) * width].rearrange("p (c w) -> p c w", w=width)
            cs = slice(tiles[0], tiles[-1] + 1)
            if kind == "x1":
                eng.tensor_tensor(O[:, k, cs, :], z, R2[:, b, cs, 0:D], ALU.add).then_inc(st["ev"], 1)
            elif kind == "qkv_edges":
                eng.activation(O[:, k, cs, 0:D], z[:, :, 0:D], ACT.Copy)
                eng.activation(O[:, k, cs, 2 * D:4 * D], z[:, :, D:3 * D], ACT.Copy).then_inc(st["ev"], 1)
            else:
                eng.activation(O[:, k, cs, 0:width], z, ACT.Relu if kind in ("h1", "h2") else ACT.Copy)                   .then_inc(st["ev"], 1)

    def store(act, n, k, i, b, j):
        if product:
            act.wait_ge(st["ev"], at("ev", n))
        if has_y:
            act.wait_ge(st["y"], at("y", n))
        if kind == "qkv_edges":
            act.dma_start(chunk_rows(d["qy"], n, row), O[:, k, :, 0:2 * D]).then_inc(sto[k], 16)
            act.dma_start(chunk_rows(d["ykv"], n), O[:, k, :, D:4 * D]).then_inc(sto[k], 16)
        else:
            act.dma_start(chunk_rows(to, n, 0 if kind == "out" else row), O[:, k]).then_inc(sto[k], 16)

    def end(act):
        for k in (0, 1):
            act.wait_ge(sto[k], 16 * nst * (ECH * w.per // 2))
        if kind == "h1":
            for b in range(NB):
                act.wait_ge(sh[b], 16 * (ECH * w.per // NB))

    used = "var" if has_y else "ev" if kind == "x1" else "h" if norm else "tr"
    w.on("sync", (load, 0), before=lambda sp: extra["sync"](sp, brow))
    if norm and product:
        w.on("vector", *([(sum_y, 2)] if has_y else []), (stats, 0), (shift, 1), (to_sbuf, 2), before=begin_v)
        w.on("scalar", (root, 0), (apply, 1), *([(store_h, 1)] if kind == "h1" else []), (from_psum, 2), (store, 2),
             after=end)
        w.on("tensor", (multiply, 2), (turn, 1), before=extra["tensor"])
    elif norm:
        w.on("vector", (sum_y, 2), (stats, 0), (shift, 1), before=begin_v)
        w.on("scalar", (root, 0), (apply, 1), (store, 2), after=end)
    elif kind == "x1":
        w.on("vector", (to_sbuf, 1), (from_psum, 2), before=begin_v)
        w.on("scalar", (store, 2), after=end)
        w.on("tensor", (multiply, 1), (turn, 0), before=extra["tensor"])
    else:
        w.on("vector", (to_sbuf, 1), before=begin_v)
        w.on("scalar", (from_psum, 2), (store, 2), after=end)
        w.on("tensor", (multiply, 1), (turn, 0), before=extra["tensor"])
    return w


def weights(g, st, W, kind):
    t = g["t"]
    layer = {"h1": 1, "h2": 2, "x1": 3, "gcn1": 1, "gcn2": 2, "gcn3": 3}.get(kind)
    gat = {"gt": 0, "gt_edges": 0, "gat0": 1, "gat1": 2}.get(kind)
    att = st.sb("att", [D, 2, D])
    tmp = st.sb("tmp", [D, 2, D])
    loads = [0]

    def sync(sp, brow=None):
        if layer:
            sp.dma_start(W[0:D, :], t[f"gcn_w{layer}"]).then_inc(st["w"], 16)
            sp.dma_start(W[D:D + 1, :], t[f"gcn_b{layer}"].unsqueeze(0)).then_inc(st["w"], 16)
        elif gat is not None:
            sp.dma_start(W[0:D, 0:D], t["gat_w"][gat, :, :]).then_inc(st["w"], 16)
            for s, name in enumerate(("gat_src", "gat_dst")):
                sp.dma_start(att[:, s, :], over(t[name][gat].rearrange("h c -> (h c)").unsqueeze(0), [D, D]))\
                    .then_inc(st["w"], 16)
        elif kind == "qy":
            sp.dma_start(W[0:D, :], t["q_w"]).then_inc(st["w"], 16)
            sp.dma_start(brow[:], over(t["gat_b"][2:3, :], [P, D])).then_inc(st["w"], 16)
        elif kind == "qkv_edges":
            for s, name in enumerate(("q_w", "k_w", "v_w")):
                sp.dma_start(W[0:D, s * D:(s + 1) * D], t[name]).then_inc(st["w"], 16)

    n = 32 if layer or kind == "qy" else 48 if gat is not None or kind == "qkv_edges" else 0

    def vector(v):
        if gat is None:
            return
        v.wait_ge(st["w"], n)
        for s in (0, 1):
            v.tensor_tensor(tmp[:, s, :], W[0:D, 0:D], att[:, s, :], ALU.mult)
        v.drain()
        for s in (0, 1):
            last = v.reduce_sum(W[0:D, D + s * HEADS:D + (s + 1) * HEADS],
                                tmp[:, s, :].rearrange("p (h e) -> p h e", h=HEADS), AX.X)
        last.then_inc(st["wx"], 1)

    def tensor(pe):
        if n:
            pe.wait_ge(st["w"], n)
        if gat is not None:
            pe.wait_ge(st["wx"], 1)

    return dict(sync=sync, vector=vector, tensor=tensor, loads=n)


def aggregate(g, kind):
    nc, t, d = g["nc"], g["t"], g["d"]
    gcn, gat, edge = kind.startswith("gcn"), kind.startswith("gat"), kind == "edge"
    first, add, last_gat = kind == "gcn1", kind == "gcn3", kind == "gat2"
    wz = D + 1 if edge else D
    wo = wz if edge or gcn or last_gat else GW
    gw = 2 * D if first else GW if gat else wz
    K = D + 1 if gcn or edge else D
    groups = groups_of(wo)
    G_ = len(groups)
    ngot = 2 * C if first else C
    st = Stage(nc, f"a_{kind}", ["tick", "one", "os", "ix", "w", "wx", "bc", "ld0", "ld1", "g0", "g1", "st0", "st1", "lx0", "lx1", "zero", "sc0", "sc1"],
               ["s", "dg", "pz", "ct", "zt", "rl", "mm", "ev"], dict(pz=2 * C, mm=2 * G_))
    pool = dict(g0=8 * ngot * ECH, g1=8 * ngot * ECH) if gcn else dict(sc0=8 * C * ECH, sc1=8 * C * ECH) if edge else {}
    w = Work(st, pool=pool)
    base = dict(COUNTED)
    G = st.sb("G", [P, 2, C, gw])
    OWN = st.sb("OWN", [P, 2, C, gw]) if gcn else None
    DG = st.sb("DG", [P, 2, C, P]) if gcn else None
    MSG = st.sb("MSG", [P, 2, C, D]) if gat else None
    al = st.sb("al", [P, 2, C, HEADS])
    DR = st.sb("DR", [P, 2, C, P], I32)
    S = st.sb("S", [P, 2, C, P])
    XM = st.sb("XM", [P, 2, C, P])
    ZT = st.sb("ZT", [D + 1, 2, CR])
    RL = st.sb("RL", [D, 2, CR]) if gat else None
    W = st.sb("W", [D + 1, wo])
    bcol = st.sb("bcol", [D, 1])
    X0 = st.sb("X0", [P, 2, C, D])
    O = st.sb("O", [P, 2, C, D if edge else wo])
    rc = st.sb("rc", [P, C])
    mc = st.sb("mc", [P, 2, M_N, C])
    ic = st.sb("ic", [P, 2, 2, C], I32)
    ld, got, sto = [st["ld0"], st["ld1"]], [st["g0"], st["g1"]], [st["st0"], st["st1"]]
    sca, lx = [st["sc0"], st["sc1"]], [st["lx0"], st["lx1"]]
    ps, ident = g["ps"], g["ident"]
    table = {"gcn1": d["hx"], "gcn2": d["h1"], "gcn3": d["h2"]}.get(kind)
    to = {"gcn1": d["h1"], "gcn2": d["h2"], "gcn3": d["x1"], "gat0": d["gt2"], "gat1": d["gt2"], "gat2": d["zr"]}.get(kind)
    nld = 3 if gat else 1 if first else 2
    nst = 2 if first else 1
    by_vector = add or edge
    extra = weights(g, st, W, kind)

    def begin_sp(sp):
        extra["sync"](sp)
        if gat:
            sp.dma_start(bcol[:], t["gat_b"][int(kind[-1]), :].unsqueeze(1)).then_inc(st["bc"], 16)

    def load(sp, n, k, i):
        sp.wait_ge(st["s"], n + 1)
        sp.dma_start(DR[:, k], over(t["dst_lin"][bass.ds(n * CR, CR)].rearrange("(c p) -> c p", p=P).unsqueeze(0), [P, C, P]))\
            .then_inc(ld[k], 16)
        if gat:
            sp.dma_start(G[:, k], chunk_tiles(d["gr"], n)).then_inc(ld[k], 16)
            sp.dma_start(al[:, k], chunk_tiles(d["alpha"], n)).then_inc(ld[k], 16)
        elif edge:
            sp.wait_ge(st["pz"], C * n + C)
            sp.dma_start(G[:, k], chunk_tiles(d["msg3"], n)).then_inc(ld[k], 16)
        elif not first:
            sp.wait_ge(st["pz"], C * n + C)
            sp.dma_start(OWN[:, k], chunk_tiles(table[0:EP, :], n)).then_inc(ld[k], 16)

    def load_x0(sp, n, k, i):
        sp.wait_ge(st["ev"], G_ * n + 2 - G_)
        sp.dma_start(X0[:, k], chunk_tiles(d["base" if edge else "x0d"], n)).then_inc(lx[k], 16)

    def fetch(po, n, k, i):
        po.wait_ge(st["pz"], C * n + C)
        if first:
            po.wait_ge(sto[k], 16 * nst * i)
        po.tensor_copy(ic[:, k, 0, :], g["IDX"][:, I_SRC if first else I_SRCROW, bass.ds(n * C, C)])
        po.tensor_copy(ic[:, k, 1, :], g["IDX"][:, I_DST, bass.ds(n * C, C)]).then_inc(st["ix"], 1)
        po.wait_ge(st["ix"], n + 1)
        po.sem_inc(st["tick"], 1)
        for c in range(C):
            po.indirect_dma_start(out=G[:, k, c, :], out_offset=None, in_=table,
                                  in_offset=bass.IndirectOffsetOnAxis(ap=ic[:, k, 0, c:c + 1], axis=0),
                                  bounds_check=table.shape[0] - 1, oob_is_err=False).then_inc(got[k], 16)
            if first:
                po.indirect_dma_start(out=OWN[:, k, c, :], out_offset=None, in_=table,
                                      in_offset=bass.IndirectOffsetOnAxis(ap=ic[:, k, 1, c:c + 1], axis=0),
                                      bounds_check=NP - 1, oob_is_err=False).then_inc(got[k], 16)

    def begin_v(v):
        v.memset(ZT[:], 1.0)
        v.drain()
        if edge or last_gat:
            v.tensor_copy(W[0:wo, :], ident[0:wo, 0:wo]).then_inc(st["zero"], 1)
        else:
            v.memset(rc[:], 0.0).then_inc(st["zero"], 1)
        extra["vector"](v)

    def build_s(v, n, k, i):
        v.wait_ge(ld[k], 16 * nld * (i + 1))
        v.wait_ge(st["pz"], C * n + C)
        v.wait_ge(st["zt"], n + 1)
        v.wait_ge(st["dg"], n + 1) if gcn else None
        v.tensor_copy(mc[:, k], g["META"][:, :, bass.ds(n * C, C)])
        v.drain()
        if gat:
            v.tensor_tensor(MSG[:, k].rearrange("p c (h e) -> p c h e", h=HEADS),
                            G[:, k, :, 0:D].rearrange("p c (h e) -> p c h e", h=HEADS),
                            over(al[:, k].unsqueeze(3), [P, C, HEADS, HC]), ALU.mult)
        v.tensor_tensor(XM[:, k], DR[:, k], over(mc[:, k, M_PREV, :].unsqueeze(2), [P, C, P]), ALU.is_equal)
        for c in range(C):
            if gcn:
                last = v.tensor_scalar(S[:, k, c, :], DR[:, k, c, :], mc[:, k, M_DST, c:c + 1],
                                       mc[:, k, M_NORM, c:c + 1], ALU.is_equal, ALU.mult)
            else:
                last = v.tensor_scalar(S[:, k, c, :], DR[:, k, c, :], mc[:, k, M_DST, c:c + 1], None, ALU.is_equal)
        last.then_inc(st["s"], 1)

    def build_dg(act, n, k, i):
        act.wait_ge(st["s"], n + 3)
        act.wait_ge(st["pz"], C * n + C)
        for c in range(C):
            last = act.activation(DG[:, k, c, :], ident[:], ACT.Copy, scale=mc[:, k, M_SELF, c:c + 1])
        last.then_inc(st["dg"], 1)

    def sums(pe, n, k, i):
        pe.wait_ge(st["s"], n + 3)
        if gcn:
            pe.wait_ge(st["dg"], n + 3)
            pe.wait_ge(got[k], base[f"g{k}"] + 16 * ngot * (i + 1))
        pe.wait_ge(ld[k], 16 * nld * (i + 1))
        for c in range(C):
            z = ps[0:wz, ((k * C + c) % 2) * 512:((k * C + c) % 2) * 512 + P]
            pe.wait_ge(st["ct"], C * n + c + 1)
            rows_ = MSG[:, k, c, :] if gat else G[:, k, c, 0:wz]
            last = nc.tensor.matmul(z, rows_, S[:, k, c, :], start=True, stop=not gcn)
            if gcn:
                last = nc.tensor.matmul(z, OWN[:, k, c, 0:D], DG[:, k, c, :], start=False, stop=True)
            last.then_inc(st["pz"], 1)

    def carry(v, n, k, i):
        v.wait_ge(st["mm"], G_ * n + G_)
        for c in range(C):
            before = ZT[0:wz, k, c * P - 1:c * P] if c else ZT[0:wz, 1 - k, CR - 1:CR]
            z = ps[0:wz, ((k * C + c) % 2) * 512:((k * C + c) % 2) * 512 + P]
            v.wait_ge(st["pz"], C * n + c + 1 + 2 * C)
            v.wait_ge(st["ct"], C * n + c + 2)
            v.scalar_tensor_tensor(out=ZT[0:wz, k, c * P:(c + 1) * P], in0=XM[0:wz, k, c, :], scalar=before, in1=z,
                                   op0=ALU.mult, op1=ALU.add).then_inc(st["ct"], 1)
        v.wait_ge(st["ct"], C * n + C + 2)
        v.sem_inc(st["zt"], 1)

    def activate(act, n, k, i):
        act.wait_ge(st["zt"], n + 3)
        act.wait_ge(st["mm"], G_ * n + G_)
        act.activation(RL[:, k, :], ZT[0:D, k, :], ACT.Relu, bias=bcol[:]).then_inc(st["rl"], 1)

    def multiply(pe, n, k, i):
        if gat:
            pe.wait_ge(st["rl"], n + 3)
        else:
            pe.wait_ge(st["zt"], n + 3)
        for q, tiles in enumerate(groups):
            pe.wait_ge(st["ev"], G_ * n + q + 1)
            bank = 1024 + 512 * ((G_ * k + q) % 2)
            for m, c in enumerate(tiles):
                lhs = (RL if gat else ZT)[0:K, k, c * P:(c + 1) * P]
                last = nc.tensor.matmul(ps[:, bank + m * wo:bank + (m + 1) * wo], lhs, W[0:K, :], start=True, stop=True)
            last.then_inc(st["mm"], 1)

    def from_psum(eng, n, k, i):
        if edge:
            eng.wait_ge(sca[k], base[f"sc{k}"] + 16 * C * i)
        else:
            eng.wait_ge(sto[k], 16 * nst * i)
        if by_vector:
            eng.wait_ge(lx[k], 16 * (i + 1))
        for q, tiles in enumerate(groups):
            eng.wait_ge(st["mm"], G_ * n + q + 1 + 2 * G_)
            bank = 1024 + 512 * ((G_ * k + q) % 2)
            z = ps[:, bank:bank + len(tiles) * wo].rearrange("p (c w) -> p c w", w=wo)
            cs = slice(tiles[0], tiles[-1] + 1)
            if add:
                eng.tensor_tensor(O[:, k, cs, :], z, X0[:, k, cs, :], ALU.add).then_inc(st["ev"], 1)
            elif edge:
                eng.tensor_scalar(rc[:, cs], z[:, :, D], 1.0, None, ALU.max)
                eng.drain()
                eng.reciprocal(rc[:, cs], rc[:, cs])
                eng.drain()
                eng.tensor_tensor(O[:, k, cs, :], z[:, :, 0:D], over(rc[:, cs].unsqueeze(2), [P, len(tiles), D]), ALU.mult)
                eng.drain()
                eng.tensor_tensor(O[:, k, cs, :], O[:, k, cs, :], X0[:, k, cs, :], ALU.add).then_inc(st["ev"], 1)
            else:
                eng.activation(O[:, k, cs, :], z, ACT.Relu if gcn else ACT.Copy).then_inc(st["ev"], 1)

    def store(act, n, k, i):
        act.wait_ge(st["ev"], G_ * n + G_ + 2)
        act.dma_start(chunk_tiles(to[0:EP, :], n), O[:, k]).then_inc(sto[k], 16)
        if first:
            act.dma_start(chunk_tiles(d["x0d"], n), OWN[:, k, :, D:2 * D]).then_inc(sto[k], 16)

    def end(act):
        for k in (0, 1):
            act.wait_ge(sto[k], 16 * nst * (ECH // 2))

    def scatter(po, n, k, i):
        po.wait_ge(sca[k], base[f"sc{k}"] + 16 * C * i)
        po.tensor_copy(ic[:, k, 0, :], g["IDX"][:, I_OUT, bass.ds(n * C, C)]).then_inc(st["ix"], 1)
        po.wait_ge(st["ix"], n + 1)
        po.wait_ge(st["ev"], G_ * n + G_ + 2)
        po.sem_inc(st["tick"], 1)
        for c in range(C):
            po.indirect_dma_start(out=g["out"], in_=O[:, k, c, :], in_offset=None,
                                  out_offset=bass.IndirectOffsetOnAxis(ap=ic[:, k, 0, c:c + 1], axis=0),
                                  bounds_check=NP - 1, oob_is_err=False).then_inc(sca[k], 16)

    def end_scatter(po):
        for k in (0, 1):
            po.wait_ge(sca[k], base[f"sc{k}"] + 16 * C * (ECH // 2))

    def begin_pe(pe):
        pe.wait_ge(st["zero"], 1)
        extra["tensor"](pe)

    def begin_act(act):
        if gat:
            act.wait_ge(st["bc"], 16)
        if kind == "gat0" or kind == "gat1":
            act.wait_ge(st["zero"], 1)
            act.activation(RL[:, 0, 0:P], ZT[0:D, 0, 0:P], ACT.Relu, bias=bcol[:], scale=0.0).then_inc(st["one"], 1)
            act.wait_ge(st["one"], 2)
            act.activation(O[:, 0, 0, :], ps[:, 1024:1024 + wo], ACT.Copy).then_inc(st["one"], 1)
            act.wait_ge(st["one"], 3)
            act.dma_start(d["gt2"][EP:EP + P, :], O[:, 0, 0, :]).then_inc(st["os"], 16)
            act.wait_ge(st["os"], 16)

    def begin_pe2(pe):
        begin_pe(pe)
        if kind == "gat0" or kind == "gat1":
            pe.wait_ge(st["one"], 1)
            nc.tensor.matmul(ps[:, 1024:1024 + wo], RL[0:D, 0, 0:P], W[0:D, :], start=True, stop=True).then_inc(st["one"], 1)
            pe.wait_ge(st["one"], 3)

    w.on("sync", (load, 0), *([(load_x0, 1)] if by_vector else []), before=begin_sp)
    w.on("vector", (build_s, 0), (carry, 1), *([(from_psum, 2)] if by_vector else []), before=begin_v)
    act = [(build_dg, 0)] if gcn else []
    act += [(activate, 1)] if gat else []
    act += [] if by_vector else [(from_psum, 2)]
    act += [] if edge else [(store, 2)]
    if act:
        w.on("scalar", *act, before=begin_act, after=None if edge else end)
    w.on("tensor", (sums, 1), (multiply, 2), before=begin_pe2)
    if gcn:
        w.on("gpsimd", (fetch, 0))
    if edge:
        w.on("gpsimd", (scatter, 2), after=end_scatter)
    return w


def gat_gather(g, layer):
    nc, d = g["nc"], g["d"]
    st = Stage(nc, f"gg{layer}", ["tick", "ix", "g0", "g1", "st0", "st1"], [])
    w = Work(st, pool=dict(g0=8 * C * ECH, g1=8 * C * ECH))
    G = st.sb("G", [P, 2, C, GW])
    ic = st.sb("ic", [P, 2, C], I32)
    got, sto = [st["g0"], st["g1"]], [st["st0"], st["st1"]]
    base = dict(COUNTED)
    table, column = (d["gt2"], I_SRCROW2) if layer else (d["gt"], I_SRCROW)

    def fetch(po, n, k, i):
        po.wait_ge(sto[k], 32 * i)
        po.tensor_copy(ic[:, k, :], g["IDX"][:, column, bass.ds(n * C, C)]).then_inc(st["ix"], 1)
        po.wait_ge(st["ix"], n + 1)
        po.sem_inc(st["tick"], 1)
        for c in range(C):
            po.indirect_dma_start(out=G[:, k, c, :], out_offset=None, in_=table,
                                  in_offset=bass.IndirectOffsetOnAxis(ap=ic[:, k, c:c + 1], axis=0),
                                  bounds_check=table.shape[0] - 1, oob_is_err=False).then_inc(got[k], 16)

    def store(sp, n, k, i):
        sp.wait_ge(got[k], base[f"g{k}"] + 16 * C * (i + 1))
        sp.dma_start(chunk_tiles(d["gr"], n), G[:, k]).then_inc(sto[k], 16)
        sp.dma_start(chunk_tiles(d["asrc"], n), G[:, k, :, D:D + HEADS]).then_inc(sto[k], 16)

    def end(sp):
        for k in (0, 1):
            sp.wait_ge(sto[k], 32 * (ECH // 2))

    w.on("gpsimd", (fetch, 0))
    w.on("sync", (store, 0), after=end)
    return w


def gat_softmax(nc, layer, t, d, g):
    st = Stage(nc, f"gs{layer}", ["tick", "ld", "to_pe", "from_pe", "e", "st"], [])
    AS, AD, B, T, M = (st.sb(x, [P, J, HEADS]) for x in ("AS", "AD", "B", "T", "M"))
    sc = Scans(nc, st, g, HEADS)
    with nc.Block() as block:
        @block.sync
        def _(sp):
            sp.dma_start(AS[:], d["asrc"].rearrange("(q j) h -> q j h", j=J)).then_inc(st["ld"], 16)
            sp.dma_start(AD[:], (d["gt2"] if layer else d["gt"])[0:EP, D + HEADS:GW].rearrange("(q j) h -> q j h", j=J)).then_inc(st["ld"], 16)
            sp.wait_ge(st["e"], 3)
            sp.dma_start(d["alpha"].rearrange("(q j) h -> q j h", j=J), AS[:]).then_inc(st["st"], 16)
            sp.wait_ge(st["st"], 16)

        @block.tensor
        def _(pe):
            pe_part(nc, st, g, sc, [True, False, True, False, True], pe)

        @block.scalar
        def _(act):
            act.wait_ge(st["e"], 1)
            act.activation(AS[:], AS[:], ACT.Exp).then_inc(st["e"], 1)

        @block.vector
        def _(v):
            sc.begin(v)
            v.wait_ge(st["ld"], 32)
            sc.spread(v, B, AD, T)
            v.tensor_tensor(AS[:], AS[:], B[:], ALU.add)
            v.drain()
            v.scalar_tensor_tensor(out=AS[:], in0=AS[:], scalar=0.2, in1=AS[:], op0=ALU.mult, op1=ALU.max)
            v.drain()
            sc.maximum(v, M, AS)
            sc.spread(v, B, M, T)
            v.tensor_tensor(AS[:], AS[:], B[:], ALU.subtract).then_inc(st["e"], 1)
            v.wait_ge(st["e"], 2)
            sc.total(v, M, AS)
            sc.spread(v, B, M, T)
            v.tensor_scalar(B[:], B[:], 1.0e-16, None, ALU.add)
            v.drain()
            v.reciprocal(M[:], B[:])
            v.drain()
            v.tensor_tensor(AS[:], AS[:], M[:], ALU.mult).then_inc(st["e"], 1)
    st.close()


def patch_last_rows(nc, t, d, g):
    st = Stage(nc, "patch", ["tick", "ld", "c", "g0", "st"], [])
    half = ET // 2
    tf = st.sb("tf", [half, 2, P])
    tii = st.sb("tii", [half, 2], I32)
    R = st.sb("R", [half, 2, 3 * D])
    ykv_tiles = d["ykv"].rearrange("(k p) w -> k p w", p=P)
    with nc.Block() as block:
        @block.sync
        def _(sp):
            sp.dma_start(tf[:], d["lin"][5, :].rearrange("(a k p) -> k a p", a=2, p=P)).then_inc(st["ld"], 16)
            sp.wait_ge(st["g0"], COUNTED["g0"] + 32)
            for a in (0, 1):
                sp.dma_start(ykv_tiles[a * half:(a + 1) * half, P - 1, :], R[:, a, :]).then_inc(st["st"], 16)
            sp.wait_ge(st["st"], 32)

        @block.vector
        def _(v):
            v.wait_ge(st["ld"], 16)
            v.tensor_copy(tii[:], tf[:, :, P - 1]).then_inc(st["c"], 1)

        @block.gpsimd
        def _(po):
            po.wait_ge(st["c"], 1)
            for a in (0, 1):
                po.indirect_dma_start(out=R[:, a, :], out_offset=None, in_=d["ykv"],
                                      in_offset=bass.IndirectOffsetOnAxis(ap=tii[:, a:a + 1], axis=0),
                                      bounds_check=EP - 1, oob_is_err=False).then_inc(st["g0"], 16)
    st.close(g0=32)


def attention(g):
    nc, t, d = g["nc"], g["t"], g["d"]
    st = Stage(nc, "att", ["tick", "ix", "ld0", "ld1", "g0", "g1", "st0", "st1", "sy0", "sy1"],
               ["s", "kv", "ev", "sc", "ex", "ms"], dict(kv=2 * C, ev=C))
    w = Work(st, pool=dict(g0=8 * C * ECH, g1=8 * C * ECH))
    base = dict(COUNTED)
    G = st.sb("G", [P, 2, C, 2 * D])
    K = st.sb("K", [P, 2, C, 3 * D])
    KD = st.sb("KD", [P, 2, C, 3 * D])
    DR = st.sb("DR", [P, 2, CR], I32)
    S = st.sb("S", [P, 2, C, P])
    PR = st.sb("PR", [P, C, D])
    ss = st.sb("ss", [P, 2, C, HEADS])
    MS = st.sb("MS", [P, 2, C, D + HEADS])
    mc = st.sb("mc", [P, 2, M_N, C])
    ic = st.sb("ic", [P, 2, C], I32)
    ld, got, sto = [st["ld0"], st["ld1"]], [st["g0"], st["g1"]], [st["st0"], st["st1"]]
    sy = [st["sy0"], st["sy1"]]
    ps = g["ps"]

    def load(sp, n, k, i):
        sp.wait_ge(st["kv"], C * n + C)
        sp.dma_start(DR[:, k], over(t["dst_lin"][bass.ds(n * CR, CR)].unsqueeze(0), [P, CR])).then_inc(ld[k], 16)
        sp.dma_start(K[:, k], chunk_tiles(d["ykv"], n)).then_inc(ld[k], 16)

    def store_ys(sp, n, k, i):
        sp.wait_ge(got[k], base[f"g{k}"] + 16 * C * (i + 1))
        sp.dma_start(chunk_tiles(d["ys"], n), G[:, k, :, D:2 * D]).then_inc(sy[k], 16)

    def end_ys(sp):
        for k in (0, 1):
            sp.wait_ge(sy[k], 16 * (ECH // 2))

    def fetch(po, n, k, i):
        po.wait_ge(sy[k], 16 * i)
        po.sem_inc(st["tick"], 1)
        po.wait_ge(st["sc"], n + 1)
        po.tensor_copy(ic[:, k, :], g["IDX"][:, I_SRCROW, bass.ds(n * C, C)]).then_inc(st["ix"], 1)
        po.wait_ge(st["ix"], n + 1)
        po.sem_inc(st["tick"], 1)
        for c in range(C):
            po.indirect_dma_start(out=G[:, k, c, :], out_offset=None, in_=d["qy"],
                                  in_offset=bass.IndirectOffsetOnAxis(ap=ic[:, k, c:c + 1], axis=0),
                                  bounds_check=ROWS - 1, oob_is_err=False).then_inc(got[k], 16)

    def spread(pe, n, k, i):
        pe.wait_ge(st["s"], n + 3)
        pe.wait_ge(ld[k], 32 * (i + 1))
        for c in range(C):
            pe.wait_ge(st["ev"], C * n + c + 1)
            nc.tensor.matmul(ps[:, c * 512:c * 512 + 3 * D], S[:, k, c, :], K[:, k, c, :],
                             start=True, stop=True).then_inc(st["kv"], 1)

    def exps(act, n, k, i):
        act.wait_ge(st["sc"], n + 3)
        act.activation(MS[:, k, :, D:D + HEADS], ss[:, k], ACT.Exp).then_inc(st["ex"], 1)

    def to_sbuf(act, n, k, i):
        act.wait_ge(st["ms"], n + 1)
        act.wait_ge(sto[k], 32 * i)
        for c in range(C):
            act.wait_ge(st["kv"], C * n + c + 1 + 2 * C)
            act.activation(KD[:, k, c, :], ps[:, c * 512:c * 512 + 3 * D], ACT.Copy).then_inc(st["ev"], 1)

    def store(act, n, k, i):
        act.wait_ge(st["ms"], n + 3)
        act.dma_start(chunk_tiles(d["msg"], n), MS[:, k]).then_inc(sto[k], 16)
        act.dma_start(chunk_tiles(d["yd"], n), KD[:, k, :, 0:D]).then_inc(sto[k], 16)

    def end(act):
        for k in (0, 1):
            act.wait_ge(sto[k], 32 * (ECH // 2))

    def scores(v, n, k, i):
        v.wait_ge(st["ev"], C * n + C + C)
        v.wait_ge(got[k], base[f"g{k}"] + 16 * C * (i + 1))
        v.wait_ge(sto[k], 32 * i)
        v.tensor_tensor(PR[:], G[:, k, :, 0:D], KD[:, k, :, D:2 * D], ALU.mult)
        v.drain()
        v.reduce_sum(ss[:, k], PR[:].rearrange("p c (h e) -> p c h e", h=HEADS), AX.X)
        v.drain()
        v.tensor_scalar(ss[:, k], ss[:, k], -10.0, 10.0, ALU.max, ALU.min).then_inc(st["sc"], 1)

    def build_s(v, n, k, i):
        v.wait_ge(ld[k], 32 * (i + 1))
        v.wait_ge(st["kv"], C * n + C)
        v.tensor_copy(mc[:, k], g["META"][:, :, bass.ds(n * C, C)])
        v.drain()
        for c in range(C):
            last = v.tensor_scalar(S[:, k, c, :], DR[:, k, c * P:(c + 1) * P], mc[:, k, M_DST, c:c + 1],
                                   mc[:, k, M_REP, c:c + 1], ALU.is_equal, ALU.mult)
        last.then_inc(st["s"], 1)

    def messages(v, n, k, i):
        v.wait_ge(st["ex"], n + 3)
        v.tensor_tensor(MS[:, k, :, 0:D].rearrange("p c (h e) -> p c h e", h=HEADS),
                        KD[:, k, :, 2 * D:3 * D].rearrange("p c (h e) -> p c h e", h=HEADS),
                        over(MS[:, k, :, D:D + HEADS].unsqueeze(3), [P, C, HEADS, HC]),
                        ALU.mult).then_inc(st["ms"], 1)

    w.on("sync", (load, 0), (store_ys, 1), after=end_ys)
    w.on("gpsimd", (fetch, 0))
    w.on("tensor", (spread, 0))
    w.on("vector", (scores, 1), (build_s, 0), (messages, 1))
    w.on("scalar", (exps, 1), (to_sbuf, 0), (store, 1), after=end)
    return w


def accumulate(nc, t, d, g):
    st = Stage(nc, "acc", ["tick", "ld0", "ld1", "k", "dump", "add0", "add1"], ["s", "mm", "ev"])
    MS = st.sb("MS", [P, 2, C, D + HEADS])
    SR = st.sb("SR", [P, 2, CR], I32)
    S = st.sb("S", [P, 2, C, CR])
    LOW = st.sb("LOW", [P, C, CR])
    junk = st.sb("junk", [P, CR])
    cnt = st.sb("cnt", [P, C])
    dump = st.sb("dump", [P, C])
    sc = st.sb("sc", [P, 2, C])
    SF = st.sb("SF", [P, ET])
    ic = st.sb("ic", [P, 2, C], I32)
    O = st.sb("O", [P, 2, C, D + HEADS])
    ld, add = [st["ld0"], st["ld1"]], [st["add0"], st["add1"]]
    ps = g["ps"]
    WM = D + HEADS

    def at(b):
        return (b // 4) * 512 + (b % 4) * P

    with nc.Block() as block:
        @block.sync
        def _(sp):
            sp.dma_start(dump[:], t["dump_row"]).then_inc(st["dump"], 16)
            with sp.Fori(0, ECH // 2) as i:
                for k in (0, 1):
                    n = 2 * i + k
                    sp.wait_ge(st["mm"], n + 1)
                    sp.dma_start(SR[:, k], over(t["src_lin"][bass.ds(n * CR, CR)].unsqueeze(0), [P, CR])).then_inc(ld[k], 16)
                    sp.dma_start(MS[:, k], chunk_tiles(d["msg"], n)).then_inc(ld[k], 16)

        @block.gpsimd
        def _(po):
            po.memset(LOW[:], 1.0)
            po.drain()
            po.affine_select(out=LOW[:], in_=LOW[:], compare_op=ALU.is_gt, fill=0.0, base=0,
                             pattern=[[P, C], [-1, CR]], channel_multiplier=1).then_inc(st["k"], 1)
            with po.Fori(0, ECH // 2) as i:
                for k in (0, 1):
                    n = 2 * i + k
                    po.wait_ge(st["ev"], n + 3)
                    po.sem_inc(st["tick"], 1)
                    for c in range(C):
                        po.indirect_dma_start(out=d["res"], in_=O[:, k, c, :], in_offset=None,
                                              out_offset=bass.IndirectOffsetOnAxis(ap=ic[:, k, c:c + 1], axis=0),
                                              bounds_check=NP + CR - 1, oob_is_err=True,
                                              compute_op=ALU.add).then_inc(add[k], 16)
                    po.wait_ge(add[k], COUNTED[f"add{k}"] + 16 * C * (i + 1))
            for k in (0, 1):
                po.wait_ge(add[k], COUNTED[f"add{k}"] + 16 * C * (ECH // 2))

        @block.tensor
        def _(pe):
            with pe.Fori(0, ECH // 2) as i:
                for k in (0, 1):
                    n = 2 * i + k
                    pe.wait_ge(st["s"], n + 3)
                    pe.wait_ge(ld[k], 32 * (i + 1))
                    pe.wait_ge(st["ev"], n + 2)
                    for b in range(C):
                        for a in range(C):
                            last = nc.tensor.matmul(ps[:, at(b):at(b) + WM], S[:, k, a, b * P:(b + 1) * P],
                                                    MS[:, k, a, :], start=(a == 0), stop=(a == C - 1))
                    last.then_inc(st["mm"], 1)

        @block.vector
        def _(v):
            v.wait_ge(st["k"], 1)
            v.wait_ge(st["dump"], 16)
            v.tensor_copy(SF[:], g["IDX"][:, I_SRC, :])
            v.drain()
            with v.Fori(0, ECH // 2) as i:
                for k in (0, 1):
                    n = 2 * i + k
                    v.wait_ge(ld[k], 32 * (i + 1))
                    v.wait_ge(st["mm"], n + 1)
                    v.tensor_copy(sc[:, k], SF[:, bass.ds(n * C, C)])
                    v.drain()
                    for c in range(C):
                        v.tensor_scalar(S[:, k, c, :], SR[:, k, :], sc[:, k, c:c + 1], None, ALU.is_equal)
                    v.drain()
                    for c in range(C):
                        v.scalar_tensor_tensor(out=junk[:], in0=S[:, k, c, :], scalar=1.0, in1=LOW[:, c, :],
                                               op0=ALU.mult, op1=ALU.mult, accum_out=cnt[:, c:c + 1])
                        v.drain()
                    v.tensor_scalar(cnt[:], cnt[:], 0.5, None, ALU.is_gt).then_inc(st["s"], 1)
                    v.drain()
                    v.tensor_tensor(junk[:, 0:C], dump[:], sc[:, k], ALU.subtract)
                    v.drain()
                    v.tensor_tensor(junk[:, 0:C], junk[:, 0:C], cnt[:], ALU.mult)
                    v.drain()
                    v.wait_ge(add[k], COUNTED[f"add{k}"] + 16 * C * i)
                    v.tensor_tensor(ic[:, k], junk[:, 0:C], sc[:, k], ALU.add)
                    v.wait_ge(st["mm"], n + 3)
                    v.tensor_copy(O[:, k, 0:4, :], ps[:, 0:512].rearrange("p (c w) -> p c w", w=P)[:, :, 0:WM])
                    v.drain()
                    v.tensor_copy(O[:, k, 4:C, :],
                                  ps[:, 512:512 + 3 * P].rearrange("p (c w) -> p c w", w=P)[:, :, 0:WM]).then_inc(st["ev"], 1)
    st.close(add0=8 * C * ECH, add1=8 * C * ECH)


def layer_norm(nc, v, st, X, H, SQ, small, n, av):
    tiles = X.shape[1]
    v.reduce_sum(small[:, 0, :], X, AX.X)
    v.drain()
    v.tensor_scalar(small[:, 0, :], small[:, 0, :], 1.0 / D, None, ALU.mult)
    v.drain()
    v.tensor_tensor(H, X, over(small[:, 0, :].unsqueeze(2), [P, tiles, D]), ALU.subtract)
    v.drain()
    v.tensor_tensor(SQ, H, H, ALU.mult)
    v.drain()
    v.reduce_sum(small[:, 1, :], SQ, AX.X).then_inc(st["var"], 1)
    v.wait_ge(av, n + 3)
    v.tensor_tensor(H, H, over(small[:, 2, :].unsqueeze(2), [P, tiles, D]), ALU.mult)
    v.drain()


def norm_scalar(act, st, g, small, n):
    act.wait_ge(st["var"], n + 3)
    act.activation(small[:, 1, :], small[:, 1, :], ACT.Ln, bias=g["eps_col"][:], scale=1.0 / D)
    act.drain()
    act.activation(small[:, 2, :], small[:, 1, :], ACT.Exp, scale=-0.5).then_inc(st["root"], 1)


def gates(nc, t, d, g):
    st = Stage(nc, "gate", ["tick", "ix", "w", "ld0", "ld1", "g0", "g1", "st0", "st1"],
               ["x", "var", "root", "h", "tr", "ht", "mm", "ab", "ms"])
    Y = st.sb("Y", [P, 2, 2 * C, D])
    RG = st.sb("RG", [P, 2, 2 * C, D + HEADS])
    EA = st.sb("EA", [DE, 2, CR])
    H = st.sb("H", [P, 2 * C, D])
    SQ = st.sb("SQ", [P, 2 * C, D])
    small = st.sb("small", [P, 3, 2 * C])
    rb = st.sb("rb", [P, 2 * C, HEADS])
    B = st.sb("B", [P, 2, C, D])
    HT = st.sb("HT", [D + 1, C, 2 * P])
    W = st.sb("W", [D + 1, 3, 2 * D])
    AB, TT, LG = (st.sb(x, [P, C, 2 * D]) for x in ("AB", "TT", "LG"))
    MS = st.sb("MS", [P, 2, C, D + 1])
    GE = st.sb("GE", [P, C, D])
    ic = st.sb("ic", [P, 2, 2, C], I32)
    ld, got, sto = [st["ld0"], st["ld1"]], [st["g0"], st["g1"]], [st["st0"], st["st1"]]
    ps, ident = g["ps"], g["ident"]
    z = ps[:, 2048:2048 + C * 256].rearrange("p (c w) -> p c w", w=256)[:, :, 0:2 * D]

    with nc.Block() as block:
        @block.sync
        def _(sp):
            for s, (w, b) in enumerate((("we", "be"), ("wn", "bn"))):
                cols = slice(s * D, (s + 1) * D)
                for part in range(2):
                    sp.dma_start(W[0:D, part, cols], t[w][part * D:(part + 1) * D, :]).then_inc(st["w"], 16)
                sp.dma_start(W[0:DE, 2, cols], t[w][2 * D:2 * D + DE, :]).then_inc(st["w"], 16)
                sp.dma_start(W[D:D + 1, 0, cols], t[b].unsqueeze(0)).then_inc(st["w"], 16)
            with sp.Fori(0, ECH // 2) as i:
                for k in (0, 1):
                    n = 2 * i + k
                    sp.wait_ge(st["mm"], n + 1)
                    sp.dma_start(Y[:, k, 0:C, :], chunk_tiles(d["ys"], n)).then_inc(ld[k], 16)
                    sp.dma_start(Y[:, k, C:2 * C, :], chunk_tiles(d["yd"], n)).then_inc(ld[k], 16)
                    sp.dma_start(EA[:, k, :], t["ea_t"][:, bass.ds(n * CR, CR)]).then_inc(ld[k], 16)

        @block.gpsimd
        def _(po):
            with po.Fori(0, ECH // 2) as i:
                for k in (0, 1):
                    n = 2 * i + k
                    po.wait_ge(st["h"], n + 1)
                    po.tensor_copy(ic[:, k, 0, :], g["IDX"][:, I_SRC, bass.ds(n * C, C)])
                    po.tensor_copy(ic[:, k, 1, :], g["IDX"][:, I_DST, bass.ds(n * C, C)]).then_inc(st["ix"], 1)
                    po.wait_ge(st["ix"], n + 1)
                    po.sem_inc(st["tick"], 1)
                    for s in (0, 1):
                        for c in range(C):
                            po.indirect_dma_start(out=RG[:, k, s * C + c, :], out_offset=None, in_=d["res"],
                                                  in_offset=bass.IndirectOffsetOnAxis(ap=ic[:, k, s, c:c + 1], axis=0),
                                                  bounds_check=NP - 1, oob_is_err=False).then_inc(got[k], 16)

        @block.vector
        def _(v):
            v.wait_ge(st["w"], 128)
            v.memset(HT[:], 1.0)
            v.memset(MS[:], 1.0)
            v.drain()
            with v.Fori(0, ECH // 2) as i:
                for k in (0, 1):
                    n = 2 * i + k
                    v.wait_ge(ld[k], 48 * (i + 1))
                    v.wait_ge(got[k], COUNTED[f"g{k}"] + 16 * 2 * C * (i + 1))
                    v.wait_ge(st["tr"], n + 2)
                    v.tensor_scalar(rb[:], RG[:, k, :, D:D + HEADS], 1.0e-8, None, ALU.add)
                    v.drain()
                    v.reciprocal(rb[:], rb[:])
                    v.drain()
                    v.tensor_tensor(H[:].rearrange("p c (h e) -> p c h e", h=HEADS),
                                    RG[:, k, :, 0:D].rearrange("p c (h e) -> p c h e", h=HEADS),
                                    over(rb[:].unsqueeze(3), [P, 2 * C, HEADS, HC]), ALU.mult)
                    v.drain()
                    v.tensor_tensor(Y[:, k], Y[:, k], H[:], ALU.add)
                    v.drain()
                    layer_norm(nc, v, st, Y[:, k], H[:], SQ[:], small[:], n, st["root"])
                    v.wait_ge(sto[k], 32 * i)
                    v.tensor_scalar(H[:], H[:], 0.0, None, ALU.max)
                    v.drain()
                    v.tensor_tensor(B[:, k], Y[:, k, C:2 * C, :], H[:, C:2 * C, :], ALU.add).then_inc(st["h"], 1)
                    v.wait_ge(st["tr"], n + 3)
                    v.wait_ge(st["mm"], n + 2)
                    v.tensor_copy(HT[0:D], ps[0:D, 0:C * 256].rearrange("p (c w) -> p c w", w=256)).then_inc(st["ht"], 1)
                    v.wait_ge(st["mm"], n + 3)
                    v.wait_ge(st["ab"], n + 3)
                    v.tensor_scalar(GE[:], z[:, :, 0:D], 0.0, None, ALU.is_ge)
                    v.drain()
                    v.tensor_tensor(GE[:], GE[:], TT[:, :, 0:D], ALU.max)
                    v.tensor_scalar(TT[:, :, D:2 * D], TT[:, :, 0:D], 1.0, None, ALU.add)
                    v.drain()
                    v.reciprocal(TT[:, :, 0:D], TT[:, :, D:2 * D])
                    v.scalar_tensor_tensor(out=LG[:, :, D:2 * D], in0=z[:, :, D:2 * D], scalar=0.0,
                                           in1=LG[:, :, D:2 * D], op0=ALU.max, op1=ALU.add)
                    v.drain()
                    v.tensor_tensor(GE[:], GE[:], TT[:, :, 0:D], ALU.mult)
                    v.drain()
                    v.tensor_tensor(MS[:, k, :, 0:D], GE[:], LG[:, :, D:2 * D], ALU.mult).then_inc(st["ms"], 1)

        @block.tensor
        def _(pe):
            pe.wait_ge(st["w"], 128)
            with pe.Fori(0, ECH // 2) as i:
                for k in (0, 1):
                    n = 2 * i + k
                    pe.wait_ge(st["h"], n + 3)
                    pe.wait_ge(st["ht"], n + 2)
                    for c in range(C):
                        for s in (0, 1):
                            last = nc.tensor.transpose(ps[0:D, c * 256 + s * P:c * 256 + (s + 1) * P],
                                                       H[:, s * C + c, :], ident[:])
                    last.then_inc(st["tr"], 1)
                    pe.wait_ge(st["ht"], n + 3)
                    pe.wait_ge(st["ms"], n + 2)
                    for c in range(C):
                        o = ps[:, 2048 + c * 256:2048 + c * 256 + 2 * D]
                        nc.tensor.matmul(o, HT[0:D + 1, c, 0:P], W[0:D + 1, 0, :], start=True, stop=False)
                        nc.tensor.matmul(o, HT[0:D, c, P:2 * P], W[0:D, 1, :], start=False, stop=False)
                        last = nc.tensor.matmul(o, EA[:, k, c * P:(c + 1) * P], W[0:DE, 2, :], start=False, stop=True)
                    last.then_inc(st["mm"], 1)

        @block.scalar
        def _(act):
            with act.Fori(0, ECH // 2) as i:
                for k in (0, 1):
                    n = 2 * i + k
                    norm_scalar(act, st, g, small[:], n)
                    act.wait_ge(st["mm"], n + 3)
                    act.wait_ge(st["ms"], n + 2)
                    act.activation(AB[:], z, ACT.Abs)
                    act.drain()
                    act.activation(TT[:], AB[:], ACT.Exp, scale=-1.0)
                    act.drain()
                    act.activation(LG[:], TT[:], ACT.Ln, bias=1.0).then_inc(st["ab"], 1)
                    act.wait_ge(st["ms"], n + 3)
                    act.dma_start(chunk_tiles(d["msg3"], n), MS[:, k]).then_inc(sto[k], 16)
                    act.dma_start(chunk_tiles(d["base"], n), B[:, k]).then_inc(sto[k], 16)
            for k in (0, 1):
                act.wait_ge(sto[k], 32 * (ECH // 2))
    st.close(g0=2 * 8 * C * ECH, g1=2 * 8 * C * ECH)


def kernel(**inputs):
    import numpy as np
    import concourse.bacc as bacc
    from concourse.bass_utils import run_bass_kernel_spmd

    a = {k: np.asarray(v) for k, v in inputs.items()}

    def padded(x, rows, value):
        x = np.ascontiguousarray(x)
        return np.concatenate([x, np.full((rows - x.shape[0], *x.shape[1:]), value, x.dtype)])

    src, dst = padded(a["src"], EP, N), padded(a["dst"], EP, N)
    ew = padded(a["edge_weight"], EP, 0)
    around = np.concatenate([np.full(1, -1, dst.dtype), dst, np.full(1, N + 1, dst.dtype)])
    arrays = {
        "x": padded(a["x"], NP, 0),
        "src_lin": src, "dst_lin": dst, "src_tiles": src.reshape(ET, P).T, "dst_tiles": dst.reshape(ET, P).T,
        "dst_runs": np.stack([around[i:i + EP].reshape(P, J) for i in range(3)], axis=1),
        "first": dst[::P], "prev_tiles": np.broadcast_to(around[0:EP:P], (P, ET)),
        "ew_runs": ew.reshape(P, J), "ew_tiles": ew.reshape(ET, P).T,
        "edge_no": np.arange(EP, dtype=np.float32).reshape(P, J),
        "dump_row": (NP + np.arange(CR, dtype=np.float32)).reshape(C, P).T,
        "ea_t": padded(a["edge_attr_64"], EP, 0).T,
        "gat_w": a["L1_gnn_W"], "gat_src": a["L1_gnn_att_src"], "gat_dst": a["L1_gnn_att_dst"],
        "gat_b": a["L1_gnn_bias"], "q_w": a["L2_gnn_qW"], "k_w": a["L2_gnn_kW"], "v_w": a["L2_gnn_vW"],
        "we": a["L3_gnn_W_e"], "be": a["L3_gnn_b_e"], "wn": a["L3_gnn_W_n"], "bn": a["L3_gnn_b_n"],
    }
    for i in (1, 2, 3):
        arrays[f"gcn_w{i}"], arrays[f"gcn_b{i}"] = a[f"L0_gnn_W{i}"], a[f"L0_gnn_b{i}"]
    arrays = {k: np.ascontiguousarray(v) for k, v in arrays.items()}

    nc = bacc.Bacc("TRN2", target_bir_lowering=False, num_devices=1)
    t = {k: nc.dram_tensor(f"in_{k}", v.shape, mybir.dt.from_np(v.dtype), kind="ExternalInput").ap()
         for k, v in arrays.items()}
    out = nc.dram_tensor("out_0", (NP, D), F32, kind="ExternalOutput").ap()
    build(nc, t, out)
    r = run_bass_kernel_spmd(nc, [{f"in_{k}": v for k, v in arrays.items()}], core_ids=[0])
    return r.results[0]["out_0"][0:N]
```

```python
import concourse.bass as bass
from concourse import mybir
from contextlib import ExitStack

ALU = mybir.AluOpType
ACT = mybir.ActivationFunctionType
AX = mybir.AxisListType
F32 = mybir.dt.float32
I32 = mybir.dt.int32

P = 128
N, D, E, DE = 50000, 96, 25000, 64
HE = DE // 2
HEADS = 4
HC = D // HEADS
C = 7
CR = C * P
ET = 28 * C
EP = ET * P
ECH = ET // C
NCH = 56
NP = NCH * CR
ROWS = EP + NP
J = EP // P
GW = D + 2 * HEADS
BIG = 1.0e30
SKIP = 65536.0
EPS = 1.0e-5
M_DST, M_PREV, M_NORM, M_SELF, M_REP, M_N = 0, 1, 2, 3, 4, 5
I_SRCROW, I_SRCROW2, I_SRC, I_DST, I_OUT, I_ADD, I_N = 0, 1, 2, 3, 4, 5, 6


POOL_DMA = {}
COUNTED = {}


class Stage:

    def __init__(self, nc, name, plain, credited, credit_of=None):
        self.nc, self.stack = nc, ExitStack()
        self.name = name
        self.s = {n: POOL_DMA[n] if n in POOL_DMA else self.stack.enter_context(nc.semaphore(f"{name}_{n}"))
                  for n in [*plain, *credited]}
        with nc.Block() as block:
            @block.sync
            def _(sp):
                for n in self.s:
                    if n not in POOL_DMA:
                        sp.sem_clear(self.s[n])
        with nc.Block() as block:
            @block.sync
            def _(sp):
                for n in credited:
                    sp.sem_inc(self.s[n], (credit_of or {}).get(n, 2))
                sp.drain()

    def __getitem__(self, n):
        return self.s[n]

    def sb(self, name, shape, dt=F32):
        return self.stack.enter_context(self.nc.sbuf_tensor(f"{self.name}_{name}", shape, dt))

    def close(self, **pool):
        for n, added in pool.items():
            COUNTED[n] += added
        self.stack.close()


def chunk_rows(table, n, base=0):
    return table[bass.ds(n * CR + base, CR), :].rearrange("(p c) d -> p c d", c=C)


def chunk_tiles(table, n):
    return table[bass.ds(n * CR, CR), :].rearrange("(c p) d -> p c d", p=P)


def over(ap, shape):
    return ap.to_broadcast(shape)


def build(nc, t, out):
    top = ExitStack()
    with top:
        def dram(name, shape, dt=F32):
            return nc.dram_tensor(name, shape, dt).ap()

        def sb(name, shape, dt=F32):
            return top.enter_context(nc.sbuf_tensor(name, shape, dt))

        for n in ("g0", "g1", "sc0", "sc1", "add0", "add1"):
            POOL_DMA[n] = top.enter_context(nc.semaphore(n))
            COUNTED[n] = 0
        ident = sb("ident", [P, P])
        eps_col = sb("eps_col", [P, 1])
        last_row = sb("last_row", [P, 1])
        META = sb("META", [P, M_N, ET])
        IDX = sb("IDX", [P, I_N, ET], I32)
        FL = {n: sb(f"fl_{n}", [P, J]) for n in ("same_prev", "same_next", "tail", "first", "last",
                                                "pen_prev", "pen_first")}
        RT = {n: sb(f"rt_{n}", [HEADS, P]) for n in ("whole_prev", "whole_next", "pen_whole")}
        ps = top.enter_context(nc.psum_tensor("ps", [P, 4096], F32))

        d = dict(
            lin=dram("lin", (6, EP)), search=dram("search", (ET, 3 * P)),
            hx=dram("hx", (NP, 2 * D)), x0d=dram("x0d", (EP, D)),
            h1=dram("h1", (ROWS, D)), h2=dram("h2", (ROWS, D)),
            x1=dram("x1", (ROWS, D)), gt=dram("gt", (ROWS, GW)), gt2=dram("gt2", (EP + P, GW)),
            asrc=dram("asrc", (EP, HEADS)), alpha=dram("alpha", (EP, HEADS)),
            zr=dram("zr", (EP, D)), q=dram("q", (ROWS, D)),
            kv=dram("kv", (EP, 2 * D)), yn=dram("yn", (NP, D)), hy=dram("hy", (NP, 2 * D)),
            msg=dram("msg", (EP, D + HEADS)), res=dram("res", (NP + CR, D + HEADS)),
            msg3=dram("msg3", (EP, D + 1)), base=dram("base", (EP, D)),
        )
        g = dict(nc=nc, t=t, d=d, out=out, ident=ident, last_row=last_row, eps_col=eps_col,
                 META=META, IDX=IDX, FL=FL, RT=RT, ps=ps)
        prepare(nc, t, d, g)
        run(g, find_sources(g), rows(g, "h1"))
        run(g, aggregate(g, "gcn1"), rows(g, "h2"))
        run(g, aggregate(g, "gcn2"), rows(g, "x1"))
        run(g, aggregate(g, "gcn3"), rows(g, "gt"))
        run(g, rows(g, "gt_edges"), chunks=ECH // 2)
        with nc.sbuf_tensor("GR", [P, ET, GW], F32) as GR:
            g["GR"] = GR
            for layer in range(3):
                if layer == 0:
                    run(g, gat_gather(g, layer), rows(g, "qy"))
                elif layer == 1:
                    run(g, gat_gather(g, layer), first_of_source(g))
                else:
                    run(g, gat_gather(g, layer))
                gat_softmax(nc, layer, t, d, g)
                run(g, aggregate(g, f"gat{layer}"))
        run(g, rows(g, "qkv_edges"), chunks=ECH // 2)
        patch_last_rows(nc, t, d, g)
        run(g, attention(g))
        run(g, accumulate(g))
        run(g, rows(g, "out"))
        run(g, gates(g))
        run(g, aggregate(g, "edge"))


class Work:

    def __init__(self, st, per=1, pool=None, deep=False):
        self.st, self.per, self.pool, self.deep = st, per, pool or {}, deep
        self.before, self.steps, self.after = {}, {}, {}

    def on(self, engine, *steps, before=None, after=None):
        self.steps[engine] = steps
        self.before[engine], self.after[engine] = before, after


def run(g, *works, chunks=ECH):
    nc = g["nc"]
    pairs = chunks // 2

    def program(engine, eng):
        mine = [w for w in works if engine in w.steps]
        if not mine:
            return
        lags = max([lag for w in mine for _, lag in w.steps[engine]], default=0)

        def turns(i, edge=True):
            for k in (0, 1):
                for w in mine:
                    for j in range(w.per):
                        slot = w.per * k + j
                        for step, lag in w.steps[engine]:
                            back = slot - lag
                            n = 2 * w.per * i + back
                            if edge and not 0 <= n < chunks * w.per:
                                continue
                            if w.deep:
                                step(eng, n, back % 2, w.per * i + back // 2, back % (2 * w.per), i + back // (2 * w.per))
                            else:
                                step(eng, n, back % 2, w.per * i + back // 2)

        for w in mine:
            if w.before[engine]:
                w.before[engine](eng)
        outside = -(-lags // 2)
        for i in range(outside):
            turns(i)
        if any(w.steps[engine] for w in mine):
            with eng.Fori(outside, pairs) as i:
                turns(i, False)
        for i in range(outside):
            turns(pairs + i)
        for w in mine:
            if w.after[engine]:
                w.after[engine](eng)

    with nc.Block() as block:
        @block.sync
        def _(sp):
            program("sync", sp)

        @block.gpsimd
        def _(po):
            program("gpsimd", po)

        @block.vector
        def _(v):
            program("vector", v)

        @block.tensor
        def _(pe):
            program("tensor", pe)

        @block.scalar
        def _(act):
            program("scalar", act)
    for w in reversed(works):
        w.st.close(**w.pool)


class Scans:

    def __init__(self, nc, st, g, heads):
        self.nc, self.st, self.g, self.heads, self.n = nc, st, g, heads, 0
        self.edge = st.sb("edge", [P, HEADS])
        self.edge_t = st.sb("edge_t", [HEADS, P])
        self.carry_t = st.sb("carry_t", [HEADS, P + 1])
        self.carry = st.sb("carry", [P, HEADS])

    def begin(self, v):
        v.memset(self.edge[:], 0.0)
        v.drain()

    def cross(self, v, y, col, flags, op0, op1, first, back):
        nc, g, st, H = self.nc, self.g, self.st, self.heads
        v.drain()
        v.tensor_copy(self.edge[:, 0:H], y[:, col, :]).then_inc(st["to_pe"], 1)
        v.wait_ge(st["from_pe"], 2 * self.n + 1)
        v.tensor_copy(self.edge_t[:], g["ps"][0:HEADS, 0:P])
        v.memset(self.carry_t[:], first)
        v.drain()
        if back:
            v.tensor_tensor_scan(self.carry_t[:, 0:P][:, ::-1], g["RT"][flags][:, ::-1],
                                 self.edge_t[:, ::-1], first, op0, op1).then_inc(st["to_pe"], 1)
        else:
            v.tensor_tensor_scan(self.carry_t[:, 1:P + 1], g["RT"][flags][:],
                                 self.edge_t[:], first, op0, op1).then_inc(st["to_pe"], 1)
        v.wait_ge(st["from_pe"], 2 * self.n + 2)
        v.tensor_copy(self.carry[:], g["ps"][:, 512:512 + HEADS])
        v.drain()
        self.n += 1

    def total(self, v, y, x):
        F = self.g["FL"]
        for h in range(self.heads):
            v.tensor_tensor_scan(y[:, :, h], F["same_prev"][:], x[:, :, h], 0.0, ALU.mult, ALU.add)
        self.cross(v, y, J - 1, "whole_prev", ALU.mult, ALU.add, 0.0, False)
        for h in range(self.heads):
            v.scalar_tensor_tensor(out=y[:, :, h], in0=F["first"][:], scalar=self.carry[:, h:h + 1],
                                   in1=y[:, :, h], op0=ALU.mult, op1=ALU.add)
        v.drain()

    def maximum(self, v, y, x):
        F = self.g["FL"]
        for h in range(self.heads):
            v.tensor_tensor_scan(y[:, :, h], F["pen_prev"][:], x[:, :, h], -BIG, ALU.add, ALU.max)
        self.cross(v, y, J - 1, "pen_whole", ALU.add, ALU.max, -BIG, False)
        for h in range(self.heads):
            v.scalar_tensor_tensor(out=y[:, :, h], in0=F["pen_first"][:], scalar=self.carry[:, h:h + 1],
                                   in1=y[:, :, h], op0=ALU.add, op1=ALU.max)
        v.drain()

    def spread(self, v, y, x, tmp):
        F = self.g["FL"]
        for h in range(self.heads):
            v.tensor_tensor(tmp[:, :, h], x[:, :, h], F["tail"][:], ALU.mult)
        v.drain()
        for h in range(self.heads):
            v.tensor_tensor_scan(y[:, ::-1, h], F["same_next"][:, ::-1], tmp[:, ::-1, h], 0.0, ALU.mult, ALU.add)
        self.cross(v, y, 0, "whole_next", ALU.mult, ALU.add, 0.0, True)
        for h in range(self.heads):
            v.scalar_tensor_tensor(out=y[:, :, h], in0=F["last"][:], scalar=self.carry[:, h:h + 1],
                                   in1=y[:, :, h], op0=ALU.mult, op1=ALU.add)
        v.drain()


def pe_part(nc, st, g, sc, backs, pe):
    for n, back in enumerate(backs):
        pe.wait_ge(st["to_pe"], 2 * n + 1)
        nc.tensor.transpose(g["ps"][0:HEADS, 0:P], sc.edge[:], g["ident"][:]).then_inc(st["from_pe"], 1)
        pe.wait_ge(st["to_pe"], 2 * n + 2)
        c = sc.carry_t[:, 1:P + 1] if back else sc.carry_t[:, 0:P]
        nc.tensor.transpose(g["ps"][:, 512:512 + HEADS], c, g["ident"][0:HEADS, 0:HEADS]).then_inc(st["from_pe"], 1)


def prepare(nc, t, d, g):
    st = Stage(nc, "prep", ["tick", "ld", "k", "to_pe", "from_pe", "rt", "sq", "out"], [])
    raw = st.sb("raw", [P, 3, J], I32)
    ew = st.sb("ew", [P, J])
    eno = st.sb("eno", [P, J])
    dp, dc, dn = (st.sb(x, [P, J]) for x in ("dp", "dc", "dn"))
    X, Y, Z, T = (st.sb(x, [P, J, 1]) for x in ("X", "Y", "Z", "T"))
    whole = st.sb("whole", [P, 3, HEADS])
    L = st.sb("L", [P, 6, J])
    ti = st.sb("ti", [P, 2, ET], I32)
    zero = st.sb("zero", [P, C * (D + HEADS)])
    sc = Scans(nc, st, g, 1)
    F, RT, ps, ident = g["FL"], g["RT"], g["ps"], g["ident"]

    with nc.Block() as block:
        @block.sync
        def _(sp):
            sp.dma_start(raw[:], t["dst_runs"]).then_inc(st["ld"], 16)
            sp.dma_start(ew[:], t["ew_runs"]).then_inc(st["ld"], 16)
            sp.dma_start(eno[:], t["edge_no"]).then_inc(st["ld"], 16)
            sp.dma_start(ti[:, 0, :], t["dst_tiles"]).then_inc(st["ld"], 16)
            sp.dma_start(ti[:, 1, :], t["prev_tiles"]).then_inc(st["ld"], 16)
            sp.wait_ge(st["k"], 3)
            with sp.Fori(0, NCH + 1) as i:
                sp.dma_start(d["res"][bass.ds(i * CR, CR), :].rearrange("(p c) d -> p (c d)", c=C),
                             zero[:]).then_inc(st["out"], 16)
            sp.wait_ge(st["out"], 16 * (NCH + 1))
            sp.wait_ge(st["sq"], 3)
            sp.dma_start(d["lin"].rearrange("s (q j) -> q s j", j=J), L[:]).then_inc(st["ld"], 16)
            sp.wait_ge(st["ld"], 96)
            for s in range(3):
                sp.dma_start(d["search"][:, s * P:(s + 1) * P],
                             d["lin"][s, :].rearrange("(k f) -> k f", f=P)).then_inc(st["ld"], 16)
            sp.wait_ge(st["ld"], 144)

        @block.gpsimd
        def _(po):
            po.memset(ident[:], 0.0)
            po.memset(g["last_row"][:], 0.0)
            po.drain()
            po.affine_select(out=ident[:], in_=ident[:], compare_op=ALU.not_equal, fill=1.0,
                             base=0, pattern=[[-1, P]], channel_multiplier=1).then_inc(st["k"], 1)
            po.affine_select(out=g["last_row"][:], in_=g["last_row"][:], compare_op=ALU.not_equal, fill=1.0,
                             base=1 - P, pattern=[[1, 1]], channel_multiplier=1).then_inc(st["k"], 1)
            po.memset(zero[:], 0.0).then_inc(st["k"], 1)

        @block.tensor
        def _(pe):
            pe.wait_ge(st["k"], 2)
            pe.wait_ge(st["rt"], 1)
            for n in range(3):
                last = nc.tensor.transpose(ps[0:HEADS, 1024 + n * P:1024 + (n + 1) * P], whole[:, n, :], ident[:])
            last.then_inc(st["rt"], 1)
            pe_part(nc, st, g, sc, [False, True, True], pe)

        @block.scalar
        def _(act):
            act.wait_ge(st["sq"], 1)
            act.activation(Z[:], Z[:], ACT.Sqrt).then_inc(st["sq"], 1)

        @block.vector
        def _(v):
            v.memset(g["eps_col"][:], EPS)
            sc.begin(v)
            v.wait_ge(st["ld"], 80)
            v.wait_ge(st["k"], 3)
            for n, a in enumerate((dp, dc, dn)):
                v.tensor_copy(a[:], raw[:, n, :])
            v.drain()
            v.tensor_tensor(F["same_prev"][:], dc[:], dp[:], ALU.is_equal)
            v.tensor_tensor(F["same_next"][:], dc[:], dn[:], ALU.is_equal)
            v.tensor_scalar(F["first"][:], dc[:], dp[:, 0:1], None, ALU.is_equal)
            v.tensor_scalar(F["last"][:], dc[:], dn[:, J - 1:J], None, ALU.is_equal)
            v.tensor_tensor(whole[:, 0, :], over(dc[:, J - 1:J], [P, HEADS]), over(dp[:, 0:1], [P, HEADS]), ALU.is_equal)
            v.tensor_tensor(whole[:, 1, :], over(dc[:, 0:1], [P, HEADS]), over(dn[:, J - 1:J], [P, HEADS]), ALU.is_equal)
            v.drain()
            v.tensor_scalar(F["tail"][:], F["same_next"][:], -1.0, 1.0, ALU.mult, ALU.add)
            v.tensor_scalar(F["pen_prev"][:], F["same_prev"][:], -1.0, BIG, ALU.add, ALU.mult)
            v.tensor_scalar(F["pen_first"][:], F["first"][:], -1.0, BIG, ALU.add, ALU.mult)
            v.tensor_scalar(whole[:, 2, :], whole[:, 0, :], -1.0, BIG, ALU.add, ALU.mult).then_inc(st["rt"], 1)
            v.wait_ge(st["rt"], 2)
            for n, name in enumerate(("whole_prev", "whole_next", "pen_whole")):
                v.tensor_copy(RT[name][:], ps[0:HEADS, 1024 + n * P:1024 + (n + 1) * P])
            v.drain()
            v.tensor_copy(X[:, :, 0], ew[:])
            v.drain()
            sc.total(v, Y, X)
            sc.spread(v, X, Y, T)
            v.tensor_scalar(Y[:], X[:], 1.0, None, ALU.add)
            v.drain()
            v.tensor_scalar(X[:], Y[:], 0.0, None, ALU.is_gt)
            v.tensor_scalar(Z[:], Y[:], 1.0e-30, None, ALU.max).then_inc(st["sq"], 1)
            v.wait_ge(st["sq"], 2)
            v.reciprocal(Y[:], Z[:])
            v.drain()
            v.tensor_tensor(L[:, 3, :], Y[:, :, 0], X[:, :, 0], ALU.mult)
            v.drain()
            v.tensor_scalar(Y[:, :, 0], eno[:], 1.0, None, ALU.mult)
            v.drain()
            sc.spread(v, X, Y, T)
            v.tensor_copy(L[:, 5, :], X[:, :, 0])
            v.tensor_copy(L[:, 4, :], F["tail"][:])
            v.tensor_copy(L[:, 0, :], dc[:])
            v.tensor_tensor(L[:, 2, :], L[:, 3, :], F["tail"][:], ALU.mult)
            v.scalar_tensor_tensor(out=L[:, 1, :], in0=eno[:], scalar=1.0, in1=F["tail"][:], op0=ALU.add, op1=ALU.mult)
            v.tensor_copy(g["META"][:, M_DST, :], ti[:, 0, :])
            v.tensor_copy(g["META"][:, M_PREV, :], ti[:, 1, :]).then_inc(st["sq"], 1)
    st.close()


def find_sources(g):
    nc, t, d = g["nc"], g["t"], g["d"]
    st = Stage(nc, "find", ["tick", "ld", "tl", "g0", "g1"], ["kf", "fine"])
    w = Work(st, pool=dict(g0=8 * C * ECH, g1=8 * C * ECH))
    half = ET // 2
    src = st.sb("src", [P, ET], I32)
    srcf = st.sb("srcf", [P, ET])
    firsti = st.sb("firsti", [P, ET], I32)
    first = st.sb("first", [P, ET])
    junk = st.sb("junk", [P, C, ET])
    kf = st.sb("kf", [P, 2, C])
    kc = st.sb("kc", [P, 2, C], I32)
    S = st.sb("S", [P, 2, C, 3 * P])
    acc = st.sb("acc", [P, 2, 2, C])
    POS = st.sb("POS", [P, 2, ET])
    TR = st.sb("TR", [half, 3, 2, P])
    TL = st.sb("TL", [P, 3, ET])
    ew = st.sb("ew", [P, ET])
    a, b, c = (st.sb(x, [P, ET]) for x in ("a", "b", "c"))
    dsti = st.sb("dsti", [P, ET], I32)
    got = [st["g0"], st["g1"]]
    META, IDX, ps = g["META"], g["IDX"], g["ps"]

    def load(sp):
        sp.dma_start(src[:], t["src_tiles"]).then_inc(st["ld"], 16)
        sp.dma_start(firsti[:], over(t["first"].unsqueeze(0), [P, ET])).then_inc(st["ld"], 16)
        sp.dma_start(ew[:], t["ew_tiles"]).then_inc(st["ld"], 16)
        sp.dma_start(dsti[:], t["dst_tiles"]).then_inc(st["ld"], 16)
        for s in range(3):
            sp.dma_start(TR[:, s], d["lin"][3 + s, :].rearrange("(a k p) -> k a p", a=2, p=P)).then_inc(st["ld"], 16)

    def turn_runs(pe):
        pe.wait_ge(st["ld"], 112)
        for s in range(3):
            for h in (0, 1):
                last = nc.tensor.transpose(ps[:, (2 * s + h) * P:(2 * s + h) * P + half], TR[:, s, h, :],
                                           g["ident"][0:half, 0:half])
        last.then_inc(st["tl"], 1)

    def begin(v):
        v.wait_ge(st["ld"], 112)
        v.tensor_copy(srcf[:], src[:])
        v.tensor_copy(first[:], firsti[:])
        v.wait_ge(st["tl"], 1)
        for s in range(3):
            for h in (0, 1):
                v.tensor_copy(TL[:, s, h * half:(h + 1) * half], ps[:, (2 * s + h) * P:(2 * s + h) * P + half])
        v.drain()

    def coarse(v, n, k, i):
        v.drain()
        v.wait_ge(st["fine"], n + 1)
        for c_ in range(C):
            v.tensor_scalar(junk[:, c_, :], first[:], srcf[:, bass.ds(n * C + c_, 1)], -1.0, ALU.is_le, ALU.add,
                            accum_out=kf[:, k, c_:c_ + 1])
        v.drain()
        v.tensor_scalar(kc[:, k, :], kf[:, k, :], 0.0, None, ALU.max).then_inc(st["kf"], 1)

    def fetch(po, n, k, i):
        po.wait_ge(st["kf"], n + 3)
        po.sem_inc(st["tick"], 1)
        for c_ in range(C):
            po.indirect_dma_start(out=S[:, k, c_, :], out_offset=None, in_=d["search"],
                                  in_offset=bass.IndirectOffsetOnAxis(ap=kc[:, k, c_:c_ + 1], axis=0),
                                  bounds_check=ET - 1, oob_is_err=False).then_inc(got[k], 16)

    base = dict(COUNTED)

    def fine(v, n, k, i):
        v.drain()
        v.wait_ge(got[k], base[f"g{k}"] + 16 * C * (i + 1))
        for s in (0, 1):
            for c_ in range(C):
                v.scalar_tensor_tensor(out=junk[:, c_, 0:P], in0=S[:, k, c_, 0:P],
                                       scalar=srcf[:, bass.ds(n * C + c_, 1)],
                                       in1=S[:, k, c_, (s + 1) * P:(s + 2) * P],
                                       op0=ALU.is_equal, op1=ALU.mult, accum_out=acc[:, k, s, c_:c_ + 1])
            v.drain()
        v.tensor_copy(POS[:, :, bass.ds(n * C, C)], acc[:, k, :, :]).then_inc(st["fine"], 1)

    def end(v):
        v.drain()
        v.tensor_scalar(a[:], POS[:, 0, :], 0.5, None, ALU.is_gt)
        v.tensor_scalar(b[:], srcf[:], float(EP), None, ALU.add)
        v.drain()
        v.scalar_tensor_tensor(out=c[:], in0=POS[:, 0, :], scalar=-1.0, in1=b[:], op0=ALU.add, op1=ALU.subtract)
        v.drain()
        v.tensor_tensor(c[:], c[:], a[:], ALU.mult)
        v.drain()
        v.tensor_tensor(IDX[:, I_SRCROW, :], c[:], b[:], ALU.add)
        v.drain()
        v.scalar_tensor_tensor(out=c[:], in0=POS[:, 0, :], scalar=-1.0 - EP, in1=a[:], op0=ALU.add, op1=ALU.mult)
        v.drain()
        v.tensor_scalar(IDX[:, I_SRCROW2, :], c[:], float(EP), None, ALU.add)
        v.tensor_copy(IDX[:, I_SRC, :], src[:])
        v.tensor_copy(IDX[:, I_DST, :], dsti[:])
        v.tensor_scalar(b[:], TL[:, 1, :], -SKIP, SKIP, ALU.mult, ALU.add)
        v.drain()
        v.tensor_tensor(IDX[:, I_OUT, :], b[:], META[:, M_DST, :], ALU.add)
        v.scalar_tensor_tensor(out=c[:], in0=a[:], scalar=-1.0, in1=POS[:, 1, :], op0=ALU.mult, op1=ALU.add)
        v.drain()
        v.tensor_scalar(c[:], c[:], 1.0, None, ALU.add)
        v.drain()
        v.tensor_tensor(c[:], c[:], ew[:], ALU.mult)
        v.drain()
        v.tensor_tensor(META[:, M_NORM, :], c[:], TL[:, 0, :], ALU.mult)
        v.tensor_tensor(a[:], TL[:, 0, :], TL[:, 0, :], ALU.mult)
        v.drain()
        v.tensor_tensor(META[:, M_SELF, :], a[:], TL[:, 1, :], ALU.mult)
        v.tensor_scalar(META[:, M_REP, :], TL[:, 1, :], g["last_row"][:], None, ALU.max)

    w.on("sync", before=load)
    w.on("tensor", before=turn_runs)
    w.on("vector", (coarse, 0), (fine, 1), before=begin, after=end)
    w.on("gpsimd", (fetch, 0))
    return w


def norm_stats(v, st, X, small, S6):
    tiles = X.shape[1]
    for c in range(tiles):
        v.bn_stats(S6[:, c, :], X[:, c, :])
    v.drain()
    v.tensor_tensor(small[:, 0, :], S6[:, :, 1], S6[:, :, 4], ALU.add)
    v.tensor_tensor(small[:, 2, :], S6[:, :, 1], S6[:, :, 4], ALU.subtract)
    v.tensor_tensor(small[:, 1, :], S6[:, :, 2], S6[:, :, 5], ALU.add)
    v.drain()
    v.tensor_scalar(small[:, 0, :], small[:, 0, :], -0.5, None, ALU.mult)
    v.tensor_tensor(small[:, 2, :], small[:, 2, :], small[:, 2, :], ALU.mult)
    v.drain()
    v.scalar_tensor_tensor(out=small[:, 1, :], in0=small[:, 2, :], scalar=D / 4.0, in1=small[:, 1, :],
                           op0=ALU.mult, op1=ALU.add).then_inc(st["var"], 1)


def norm_shift(v, st, small):
    v.reciprocal(small[:, 2, :], small[:, 3, :])
    v.drain()
    v.tensor_tensor(small[:, 4, :], small[:, 0, :], small[:, 2, :], ALU.mult).then_inc(st["nb"], 1)


def groups_of(width):
    m = min(4, 512 // width)
    return [list(range(c, min(c + m, C))) for c in range(0, C, m)]


def rows(g, kind):
    nc, t, d, out = g["nc"], g["t"], g["d"], g["out"]
    edges = kind.endswith("edges")
    norm = kind not in ("h2", "x1")
    product = kind != "out"
    width = {"gt": GW, "gt_edges": GW, "qkv_edges": 3 * D}.get(kind, D)
    bias = kind in ("h1", "h2", "x1")
    G = len(groups_of(width))
    has_y = kind in ("qy", "qkv_edges", "out")
    NB = 4
    total = ECH if edges else NCH
    per = dict(tr=2, ht=2, mm=G, ev=G)
    per.update({n: 1 for n in ("var", "root", "nb", "h", "y", "yc")})
    st = Stage(nc, f"r_{kind}", ["tick", "w", "wx", "ix", "st0", "st1", "sc0", "sc1"] + [f"{x}{b}" for x in ("ld", "sh") for b in range(NB)],
               list(per), {n: NB * p for n, p in per.items()})

    def at(name, n, back=0, part=None):
        return per[name] * (n - back + NB) + (per[name] if part is None else part + 1)

    tiled = kind == "qkv_edges"
    w = Work(st, 2, deep=True, pool=dict(sc0=8 * C * ECH, sc1=8 * C * ECH) if tiled else {})
    base = dict(COUNTED)
    ld, sh, sto = [st[f"ld{b}"] for b in range(NB)], [st[f"sh{b}"] for b in range(NB)], [st["st0"], st["st1"]]
    ps, ident = g["ps"], g["ident"]
    sca = [st["sc0"], st["sc1"]]
    if kind == "h1":
        XH = st.sb("XH", [P, NB, C, 2 * D])
        H, A = XH[:, :, :, 0:D], XH[:, :, :, D:2 * D]
    else:
        A = st.sb("A", [P, NB, C, D])
        HY = st.sb("HY", [P, NB, C, 2 * D] if kind == "out" else [P, 2, C, D]) if norm else None
        H = HY[:, :, :, 0:D] if norm else None
    XB = HB = NB if kind == "out" else 2
    X2 = st.sb("X2", [P, XB, C, D]) if has_y else None
    Y = st.sb("Y", [P, 2, C, D]) if has_y else None
    R2 = st.sb("R2", [P, NB, C, D + HEADS if kind == "out" else D])
    S6 = st.sb("S6", [P, C, 6])
    small = st.sb("small", [P, 2, 5, C])
    rb = st.sb("rb", [P, C, HEADS])
    HT = st.sb("HT", [D + 1, 2, CR])
    O = st.sb("O", [P, 2, C, width])
    ic = st.sb("ic", [P, 2, C], I32)
    W = st.sb("W", [D + 1, width])
    extra = weights(g, st, W, kind)
    K = D + 1 if bias else D
    brow = st.sb("brow", [P, D])
    row = 0 if edges else EP

    def chunk(table, n, base=0):
        return chunk_tiles(table, n) if tiled else chunk_rows(table, n, base)


    first = {"h1": t["x"], "h2": d["h1"], "x1": d["h2"], "out": d["yn"]}.get(kind, d["x1"])
    second = {"x1": t["x"], "qkv_edges": d["zr"], "out": d["res"]}.get(kind)
    second_row = 0

    def xs(k, b):
        return X2[:, b % XB] if has_y else A[:, b], H[:, b if kind in ("h1", "out") else k]

    to = {"h1": d["h1"], "h2": d["h2"], "x1": d["x1"], "gt": d["gt"], "gt_edges": d["gt"], "qy": d["q"],
          "qkv_edges": d["q"]}.get(kind)
    nld = 2 if second is not None else 1
    nst = 2 if kind in ("qy", "qkv_edges") else 1

    def load(sp, n, k, i, b, j):
        if kind == "h1":
            sp.wait_ge(sh[b], 16 * j)
            sp.sem_inc(st["tick"], 1)
        sp.wait_ge(st[used], at(used, n, NB))
        sp.dma_start(A[:, b], chunk(first, n, 0 if kind in ("h1", "out") else row)).then_inc(ld[b], 16)
        if second is not None:
            sp.dma_start(R2[:, b], chunk(second, n)).then_inc(ld[b], 16)

    def begin_v(v):
        if product:
            v.memset(HT[:, :, :], 1.0)
            v.drain()
            extra["vector"](v)
        if kind == "qy":
            v.wait_ge(st["w"], extra["loads"])
            v.tensor_scalar(brow[:], brow[:], 0.0, None, ALU.max)
            v.drain()

    def stats(v, n, k, i, b, j):
        X, _ = xs(k, b)
        v.drain()
        v.wait_ge(ld[b], 16 * nld * (j + 1))
        v.wait_ge(st["h"], at("h", n, 2))
        if has_y:
            v.wait_ge(st["y"], at("y", n, XB))
        if kind == "qy":
            v.tensor_tensor(X, A[:, b], over(brow[:].unsqueeze(1), [P, C, D]), ALU.add)
            v.drain()
        if kind == "qkv_edges":
            v.tensor_tensor(X, A[:, b], R2[:, b], ALU.add)
            v.drain()
        if kind == "out":
            v.tensor_scalar(rb[:], R2[:, b, :, D:D + HEADS], 1.0e-8, None, ALU.add)
            v.drain()
            v.reciprocal(rb[:], rb[:])
            v.drain()
            v.tensor_tensor(X.rearrange("p c (h e) -> p c h e", h=HEADS),
                            R2[:, b, :, 0:D].rearrange("p c (h e) -> p c h e", h=HEADS),
                            over(rb[:].unsqueeze(3), [P, C, HEADS, HC]), ALU.mult)
            v.drain()
            v.tensor_tensor(X, X, A[:, b], ALU.add)
            v.drain()
        norm_stats(v, st, X, small[:, k], S6)

    def shift(v, n, k, i, b, j):
        v.wait_ge(st["root"], at("root", n))
        norm_shift(v, st, small[:, k])

    def sum_y(v, n, k, i, b, j):
        X, Hn = xs(k, b)
        v.wait_ge(st["h"], at("h", n))
        if kind == "out":
            v.sem_inc(st["tick"], 1)
        if tiled:
            v.wait_ge(sca[k], base[f"sc{k}"] + 16 * C * i)
        else:
            v.wait_ge(sto[k], 16 * nst * i)
        if kind == "out":
            v.sem_inc(st["tick"], 1)
            v.wait_ge(st["yc"], at("yc", n, 2))
            v.sem_inc(st["tick"], 1)
        v.tensor_tensor(Y[:, k], X, Hn, ALU.add).then_inc(st["y"], 1)

    def copy_y(act, n, k, i, b, j):
        act.wait_ge(st["y"], at("y", n))
        act.activation(HY[:, b, :, D:2 * D], Y[:, k], ACT.Copy).then_inc(st["yc"], 1)

    def to_sbuf(v, n, k, i, b, j):
        for h, cols in enumerate((slice(0, 4 * P), slice(4 * P, CR))):
            v.wait_ge(st["tr"], at("tr", n, part=h))
            if h == 0:
                v.wait_ge(st["mm"], at("mm", n, 2))
            v.tensor_copy(HT[0:D, k, cols], ps[0:D, 2048 + cols.start:2048 + cols.stop]).then_inc(st["ht"], 1)

    def root(act, n, k, i, b, j):
        act.wait_ge(st["var"], at("var", n))
        act.activation(small[:, k, 3, :], small[:, k, 1, :], ACT.Sqrt, bias=g["eps_col"][:], scale=1.0 / D)           .then_inc(st["root"], 1)

    def apply(act, n, k, i, b, j):
        X, Hn = xs(k, b)
        if product:
            act.wait_ge(st["tr"], at("tr", n, 2))
        if has_y:
            act.wait_ge(st["y"], at("y", n, HB))
        if kind == "out":
            act.wait_ge(sh[b], 16 * j)
        act.wait_ge(st["nb"], at("nb", n))
        for c in range(C):
            last = act.activation(Hn[:, c, :], X[:, c, :], ACT.Relu, bias=small[:, k, 4, c:c + 1],
                                  scale=small[:, k, 2, c:c + 1])
        last.then_inc(st["h"], 1)

    def store_h(act, n, k, i, b, j):
        act.wait_ge(st["h"], at("h", n))
        act.dma_start(chunk_rows(d["hx"], n), XH[:, b]).then_inc(sh[b], 16)

    def turn(pe, n, k, i, b, j):
        if norm:
            pe.wait_ge(st["h"], at("h", n))
            rows_ = xs(k, b)[1]
        else:
            pe.wait_ge(ld[b], 16 * nld * (j + 1))
            rows_ = A[:, b]
        for h, tiles in enumerate(((0, 1, 2, 3), (4, 5, 6))):
            pe.wait_ge(st["ht"], at("ht", n, 1, h))
            for c in tiles:
                last = nc.tensor.transpose(ps[0:D, 2048 + c * P:2048 + (c + 1) * P], rows_[:, c, :], ident[:])
            last.then_inc(st["tr"], 1)

    def multiply(pe, n, k, i, b, j):
        for q, tiles in enumerate(groups_of(width)):
            pe.wait_ge(st["ht"], at("ht", n, part=int(tiles[-1] >= 4)))
            pe.wait_ge(st["ev"], at("ev", n, part=q - 2))
            bank = 3072 + 512 * ((G * k + q) % 2)
            for m, c in enumerate(tiles):
                last = nc.tensor.matmul(ps[:, bank + m * width:bank + (m + 1) * width],
                                        HT[0:K, k, c * P:(c + 1) * P], W[0:K, :], start=True, stop=True)
            last.then_inc(st["mm"], 1)

    def from_psum(eng, n, k, i, b, j):
        eng.wait_ge(sto[k], 16 * nst * i)
        for q, tiles in enumerate(groups_of(width)):
            eng.wait_ge(st["mm"], at("mm", n, part=q))
            bank = 3072 + 512 * ((G * k + q) % 2)
            z = ps[:, bank:bank + len(tiles) * width].rearrange("p (c w) -> p c w", w=width)
            cs = slice(tiles[0], tiles[-1] + 1)
            if kind == "x1":
                eng.tensor_tensor(O[:, k, cs, :], z, R2[:, b, cs, 0:D], ALU.add).then_inc(st["ev"], 1)
            else:
                eng.activation(O[:, k, cs, :], z, ACT.Relu if kind in ("h1", "h2") else ACT.Copy)                   .then_inc(st["ev"], 1)

    def store(act, n, k, i, b, j):
        if product:
            act.wait_ge(st["ev"], at("ev", n))
        if has_y:
            act.wait_ge(st["y"], at("y", n))
        if kind == "out":
            act.wait_ge(st["yc"], at("yc", n))
            act.dma_start(chunk(d["hy"], n), HY[:, b]).then_inc(sh[b], 16)
            act.dma_start(chunk(out, n), Y[:, k]).then_inc(sto[k], 16)
            return
        act.dma_start(chunk(to, n, row), O[:, k, :, 0:D] if tiled else O[:, k]).then_inc(sto[k], 16)
        if kind == "qy":
            act.dma_start(chunk(d["yn"], n), Y[:, k]).then_inc(sto[k], 16)
        if tiled:
            act.dma_start(chunk(d["kv"], n), O[:, k, :, D:3 * D]).then_inc(sto[k], 16)

    def end(act):
        for k in (0, 1):
            act.wait_ge(sto[k], 16 * nst * (total // 2))
        if kind in ("h1", "out"):
            for b in range(NB):
                act.wait_ge(sh[b], 16 * (total // NB))

    def scatter_y(po, n, k, i, b, j):
        po.wait_ge(sca[k], base[f"sc{k}"] + 16 * C * i)
        po.tensor_copy(ic[:, k, :], g["IDX"][:, I_OUT, bass.ds(n * C, C)]).then_inc(st["ix"], 1)
        po.wait_ge(st["ix"], n + 1)
        po.sem_inc(st["tick"], 1)
        po.wait_ge(st["y"], at("y", n))
        po.sem_inc(st["tick"], 1)
        for c in range(C):
            po.indirect_dma_start(out=d["yn"], in_=Y[:, k, c, :], in_offset=None,
                                  out_offset=bass.IndirectOffsetOnAxis(ap=ic[:, k, c:c + 1], axis=0),
                                  bounds_check=NP - 1, oob_is_err=False).then_inc(sca[k], 16)

    def end_scatter(po):
        for k in (0, 1):
            po.wait_ge(sca[k], base[f"sc{k}"] + 16 * C * (ECH // 2))

    used = "var" if has_y else "ev" if kind == "x1" else "h" if norm else "tr"
    w.on("sync", (load, 0), before=lambda sp: extra["sync"](sp, brow))
    if norm and product:
        w.on("vector", *([(sum_y, 2)] if has_y else []), (shift, 1), (stats, 0), (to_sbuf, 2), before=begin_v)
        w.on("scalar", (apply, 1), (root, 0), *([(store_h, 1)] if kind == "h1" else []), (from_psum, 2), (store, 2),
             after=end)
        w.on("tensor", (multiply, 2), (turn, 1), before=extra["tensor"])
        if tiled:
            w.on("gpsimd", (scatter_y, 2), after=end_scatter)
    elif norm:
        w.on("vector", (shift, 1), (stats, 0), before=begin_v)
        w.on("gpsimd", (sum_y, 2))
        w.on("scalar", (apply, 1), (copy_y, 2), (store, 2), (root, 0), after=end)
    elif kind == "x1":
        w.on("vector", (to_sbuf, 1), (from_psum, 2), before=begin_v)
        w.on("scalar", (store, 2), after=end)
        w.on("tensor", (multiply, 1), (turn, 0), before=extra["tensor"])
    else:
        w.on("vector", (to_sbuf, 1), before=begin_v)
        w.on("scalar", (from_psum, 2), (store, 2), after=end)
        w.on("tensor", (multiply, 1), (turn, 0), before=extra["tensor"])
    return w


def weights(g, st, W, kind):
    t = g["t"]
    layer = {"h1": 1, "h2": 2, "x1": 3, "gcn1": 1, "gcn2": 2, "gcn3": 3}.get(kind)
    gat = {"gt": 0, "gt_edges": 0, "gat0": 1, "gat1": 2}.get(kind)
    att = st.sb("att", [D, 2, D])
    tmp = st.sb("tmp", [D, 2, D])
    loads = [0]

    def sync(sp, brow=None):
        if layer:
            sp.dma_start(W[0:D, :], t[f"gcn_w{layer}"]).then_inc(st["w"], 16)
            sp.dma_start(W[D:D + 1, :], t[f"gcn_b{layer}"].unsqueeze(0)).then_inc(st["w"], 16)
        elif gat is not None:
            sp.dma_start(W[0:D, 0:D], t["gat_w"][gat, :, :]).then_inc(st["w"], 16)
            for s, name in enumerate(("gat_src", "gat_dst")):
                sp.dma_start(att[:, s, :], over(t[name][gat].rearrange("h c -> (h c)").unsqueeze(0), [D, D]))\
                    .then_inc(st["w"], 16)
        elif kind == "qy":
            sp.dma_start(W[0:D, :], t["q_w"]).then_inc(st["w"], 16)
            sp.dma_start(brow[:], over(t["gat_b"][2:3, :], [P, D])).then_inc(st["w"], 16)
        elif kind == "qkv_edges":
            for s, name in enumerate(("q_w", "k_w", "v_w")):
                sp.dma_start(W[0:D, s * D:(s + 1) * D], t[name]).then_inc(st["w"], 16)

    n = 32 if layer or kind == "qy" else 48 if gat is not None or kind == "qkv_edges" else 0

    def vector(v):
        if gat is None:
            return
        v.wait_ge(st["w"], n)
        for s in (0, 1):
            v.tensor_tensor(tmp[:, s, :], W[0:D, 0:D], att[:, s, :], ALU.mult)
        v.drain()
        for s in (0, 1):
            last = v.reduce_sum(W[0:D, D + s * HEADS:D + (s + 1) * HEADS],
                                tmp[:, s, :].rearrange("p (h e) -> p h e", h=HEADS), AX.X)
        last.then_inc(st["wx"], 1)

    def tensor(pe):
        if n:
            pe.wait_ge(st["w"], n)
        if gat is not None:
            pe.wait_ge(st["wx"], 1)

    return dict(sync=sync, vector=vector, tensor=tensor, loads=n)


def aggregate(g, kind):
    nc, t, d = g["nc"], g["t"], g["d"]
    gcn, gat, edge = kind.startswith("gcn"), kind.startswith("gat"), kind == "edge"
    first, add, last_gat = kind == "gcn1", kind == "gcn3", kind == "gat2"
    wz = D + 1 if edge else D
    wo = wz if edge or gcn or last_gat else GW
    gw = 2 * D if first else GW if gat else wz
    K = D + 1 if gcn or edge else D
    groups = groups_of(wo)
    G_ = len(groups)
    ngot = 2 * C if first else C
    st = Stage(nc, f"a_{kind}", ["tick", "one", "os", "ix", "w", "wx", "bc", "ld0", "ld1", "g0", "g1", "st0", "st1", "lx0", "lx1", "sx0", "sx1", "zero", "sc0", "sc1"],
               ["s", "xm", "dg", "pz", "ct", "zt", "rl", "mm", "ev"], dict(pz=2 * C, ct=C, mm=2 * G_))
    pool = dict(g0=8 * ngot * ECH, g1=8 * ngot * ECH) if gcn else dict(sc0=8 * C * ECH, sc1=8 * C * ECH) if edge else {}
    w = Work(st, pool=pool)
    base = dict(COUNTED)
    G = None if gat else st.sb("G", [P, 2, C, gw])
    OWN = st.sb("OWN", [P, 2, C, gw]) if gcn else None
    DG = st.sb("DG", [P, 2, C, P]) if gcn else None
    MSG = st.sb("MSG", [P, 2, C, D]) if gat else None
    al = st.sb("al", [P, 2, C, HEADS])
    DR = st.sb("DR", [P, 2, C, P], I32)
    S = st.sb("S", [P, 2, C, P])
    XM = st.sb("XM", [P, 2, C, P])
    ZT = st.sb("ZT", [D + 1, 2, CR])
    RL = st.sb("RL", [D, 2, CR]) if gat else None
    W = st.sb("W", [D + 1, wo])
    bcol = st.sb("bcol", [D, 1])
    X0 = st.sb("X0", [P, 2, C, D])
    O = st.sb("O", [P, 2, C, D if edge else wo])
    rc = st.sb("rc", [P, C])
    mc = st.sb("mc", [P, 2, M_N, C])
    XA = st.sb("XA", [P, C, P]) if gat else None
    ic = st.sb("ic", [P, 2, 2, C], I32)
    ld, got, sto = [st["ld0"], st["ld1"]], [st["g0"], st["g1"]], [st["st0"], st["st1"]]
    sca, lx, sx = [st["sc0"], st["sc1"]], [st["lx0"], st["lx1"]], [st["sx0"], st["sx1"]]
    ps, ident = g["ps"], g["ident"]
    table = {"gcn1": d["hx"], "gcn2": d["h1"], "gcn3": d["h2"]}.get(kind)
    to = {"gcn1": d["h1"], "gcn2": d["h2"], "gcn3": d["x1"], "gat0": d["gt2"], "gat1": d["gt2"], "gat2": d["zr"]}.get(kind)
    nld = 1 if first else 2
    nst = 1
    by_vector = add or edge
    extra = weights(g, st, W, kind)

    def begin_sp(sp):
        extra["sync"](sp)
        if gat:
            sp.dma_start(bcol[:], t["gat_b"][int(kind[-1]), :].unsqueeze(1)).then_inc(st["bc"], 16)

    def load(sp, n, k, i):
        if gat:
            sp.wait_ge(st["xm"], n + 1)
            sp.sem_inc(st["tick"], 1)
        sp.wait_ge(st["s"], n + 1)
        sp.dma_start(DR[:, k], over(t["dst_lin"][bass.ds(n * CR, CR)].rearrange("(c p) -> c p", p=P).unsqueeze(0), [P, C, P]))\
            .then_inc(ld[k], 16)
        if gat:
            sp.dma_start(al[:, k], chunk_tiles(d["alpha"], n)).then_inc(ld[k], 16)
        elif edge:
            sp.wait_ge(st["pz"], C * n + C)
            sp.dma_start(G[:, k], chunk_tiles(d["msg3"], n)).then_inc(ld[k], 16)
        elif not first:
            sp.wait_ge(st["pz"], C * n + C)
            sp.dma_start(OWN[:, k], chunk_tiles(table[0:EP, :], n)).then_inc(ld[k], 16)

    def load_x0(sp, n, k, i):
        sp.wait_ge(st["ev"], G_ * n + 2 - G_)
        sp.dma_start(X0[:, k], chunk_tiles(d["base" if edge else "x0d"], n)).then_inc(lx[k], 16)

    def fetch(po, n, k, i):
        po.wait_ge(st["pz"], C * n + C)
        if first:
            po.sem_inc(st["tick"], 1)
            po.wait_ge(sx[k], 16 * i)
        po.tensor_copy(ic[:, k, 0, :], g["IDX"][:, I_SRC if first else I_SRCROW, bass.ds(n * C, C)])
        po.tensor_copy(ic[:, k, 1, :], g["IDX"][:, I_DST, bass.ds(n * C, C)]).then_inc(st["ix"], 1)
        po.wait_ge(st["ix"], n + 1)
        po.sem_inc(st["tick"], 1)
        for c in range(C):
            po.indirect_dma_start(out=G[:, k, c, :], out_offset=None, in_=table,
                                  in_offset=bass.IndirectOffsetOnAxis(ap=ic[:, k, 0, c:c + 1], axis=0),
                                  bounds_check=table.shape[0] - 1, oob_is_err=False).then_inc(got[k], 16)
            if first:
                po.indirect_dma_start(out=OWN[:, k, c, :], out_offset=None, in_=table,
                                      in_offset=bass.IndirectOffsetOnAxis(ap=ic[:, k, 1, c:c + 1], axis=0),
                                      bounds_check=NP - 1, oob_is_err=False).then_inc(got[k], 16)

    def begin_v(v):
        v.memset(ZT[:], 1.0)
        v.drain()
        if edge or last_gat:
            v.tensor_copy(W[0:wo, :], ident[0:wo, 0:wo]).then_inc(st["zero"], 1)
        else:
            v.memset(rc[:], 0.0).then_inc(st["zero"], 1)
        extra["vector"](v)

    def build_s(v, n, k, i):
        v.wait_ge(ld[k], 16 * nld * (i + 1))
        v.wait_ge(st["pz"], C * n + C)
        v.wait_ge(st["zt"], n + 1)
        v.wait_ge(st["dg"], n + 1) if gcn else None
        v.tensor_copy(mc[:, k], g["META"][:, :, bass.ds(n * C, C)])
        v.drain()
        if gat:
            v.tensor_tensor(MSG[:, k].rearrange("p c (h e) -> p c h e", h=HEADS),
                            g["GR"][:, bass.ds(n * C, C), 0:D].rearrange("p c (h e) -> p c h e", h=HEADS),
                            over(al[:, k].unsqueeze(3), [P, C, HEADS, HC]), ALU.mult)
        if not gat:
            v.tensor_tensor(XM[:, k], DR[:, k], over(mc[:, k, M_PREV, :].unsqueeze(2), [P, C, P]), ALU.is_equal)
        for c in range(C):
            if gcn:
                last = v.tensor_scalar(S[:, k, c, :], DR[:, k, c, :], mc[:, k, M_DST, c:c + 1],
                                       mc[:, k, M_NORM, c:c + 1], ALU.is_equal, ALU.mult)
            else:
                last = v.tensor_scalar(S[:, k, c, :], DR[:, k, c, :], mc[:, k, M_DST, c:c + 1], None, ALU.is_equal)
        last.then_inc(st["s"], 1)

    def build_xm(act, n, k, i):
        act.wait_ge(st["s"], n + 3)
        act.wait_ge(st["zt"], n + 1)
        for c in range(C):
            act.activation(XA[:, c, :], DR[:, k, c, :], ACT.Abs, bias=mc[:, k, M_PREV, c:c + 1], scale=-1.0)
        act.drain()
        act.activation(XM[:, k], XA[:], ACT.Relu, bias=1.0, scale=-1.0).then_inc(st["xm"], 1)
        act.drain()

    def build_dg(act, n, k, i):
        act.wait_ge(st["s"], n + 3)
        act.wait_ge(st["pz"], C * n + C)
        for c in range(C):
            last = act.activation(DG[:, k, c, :], ident[:], ACT.Copy, scale=mc[:, k, M_SELF, c:c + 1])
        last.then_inc(st["dg"], 1)

    def sums(pe, n, k, i):
        pe.wait_ge(st["s"], n + 3)
        if gcn:
            pe.wait_ge(st["dg"], n + 3)
            pe.wait_ge(got[k], base[f"g{k}"] + 16 * ngot * (i + 1))
        pe.wait_ge(ld[k], 16 * nld * (i + 1))
        for c in range(C):
            z = ps[0:wz, c * P:(c + 1) * P]
            if c in (0, 4):
                pe.wait_ge(st["ct"], C * n + (4 if c == 0 else C))
            rows_ = MSG[:, k, c, :] if gat else G[:, k, c, 0:wz]
            last = nc.tensor.matmul(z, rows_, S[:, k, c, :], start=True, stop=not gcn)
            if gcn:
                last = nc.tensor.matmul(z, OWN[:, k, c, 0:D], DG[:, k, c, :], start=False, stop=True)
            last.then_inc(st["pz"], 1)

    def carry(v, n, k, i):
        if gat:
            v.wait_ge(st["xm"], n + 3)
        if gat:
            v.wait_ge(st["rl"], n + 1)
        else:
            v.wait_ge(st["mm"], G_ * n + G_)
        for c in range(C):
            before = ZT[0:wz, k, c * P - 1:c * P] if c else ZT[0:wz, 1 - k, CR - 1:CR]
            z = ps[0:wz, c * P:(c + 1) * P]
            if c in (0, 4):
                v.wait_ge(st["pz"], C * n + (4 if c == 0 else C) + 2 * C)
            v.wait_ge(st["ct"], C * n + c + C)
            v.scalar_tensor_tensor(out=ZT[0:wz, k, c * P:(c + 1) * P], in0=XM[0:wz, k, c, :], scalar=before, in1=z,
                                   op0=ALU.mult, op1=ALU.add).then_inc(st["ct"], 1)
        v.wait_ge(st["ct"], C * n + 2 * C)
        v.sem_inc(st["zt"], 1)

    def activate(act, n, k, i):
        act.wait_ge(st["zt"], n + 3)
        act.wait_ge(st["mm"], G_ * n + G_)
        act.activation(RL[:, k, :], ZT[0:D, k, :], ACT.Relu, bias=bcol[:]).then_inc(st["rl"], 1)

    def multiply(pe, n, k, i):
        if gat:
            pe.wait_ge(st["rl"], n + 3)
        else:
            pe.wait_ge(st["zt"], n + 3)
        for q, tiles in enumerate(groups):
            pe.wait_ge(st["ev"], G_ * n + q + 1)
            bank = 1024 + 512 * ((G_ * k + q) % 2)
            for m, c in enumerate(tiles):
                lhs = (RL if gat else ZT)[0:K, k, c * P:(c + 1) * P]
                last = nc.tensor.matmul(ps[:, bank + m * wo:bank + (m + 1) * wo], lhs, W[0:K, :], start=True, stop=True)
            last.then_inc(st["mm"], 1)

    def from_psum(eng, n, k, i):
        if edge:
            eng.wait_ge(sca[k], base[f"sc{k}"] + 16 * C * i)
        else:
            eng.wait_ge(sto[k], 16 * nst * i)
        if by_vector:
            eng.wait_ge(lx[k], 16 * (i + 1))
        for q, tiles in enumerate(groups):
            eng.wait_ge(st["mm"], G_ * n + q + 1 + 2 * G_)
            bank = 1024 + 512 * ((G_ * k + q) % 2)
            z = ps[:, bank:bank + len(tiles) * wo].rearrange("p (c w) -> p c w", w=wo)
            cs = slice(tiles[0], tiles[-1] + 1)
            if add:
                eng.tensor_tensor(O[:, k, cs, :], z, X0[:, k, cs, :], ALU.add).then_inc(st["ev"], 1)
            elif edge:
                eng.tensor_scalar(rc[:, cs], z[:, :, D], 1.0, None, ALU.max)
                eng.drain()
                eng.reciprocal(rc[:, cs], rc[:, cs])
                eng.drain()
                eng.tensor_tensor(O[:, k, cs, :], z[:, :, 0:D], over(rc[:, cs].unsqueeze(2), [P, len(tiles), D]), ALU.mult)
                eng.drain()
                eng.tensor_tensor(O[:, k, cs, :], O[:, k, cs, :], X0[:, k, cs, :], ALU.add).then_inc(st["ev"], 1)
            else:
                eng.activation(O[:, k, cs, :], z, ACT.Relu if gcn else ACT.Copy).then_inc(st["ev"], 1)

    def store(act, n, k, i):
        act.wait_ge(st["ev"], G_ * n + G_ + 2)
        act.dma_start(chunk_tiles(to[0:EP, :], n), O[:, k]).then_inc(sto[k], 16)

    def store_x(sp, n, k, i):
        sp.wait_ge(got[k], base[f"g{k}"] + 16 * ngot * (i + 1))
        sp.dma_start(chunk_tiles(d["x0d"], n), OWN[:, k, :, D:2 * D]).then_inc(sx[k], 16)

    def end_x(sp):
        for k in (0, 1):
            sp.wait_ge(sx[k], 16 * (ECH // 2))

    def end(act):
        for k in (0, 1):
            act.wait_ge(sto[k], 16 * nst * (ECH // 2))

    def scatter(po, n, k, i):
        po.wait_ge(sca[k], base[f"sc{k}"] + 16 * C * i)
        po.tensor_copy(ic[:, k, 0, :], g["IDX"][:, I_OUT, bass.ds(n * C, C)]).then_inc(st["ix"], 1)
        po.wait_ge(st["ix"], n + 1)
        po.wait_ge(st["ev"], G_ * n + G_ + 2)
        po.sem_inc(st["tick"], 1)
        for c in range(C):
            po.indirect_dma_start(out=g["out"], in_=O[:, k, c, :], in_offset=None,
                                  out_offset=bass.IndirectOffsetOnAxis(ap=ic[:, k, 0, c:c + 1], axis=0),
                                  bounds_check=NP - 1, oob_is_err=False).then_inc(sca[k], 16)

    def end_scatter(po):
        for k in (0, 1):
            po.wait_ge(sca[k], base[f"sc{k}"] + 16 * C * (ECH // 2))

    def begin_pe(pe):
        pe.wait_ge(st["zero"], 1)
        extra["tensor"](pe)

    def begin_act(act):
        if gat:
            act.wait_ge(st["bc"], 16)
        if kind == "gat0" or kind == "gat1":
            act.wait_ge(st["zero"], 1)
            act.activation(RL[:, 0, 0:P], ZT[0:D, 0, 0:P], ACT.Relu, bias=bcol[:], scale=0.0).then_inc(st["one"], 1)
            act.wait_ge(st["one"], 2)
            act.activation(O[:, 0, 0, :], ps[:, 1024:1024 + wo], ACT.Copy).then_inc(st["one"], 1)
            act.wait_ge(st["one"], 3)
            act.dma_start(d["gt2"][EP:EP + P, :], O[:, 0, 0, :]).then_inc(st["os"], 16)
            act.wait_ge(st["os"], 16)

    def begin_pe2(pe):
        begin_pe(pe)
        if kind == "gat0" or kind == "gat1":
            pe.wait_ge(st["one"], 1)
            nc.tensor.matmul(ps[:, 1024:1024 + wo], RL[0:D, 0, 0:P], W[0:D, :], start=True, stop=True).then_inc(st["one"], 1)
            pe.wait_ge(st["one"], 3)

    w.on("sync", (load, 0), *([(load_x0, 2)] if by_vector else []), *([(store_x, 2)] if first else []),
         before=begin_sp, after=end_x if first else None)
    w.on("vector", (carry, 2), (build_s, 0), *([(from_psum, 3)] if by_vector else []), before=begin_v)
    act = [(build_dg, 0)] if gcn else []
    act += [(activate, 2), (build_xm, 0)] if gat else []
    act += [] if by_vector else [(from_psum, 3)]
    act += [] if edge else [(store, 3)]
    if act:
        w.on("scalar", *act, before=begin_act, after=None if edge else end)
    w.on("tensor", *([(sums, 1), (multiply, 3)] if gat else [(multiply, 3), (sums, 1)]), before=begin_pe2)
    if gcn:
        w.on("gpsimd", (fetch, 0))
    if edge:
        w.on("gpsimd", (scatter, 3), after=end_scatter)
    return w


def gat_gather(g, layer):
    nc, d = g["nc"], g["d"]
    st = Stage(nc, f"gg{layer}", ["tick", "ix", "g0", "g1", "st0", "st1"], ["cp"])
    w = Work(st, pool=dict(g0=8 * C * ECH, g1=8 * C * ECH))
    G = st.sb("G", [P, 2, C, GW])
    ic = st.sb("ic", [P, 2, C], I32)
    got, sto = [st["g0"], st["g1"]], [st["st0"], st["st1"]]
    base = dict(COUNTED)
    table, column = (d["gt2"], I_SRCROW2) if layer else (d["gt"], I_SRCROW)

    def fetch(po, n, k, i):
        po.wait_ge(sto[k], 16 * i)
        po.sem_inc(st["tick"], 1)
        po.wait_ge(st["cp"], n + 1)
        po.tensor_copy(ic[:, k, :], g["IDX"][:, column, bass.ds(n * C, C)]).then_inc(st["ix"], 1)
        po.wait_ge(st["ix"], n + 1)
        po.sem_inc(st["tick"], 1)
        for c in range(C):
            po.indirect_dma_start(out=G[:, k, c, :], out_offset=None, in_=table,
                                  in_offset=bass.IndirectOffsetOnAxis(ap=ic[:, k, c:c + 1], axis=0),
                                  bounds_check=table.shape[0] - 1, oob_is_err=False).then_inc(got[k], 16)

    def store(sp, n, k, i):
        sp.wait_ge(got[k], base[f"g{k}"] + 16 * C * (i + 1))
        sp.sem_inc(st["tick"], 1)
        sp.dma_start(chunk_tiles(d["asrc"], n), G[:, k, :, D:D + HEADS]).then_inc(sto[k], 16)

    def keep(act, n, k, i):
        act.wait_ge(got[k], base[f"g{k}"] + 16 * C * (i + 1))
        act.activation(g["GR"][:, bass.ds(n * C, C), :], G[:, k], ACT.Copy).then_inc(st["cp"], 1)

    def end(sp):
        for k in (0, 1):
            sp.wait_ge(sto[k], 16 * (ECH // 2))

    w.on("gpsimd", (fetch, 0))
    w.on("scalar", (keep, 1))
    w.on("sync", (store, 1), after=end)
    return w


def first_of_source(g):
    nc, t, d = g["nc"], g["t"], g["d"]
    st = Stage(nc, "fos", ["ld0", "ld1", "k", "dump"], ["cnt"])
    w = Work(st)
    SR = st.sb("SR", [P, 2, CR], I32)
    LOW = st.sb("LOW", [P, C, CR])
    junk = st.sb("junk", [P, C, CR])
    cnt = st.sb("cnt", [P, C])
    dump = st.sb("dump", [P, C])
    sc = st.sb("sc", [P, C])
    SF = st.sb("SF", [P, ET])
    ld = [st["ld0"], st["ld1"]]

    def begin_sp(sp):
        sp.dma_start(dump[:], t["dump_row"]).then_inc(st["dump"], 16)

    def load(sp, n, k, i):
        sp.wait_ge(st["cnt"], n + 1)
        sp.dma_start(SR[:, k], over(t["src_lin"][bass.ds(n * CR, CR)].unsqueeze(0), [P, CR])).then_inc(ld[k], 16)

    def begin_po(po):
        po.memset(LOW[:], 1.0)
        po.drain()
        po.affine_select(out=LOW[:], in_=LOW[:], compare_op=ALU.is_gt, fill=0.0, base=0,
                         pattern=[[P, C], [-1, CR]], channel_multiplier=1).then_inc(st["k"], 1)

    def begin_v(v):
        v.wait_ge(st["k"], 1)
        v.wait_ge(st["dump"], 16)
        v.tensor_copy(SF[:], g["IDX"][:, I_SRC, :])

    def count(v, n, k, i):
        v.drain()
        v.wait_ge(ld[k], 16 * (i + 1))
        v.tensor_copy(sc[:], SF[:, bass.ds(n * C, C)])
        v.drain()
        for c in range(C):
            cols = (c + 1) * P
            v.scalar_tensor_tensor(out=junk[:, c, 0:cols], in0=SR[:, k, 0:cols], scalar=sc[:, c:c + 1],
                                   in1=LOW[:, c, 0:cols], op0=ALU.is_equal, op1=ALU.mult, accum_out=cnt[:, c:c + 1])
        v.drain()
        v.tensor_scalar(cnt[:], cnt[:], 0.5, None, ALU.is_gt)
        v.tensor_tensor(junk[:, 0, 0:C], dump[:], sc[:], ALU.subtract)
        v.drain()
        v.tensor_tensor(junk[:, 1, 0:C], junk[:, 0, 0:C], cnt[:], ALU.mult)
        v.drain()
        v.tensor_tensor(g["IDX"][:, I_ADD, bass.ds(n * C, C)], junk[:, 1, 0:C], sc[:], ALU.add).then_inc(st["cnt"], 1)

    w.on("sync", (load, 0), before=begin_sp)
    w.on("gpsimd", before=begin_po)
    w.on("vector", (count, 0), before=begin_v)
    return w


def gat_softmax(nc, layer, t, d, g):
    st = Stage(nc, f"gs{layer}", ["tick", "ld", "to_pe", "from_pe", "e", "st"], [])
    AS, AD, B, T, M = (st.sb(x, [P, J, HEADS]) for x in ("AS", "AD", "B", "T", "M"))
    sc = Scans(nc, st, g, HEADS)
    with nc.Block() as block:
        @block.sync
        def _(sp):
            sp.dma_start(AS[:], d["asrc"].rearrange("(q j) h -> q j h", j=J)).then_inc(st["ld"], 16)
            sp.dma_start(AD[:], (d["gt2"] if layer else d["gt"])[0:EP, D + HEADS:GW].rearrange("(q j) h -> q j h", j=J)).then_inc(st["ld"], 16)
            sp.wait_ge(st["e"], 3)
            sp.dma_start(d["alpha"].rearrange("(q j) h -> q j h", j=J), AS[:]).then_inc(st["st"], 16)
            sp.wait_ge(st["st"], 16)

        @block.tensor
        def _(pe):
            pe_part(nc, st, g, sc, [True, False, True, False, True], pe)

        @block.scalar
        def _(act):
            act.wait_ge(st["e"], 1)
            act.activation(AS[:], AS[:], ACT.Exp).then_inc(st["e"], 1)

        @block.vector
        def _(v):
            sc.begin(v)
            v.wait_ge(st["ld"], 32)
            sc.spread(v, B, AD, T)
            v.tensor_tensor(AS[:], AS[:], B[:], ALU.add)
            v.drain()
            v.scalar_tensor_tensor(out=AS[:], in0=AS[:], scalar=0.2, in1=AS[:], op0=ALU.mult, op1=ALU.max)
            v.drain()
            sc.maximum(v, M, AS)
            sc.spread(v, B, M, T)
            v.tensor_tensor(AS[:], AS[:], B[:], ALU.subtract).then_inc(st["e"], 1)
            v.wait_ge(st["e"], 2)
            sc.total(v, M, AS)
            sc.spread(v, B, M, T)
            v.tensor_scalar(B[:], B[:], 1.0e-16, None, ALU.add)
            v.drain()
            v.reciprocal(M[:], B[:])
            v.drain()
            v.tensor_tensor(AS[:], AS[:], M[:], ALU.mult).then_inc(st["e"], 1)
    st.close()


def patch_last_rows(nc, t, d, g):
    st = Stage(nc, "patch", ["tick", "ld", "c", "g0", "st"], [])
    half = ET // 2
    tf = st.sb("tf", [half, 2, P])
    tii = st.sb("tii", [half, 2], I32)
    R = st.sb("R", [half, 2, 2 * D])
    kv_tiles = d["kv"].rearrange("(k p) w -> k p w", p=P)
    with nc.Block() as block:
        @block.sync
        def _(sp):
            sp.dma_start(tf[:], d["lin"][5, :].rearrange("(a k p) -> k a p", a=2, p=P)).then_inc(st["ld"], 16)
            sp.wait_ge(st["g0"], COUNTED["g0"] + 32)
            for a in (0, 1):
                sp.dma_start(kv_tiles[a * half:(a + 1) * half, P - 1, :], R[:, a, :]).then_inc(st["st"], 16)
            sp.wait_ge(st["st"], 32)

        @block.vector
        def _(v):
            v.wait_ge(st["ld"], 16)
            v.tensor_copy(tii[:], tf[:, :, P - 1]).then_inc(st["c"], 1)

        @block.gpsimd
        def _(po):
            po.wait_ge(st["c"], 1)
            for a in (0, 1):
                po.indirect_dma_start(out=R[:, a, :], out_offset=None, in_=d["kv"],
                                      in_offset=bass.IndirectOffsetOnAxis(ap=tii[:, a:a + 1], axis=0),
                                      bounds_check=EP - 1, oob_is_err=False).then_inc(st["g0"], 16)
    st.close(g0=32)


def attention(g):
    nc, t, d = g["nc"], g["t"], g["d"]
    st = Stage(nc, "att", ["tick", "ix", "ld0", "ld1", "g0", "g1", "st0", "st1"],
               ["s", "kv", "ev", "sc", "ex", "ms"], dict(kv=2 * C, ev=C))
    w = Work(st, pool=dict(g0=8 * C * ECH, g1=8 * C * ECH))
    base = dict(COUNTED)
    G = st.sb("G", [P, 2, C, D])
    K = st.sb("K", [P, 2, C, 2 * D])
    KD = st.sb("KD", [P, 2, C, 2 * D])
    DR = st.sb("DR", [P, 2, CR], I32)
    S = st.sb("S", [P, 2, C, P])
    PR = st.sb("PR", [P, C, D])
    ss = st.sb("ss", [P, 2, C, HEADS])
    MS = st.sb("MS", [P, 2, C, D + HEADS])
    mc = st.sb("mc", [P, 2, M_N, C])
    ic = st.sb("ic", [P, 2, C], I32)
    ld, got, sto = [st["ld0"], st["ld1"]], [st["g0"], st["g1"]], [st["st0"], st["st1"]]
    ps = g["ps"]

    def load(sp, n, k, i):
        sp.wait_ge(st["kv"], C * n + C)
        sp.dma_start(DR[:, k], over(t["dst_lin"][bass.ds(n * CR, CR)].unsqueeze(0), [P, CR])).then_inc(ld[k], 16)
        sp.dma_start(K[:, k], chunk_tiles(d["kv"], n)).then_inc(ld[k], 16)

    def fetch(po, n, k, i):
        po.wait_ge(st["sc"], n + 1)
        po.tensor_copy(ic[:, k, :], g["IDX"][:, I_SRCROW, bass.ds(n * C, C)]).then_inc(st["ix"], 1)
        po.wait_ge(st["ix"], n + 1)
        po.sem_inc(st["tick"], 1)
        for c in range(C):
            po.indirect_dma_start(out=G[:, k, c, :], out_offset=None, in_=d["q"],
                                  in_offset=bass.IndirectOffsetOnAxis(ap=ic[:, k, c:c + 1], axis=0),
                                  bounds_check=ROWS - 1, oob_is_err=False).then_inc(got[k], 16)

    def spread(pe, n, k, i):
        pe.wait_ge(st["s"], n + 3)
        pe.wait_ge(ld[k], 32 * (i + 1))
        for c in range(C):
            pe.wait_ge(st["ev"], C * n + c + 1)
            nc.tensor.matmul(ps[:, c * 512:c * 512 + 2 * D], S[:, k, c, :], K[:, k, c, :],
                             start=True, stop=True).then_inc(st["kv"], 1)

    def exps(act, n, k, i):
        act.wait_ge(st["sc"], n + 3)
        act.activation(MS[:, k, :, D:D + HEADS], ss[:, k], ACT.Exp).then_inc(st["ex"], 1)

    def to_sbuf(act, n, k, i):
        act.wait_ge(st["ms"], n + 1)
        for c in range(C):
            act.wait_ge(st["kv"], C * n + c + 1 + 2 * C)
            act.activation(KD[:, k, c, :], ps[:, c * 512:c * 512 + 2 * D], ACT.Copy).then_inc(st["ev"], 1)

    def store(act, n, k, i):
        act.wait_ge(st["ms"], n + 3)
        act.dma_start(chunk_tiles(d["msg"], n), MS[:, k]).then_inc(sto[k], 16)

    def end(act):
        for k in (0, 1):
            act.wait_ge(sto[k], 16 * (ECH // 2))

    def scores(v, n, k, i):
        v.wait_ge(st["ev"], C * n + C + C)
        v.wait_ge(got[k], base[f"g{k}"] + 16 * C * (i + 1))
        v.wait_ge(sto[k], 16 * i)
        v.tensor_tensor(PR[:], G[:, k, :, 0:D], KD[:, k, :, 0:D], ALU.mult)
        v.drain()
        v.reduce_sum(ss[:, k], PR[:].rearrange("p c (h e) -> p c h e", h=HEADS), AX.X)
        v.drain()
        v.tensor_scalar(ss[:, k], ss[:, k], -10.0, 10.0, ALU.max, ALU.min).then_inc(st["sc"], 1)

    def build_s(v, n, k, i):
        v.wait_ge(ld[k], 32 * (i + 1))
        v.wait_ge(st["kv"], C * n + C)
        v.tensor_copy(mc[:, k], g["META"][:, :, bass.ds(n * C, C)])
        v.drain()
        for c in range(C):
            last = v.tensor_scalar(S[:, k, c, :], DR[:, k, c * P:(c + 1) * P], mc[:, k, M_DST, c:c + 1],
                                   mc[:, k, M_REP, c:c + 1], ALU.is_equal, ALU.mult)
        last.then_inc(st["s"], 1)

    def messages(v, n, k, i):
        v.wait_ge(st["ex"], n + 3)
        v.tensor_tensor(MS[:, k, :, 0:D].rearrange("p c (h e) -> p c h e", h=HEADS),
                        KD[:, k, :, D:2 * D].rearrange("p c (h e) -> p c h e", h=HEADS),
                        over(MS[:, k, :, D:D + HEADS].unsqueeze(3), [P, C, HEADS, HC]),
                        ALU.mult).then_inc(st["ms"], 1)

    w.on("sync", (load, 0))
    w.on("gpsimd", (fetch, 0))
    w.on("tensor", (spread, 0))
    w.on("vector", (build_s, 0), (scores, 1), (messages, 1))
    w.on("scalar", (exps, 1), (to_sbuf, 0), (store, 1), after=end)
    return w


def accumulate(g):
    nc, t, d = g["nc"], g["t"], g["d"]
    st = Stage(nc, "acc", ["tick", "ix", "ld0", "ld1", "add0", "add1"], ["s", "mm", "ev"], dict(mm=4, ev=2))
    w = Work(st, pool=dict(add0=8 * C * ECH, add1=8 * C * ECH))
    base = dict(COUNTED)
    WM = D + HEADS
    MS = st.sb("MS", [P, 2, C, WM])
    SR = st.sb("SR", [P, 2, CR], I32)
    S = st.sb("S", [P, 2, C, CR])
    sc = st.sb("sc", [P, 2, C])
    SF = st.sb("SF", [P, ET])
    ic = st.sb("ic", [P, 2, C], I32)
    O = st.sb("O", [P, 2, C, WM])
    ld, add = [st["ld0"], st["ld1"]], [st["add0"], st["add1"]]
    ps = g["ps"]
    halves = ((0, 1, 2, 3), (4, 5, 6))

    def load(sp, n, k, i):
        sp.wait_ge(st["mm"], 2 * n + 2)
        sp.dma_start(SR[:, k], over(t["src_lin"][bass.ds(n * CR, CR)].unsqueeze(0), [P, CR])).then_inc(ld[k], 16)
        sp.dma_start(MS[:, k], chunk_tiles(d["msg"], n)).then_inc(ld[k], 16)

    def begin_v(v):
        v.tensor_copy(SF[:], g["IDX"][:, I_SRC, :])
        v.drain()

    def build_s(v, n, k, i):
        v.wait_ge(ld[k], 32 * (i + 1))
        v.wait_ge(st["mm"], 2 * n + 2)
        v.tensor_copy(sc[:, k], SF[:, bass.ds(n * C, C)])
        v.drain()
        for c in range(C):
            last = v.tensor_scalar(S[:, k, c, :], SR[:, k, :], sc[:, k, c:c + 1], None, ALU.is_equal)
        last.then_inc(st["s"], 1)

    def sums(pe, n, k, i):
        pe.wait_ge(st["s"], n + 3)
        pe.wait_ge(ld[k], 32 * (i + 1))
        for h, tiles in enumerate(halves):
            pe.wait_ge(st["ev"], 2 * n + h + 1)
            for b in tiles:
                for a in range(C):
                    last = nc.tensor.matmul(ps[:, b * P:b * P + WM], S[:, k, a, b * P:(b + 1) * P],
                                            MS[:, k, a, :], start=(a == 0), stop=(a == C - 1))
            last.then_inc(st["mm"], 1)

    def to_sbuf(act, n, k, i):
        act.wait_ge(add[k], base[f"add{k}"] + 16 * C * i)
        for h, tiles in enumerate(halves):
            act.wait_ge(st["mm"], 2 * n + h + 5)
            z = ps[:, h * 512:h * 512 + len(tiles) * P].rearrange("p (c w) -> p c w", w=P)[:, :, 0:WM]
            act.activation(O[:, k, tiles[0]:tiles[-1] + 1, :], z, ACT.Copy).then_inc(st["ev"], 1)

    def scatter(po, n, k, i):
        po.tensor_copy(ic[:, k, :], g["IDX"][:, I_ADD, bass.ds(n * C, C)]).then_inc(st["ix"], 1)
        po.wait_ge(st["ix"], n + 1)
        po.sem_inc(st["tick"], 1)
        po.wait_ge(st["ev"], 2 * n + 4)
        po.sem_inc(st["tick"], 1)
        for c in range(C):
            po.indirect_dma_start(out=d["res"], in_=O[:, k, c, :], in_offset=None,
                                  out_offset=bass.IndirectOffsetOnAxis(ap=ic[:, k, c:c + 1], axis=0),
                                  bounds_check=NP + CR - 1, oob_is_err=True,
                                  compute_op=ALU.add).then_inc(add[k], 16)
        po.wait_ge(add[k], base[f"add{k}"] + 16 * C * (i + 1))

    w.on("sync", (load, 0))
    w.on("vector", (build_s, 0), before=begin_v)
    w.on("tensor", (sums, 0))
    w.on("scalar", (to_sbuf, 0))
    w.on("gpsimd", (scatter, 0))
    return w


def gates(g):
    nc, t, d = g["nc"], g["t"], g["d"]
    st = Stage(nc, "gate", ["tick", "ix", "w", "wb", "ld0", "ld1", "g0", "g1", "st0", "st1", "sb0", "sb1"],
               ["tr", "ht", "mm", "zb", "ab", "ms"], dict(tr=8, ht=8))
    w = Work(st, pool=dict(g0=2 * 8 * C * ECH, g1=2 * 8 * C * ECH))
    base = dict(COUNTED)
    R = st.sb("R", [P, 2, 2 * C, 2 * D])
    HT = st.sb("HT", [P, 2, C, 2 * P])
    W = st.sb("W", [P, 2, 2 * D])
    bias = st.sb("bias", [P, 2 * D])
    ZB, AB = (st.sb(x, [P, C, 2 * D]) for x in ("ZB", "AB"))
    TT, LG = (st.sb(x, [P, 2, C, 2 * D]) for x in ("TT", "LG"))
    RZ, GE = (st.sb(x, [P, 2, C, D]) for x in ("RZ", "GE"))
    MS = st.sb("MS", [P, 2, C, D + 1])
    GM, GR, GI = (st.sb(x, [P, C, D]) for x in ("GM", "GR", "GI"))
    ic = st.sb("ic", [P, 2, 2, C], I32)
    ld, got = [st["ld0"], st["ld1"]], [st["g0"], st["g1"]]
    sto, sb = [st["st0"], st["st1"]], [st["sb0"], st["sb1"]]
    ps, ident = g["ps"], g["ident"]
    z = ps[:, 2048:2048 + C * 256].rearrange("p (c w) -> p c w", w=256)[:, :, 0:2 * D]
    groups = ((0, 1), (2, 3), (4, 5), (6,))

    def begin_sp(sp):
        for s, (we, b) in enumerate((("we", "be"), ("wn", "bn"))):
            cols = slice(s * D, (s + 1) * D)
            for part in range(2):
                sp.dma_start(W[0:D, part, cols], t[we][part * D:(part + 1) * D, :]).then_inc(st["w"], 16)
                sp.dma_start(W[D:P, part, cols], t[we][2 * D + part * HE:2 * D + (part + 1) * HE, :]).then_inc(st["w"], 16)
            sp.dma_start(bias[:, cols], over(t[b].unsqueeze(0), [P, D])).then_inc(st["wb"], 16)

    def store_base(sp, n, k, i):
        sp.wait_ge(got[k], base[f"g{k}"] + 32 * C * (i + 1))
        sp.dma_start(chunk_tiles(d["base"], n), R[:, k, C:2 * C, D:2 * D]).then_inc(sb[k], 16)

    def load(sp, n, k, i):
        sp.wait_ge(st["mm"], n + 1)
        sp.sem_inc(st["tick"], 1)
        for part in range(2):
            sp.dma_start(HT[D:P, k, :, part * P:(part + 1) * P],
                         t["ea_t"][part * HE:(part + 1) * HE, bass.ds(n * CR, CR)].rearrange("e (c p) -> e c p", p=P))\
              .then_inc(ld[k], 16)

    def end_sp(sp):
        for k in (0, 1):
            sp.wait_ge(sb[k], 16 * (ECH // 2))

    def fetch(po, n, k, i):
        po.wait_ge(st["tr"], 4 * n + 4)
        po.sem_inc(st["tick"], 1)
        po.wait_ge(sb[k], 16 * i)
        po.tensor_copy(ic[:, k, 0, :], g["IDX"][:, I_SRC, bass.ds(n * C, C)])
        po.tensor_copy(ic[:, k, 1, :], g["IDX"][:, I_DST, bass.ds(n * C, C)]).then_inc(st["ix"], 1)
        po.wait_ge(st["ix"], n + 1)
        po.sem_inc(st["tick"], 1)
        for s in (0, 1):
            for c in range(C):
                po.indirect_dma_start(out=R[:, k, s * C + c, :], out_offset=None, in_=d["hy"],
                                      in_offset=bass.IndirectOffsetOnAxis(ap=ic[:, k, s, c:c + 1], axis=0),
                                      bounds_check=NP - 1, oob_is_err=False).then_inc(got[k], 16)

    def begin_v(v):
        v.memset(MS[:], 1.0)
        v.wait_ge(st["wb"], 32)

    def begin_pe(pe):
        pe.wait_ge(st["w"], 128)

    def turn(pe, n, k, i):
        pe.wait_ge(got[k], base[f"g{k}"] + 32 * C * (i + 1))
        for q, tiles in enumerate(groups):
            pe.wait_ge(st["ht"], 4 * n + q + 5)
            for c in tiles:
                for s in (0, 1):
                    last = nc.tensor.transpose(ps[0:D, c * 256 + s * P:c * 256 + (s + 1) * P],
                                               R[:, k, s * C + c, 0:D], ident[:])
            last.then_inc(st["tr"], 1)

    def to_sbuf(act, n, k, i):
        act.wait_ge(st["mm"], n + 1)
        for q, tiles in enumerate(groups):
            act.wait_ge(st["tr"], 4 * n + q + 9)
            cs = slice(tiles[0], tiles[-1] + 1)
            act.activation(HT[0:D, k, cs], ps[0:D, tiles[0] * 256:(tiles[-1] + 1) * 256]
                           .rearrange("p (c w) -> p c w", w=256), ACT.Copy).then_inc(st["ht"], 1)

    def multiply(pe, n, k, i):
        pe.wait_ge(st["zb"], n + 2)
        pe.wait_ge(ld[k], 32 * (i + 1))
        pe.wait_ge(st["ht"], 4 * n + 12)
        for c in range(C):
            o = ps[:, 2048 + c * 256:2048 + c * 256 + 2 * D]
            nc.tensor.matmul(o, HT[:, k, c, 0:P], W[:, 0, :], start=True, stop=False)
            last = nc.tensor.matmul(o, HT[:, k, c, P:2 * P], W[:, 1, :], start=False, stop=True)
        last.then_inc(st["mm"], 1)

    def exps(act, n, k, i):
        act.wait_ge(st["ms"], n + 1)
        act.wait_ge(st["zb"], n + 3)
        act.activation(RZ[:, k], ZB[:, :, D:2 * D], ACT.Relu)
        act.activation(AB[:], ZB[:], ACT.Abs)
        act.drain()
        act.activation(TT[:, k], AB[:], ACT.Exp, scale=-1.0)
        act.drain()
        act.activation(LG[:, k], TT[:, k], ACT.Ln, bias=1.0).then_inc(st["ab"], 1)

    def add_bias(v, n, k, i):
        v.wait_ge(st["mm"], n + 3)
        v.wait_ge(st["ab"], n + 2)
        v.tensor_tensor(ZB[:], z, over(bias[:].unsqueeze(1), [P, C, 2 * D]), ALU.add).then_inc(st["zb"], 1)
        v.drain()
        v.tensor_scalar(GE[:, k], ZB[:, :, 0:D], 0.0, None, ALU.is_ge)
        v.drain()

    def messages(v, n, k, i):
        v.wait_ge(st["ab"], n + 3)
        v.wait_ge(sto[k], 16 * i)
        v.tensor_tensor(GM[:], GE[:, k], TT[:, k, :, 0:D], ALU.max)
        v.tensor_scalar(GR[:], TT[:, k, :, 0:D], 1.0, None, ALU.add)
        v.drain()
        v.reciprocal(GI[:], GR[:])
        v.drain()
        v.tensor_tensor(GM[:], GM[:], GI[:], ALU.mult)
        v.tensor_tensor(GR[:], RZ[:, k], LG[:, k, :, D:2 * D], ALU.add)
        v.drain()
        v.tensor_tensor(MS[:, k, :, 0:D], GM[:], GR[:], ALU.mult).then_inc(st["ms"], 1)
        v.drain()

    def store(act, n, k, i):
        act.wait_ge(st["ms"], n + 3)
        act.dma_start(chunk_tiles(d["msg3"], n), MS[:, k]).then_inc(sto[k], 16)

    def end(act):
        for k in (0, 1):
            act.wait_ge(sto[k], 16 * (ECH // 2))

    w.on("sync", (store_base, 1), (load, 1), before=begin_sp, after=end_sp)
    w.on("gpsimd", (fetch, 0))
    w.on("tensor", (turn, 1), (multiply, 2), before=begin_pe)
    w.on("scalar", (to_sbuf, 1), (exps, 2), (store, 3), after=end)
    w.on("vector", (add_bias, 2), (messages, 3), before=begin_v)
    return w


def kernel(**inputs):
    import numpy as np
    import concourse.bacc as bacc
    from concourse.bass_utils import run_bass_kernel_spmd

    a = {k: np.asarray(v) for k, v in inputs.items()}

    def padded(x, rows, value):
        x = np.ascontiguousarray(x)
        return np.concatenate([x, np.full((rows - x.shape[0], *x.shape[1:]), value, x.dtype)])

    src, dst = padded(a["src"], EP, N), padded(a["dst"], EP, N)
    ew = padded(a["edge_weight"], EP, 0)
    around = np.concatenate([np.full(1, -1, dst.dtype), dst, np.full(1, N + 1, dst.dtype)])
    arrays = {
        "x": padded(a["x"], NP, 0),
        "src_lin": src, "dst_lin": dst, "src_tiles": src.reshape(ET, P).T, "dst_tiles": dst.reshape(ET, P).T,
        "dst_runs": np.stack([around[i:i + EP].reshape(P, J) for i in range(3)], axis=1),
        "first": dst[::P], "prev_tiles": np.broadcast_to(around[0:EP:P], (P, ET)),
        "ew_runs": ew.reshape(P, J), "ew_tiles": ew.reshape(ET, P).T,
        "edge_no": np.arange(EP, dtype=np.float32).reshape(P, J),
        "dump_row": (NP + np.arange(CR, dtype=np.float32)).reshape(C, P).T,
        "ea_t": padded(a["edge_attr_64"], EP, 0).T,
        "gat_w": a["L1_gnn_W"], "gat_src": a["L1_gnn_att_src"], "gat_dst": a["L1_gnn_att_dst"],
        "gat_b": a["L1_gnn_bias"], "q_w": a["L2_gnn_qW"], "k_w": a["L2_gnn_kW"], "v_w": a["L2_gnn_vW"],
        "we": a["L3_gnn_W_e"], "be": a["L3_gnn_b_e"], "wn": a["L3_gnn_W_n"], "bn": a["L3_gnn_b_n"],
    }
    for i in (1, 2, 3):
        arrays[f"gcn_w{i}"], arrays[f"gcn_b{i}"] = a[f"L0_gnn_W{i}"], a[f"L0_gnn_b{i}"]
    arrays = {k: np.ascontiguousarray(v) for k, v in arrays.items()}

    nc = bacc.Bacc("TRN2", target_bir_lowering=False, num_devices=1)
    t = {k: nc.dram_tensor(f"in_{k}", v.shape, mybir.dt.from_np(v.dtype), kind="ExternalInput").ap()
         for k, v in arrays.items()}
    out = nc.dram_tensor("out_0", (NP, D), F32, kind="ExternalOutput").ap()
    build(nc, t, out)
    r = run_bass_kernel_spmd(nc, [{f"in_{k}": v for k, v in arrays.items()}], core_ids=[0])
    return r.results[0]["out_0"][0:N]
```
